# Optimizing a Trainium2 kernel written in Bass

```python
import numpy as np
import jax
import jax.numpy as jnp

def _softmax(x, axis=-1):
    return jax.nn.softmax(x, axis=axis)

def _gelu(x):
    return jax.nn.gelu(x, approximate=True)

def _silu(x):
    return jax.nn.silu(x)

def _sigmoid(x):
    return jax.nn.sigmoid(x)

def _layernorm(x, axis=-1, eps=1e-05):
    m = jnp.mean(x, axis=axis, keepdims=True)
    v = jnp.var(x, axis=axis, keepdims=True)
    return (x - m) / jnp.sqrt(v + eps)

def _scatter_add(tgt, idx, src, axis=0):
    return tgt.at[idx].add(src)

def _segment_sum(src, seg, n):
    return jax.ops.segment_sum(src, seg, n)
kernel_name = 'mk_sandwich_d2_jaxref_r8_42716a'

def setup_inputs(seed: int=0):
    np.random.seed(seed)
    _w = jnp.asarray

    def _L0_attn_setup():
        import jax, jax.numpy as jnp
        import numpy as np
        D_MODEL = 256
        N_HEADS = 16
        HEAD_DIM = D_MODEL // N_HEADS
        B, T = (2, 256)
        key = jax.random.key(seed)
        ks = jax.random.split(key, 9)
        s = 0.02
        x = jax.random.normal(ks[0], (B, T, D_MODEL), dtype=jnp.float32)
        Wq = jax.random.normal(ks[1], (N_HEADS, D_MODEL, HEAD_DIM), dtype=jnp.float32) * s
        bq = jax.random.normal(ks[2], (N_HEADS, HEAD_DIM), dtype=jnp.float32) * s
        Wk = jax.random.normal(ks[3], (N_HEADS, D_MODEL, HEAD_DIM), dtype=jnp.float32) * s
        bk = jax.random.normal(ks[4], (N_HEADS, HEAD_DIM), dtype=jnp.float32) * s
        Wv = jax.random.normal(ks[5], (N_HEADS, D_MODEL, HEAD_DIM), dtype=jnp.float32) * s
        bv = jax.random.normal(ks[6], (N_HEADS, HEAD_DIM), dtype=jnp.float32) * s
        Wo = jax.random.normal(ks[7], (D_MODEL, D_MODEL), dtype=jnp.float32) * s
        bo = jax.random.normal(ks[8], (D_MODEL,), dtype=jnp.float32) * s
        return {'x': x, 'Wq': Wq, 'bq': bq, 'Wk': Wk, 'bk': bk, 'Wv': Wv, 'bv': bv, 'Wo': Wo, 'bo': bo}
    _L0_attn_in = _L0_attn_setup()

    def _L0_ffn_setup():
        import jax, jax.numpy as jnp
        import numpy as np
        B, S, H = (1, 64, 256)
        I = 192
        E = 32
        K = 4
        SCALE = 1.8
        key = jax.random.key(seed)
        ks = jax.random.split(key, 9)
        init = lambda k, shape: jax.random.normal(k, shape, jnp.float32) * (1.0 / np.sqrt(shape[-1]))
        return {'x': jax.random.normal(ks[0], (B, S, H), jnp.float32), 'router_w': init(ks[1], (E, H)), 'router_b': jnp.zeros((E,), jnp.float32), 'gate_w': init(ks[2], (E, I, H)), 'up_w': init(ks[3], (E, I, H)), 'down_w': init(ks[4], (E, H, I)), 'shared_gate_w': init(ks[5], (I, H)), 'shared_up_w': init(ks[6], (I, H)), 'shared_down_w': init(ks[7], (H, I))}
    _L0_ffn_in = _L0_ffn_setup()

    def _L1_attn_setup():
        import jax, jax.numpy as jnp
        import numpy as np
        D_MODEL = 256
        NUM_HEADS = 16
        D_K = D_MODEL // NUM_HEADS
        SEQ = 256
        BATCH = 2
        THETA = 10000.0

        def _rope_tables(seq_len, d_k, theta, dtype):
            pos = jnp.arange(seq_len, dtype=dtype)[:, None]
            inv = theta ** (-(jnp.arange(0, d_k, 2, dtype=dtype) / d_k))
            ang = pos * inv
            sin = jnp.repeat(jnp.sin(ang), 2, axis=1)
            cos = jnp.repeat(jnp.cos(ang), 2, axis=1)
            return (sin, cos)

        def _apply_rope(x, sin, cos):
            xp = x.reshape(x.shape[:-1] + (x.shape[-1] // 2, 2))
            swapped = jnp.stack((-xp[..., 1], xp[..., 0]), axis=-1).reshape(x.shape)
            return x * cos + swapped * sin
        key = jax.random.key(seed)
        ks = jax.random.split(key, 5)
        s = 1.0 / np.sqrt(D_MODEL)
        return {'x': jax.random.normal(ks[0], (BATCH, SEQ, D_MODEL), jnp.float32), 'wq': jax.random.normal(ks[1], (D_MODEL, D_MODEL), jnp.float32) * s, 'wk': jax.random.normal(ks[2], (D_MODEL, D_MODEL), jnp.float32) * s, 'wv': jax.random.normal(ks[3], (D_MODEL, D_MODEL), jnp.float32) * s, 'wo': jax.random.normal(ks[4], (D_MODEL, D_MODEL), jnp.float32) * s}
    _L1_attn_in = _L1_attn_setup()

    def _L1_ffn_setup():
        import jax, jax.numpy as jnp
        import numpy as np
        B, S, H = (2, 256, 256)
        E, K, F = (32, 4, 176)
        FS = 704
        EPS = 1e-06
        CAP = 128
        key = jax.random.key(seed)
        ks = jax.random.split(key, 10)
        s = 0.02
        return {'hidden_states': jax.random.normal(ks[0], (B, S, H), jnp.float32), 'w_norm': 1.0 + 0.02 * jax.random.normal(ks[1], (H,), jnp.float32), 'w_router': s * jax.random.normal(ks[2], (H, E), jnp.float32), 'w_gate': s * jax.random.normal(ks[3], (E, H, F), jnp.float32), 'w_up': s * jax.random.normal(ks[4], (E, H, F), jnp.float32), 'w_down': s * jax.random.normal(ks[5], (E, F, H), jnp.float32), 'sw_gate': s * jax.random.normal(ks[6], (H, FS), jnp.float32), 'sw_up': s * jax.random.normal(ks[7], (H, FS), jnp.float32), 'sw_down': s * jax.random.normal(ks[8], (FS, H), jnp.float32), 'w_shared_gate': s * jax.random.normal(ks[9], (H, 1), jnp.float32)}
    _L1_ffn_in = _L1_ffn_setup()
    _d = {'L0_attn_x': _L0_attn_in['x'], 'L0_attn_Wq': _L0_attn_in['Wq'], 'L0_attn_bq': _L0_attn_in['bq'], 'L0_attn_Wk': _L0_attn_in['Wk'], 'L0_attn_bk': _L0_attn_in['bk'], 'L0_attn_Wv': _L0_attn_in['Wv'], 'L0_attn_bv': _L0_attn_in['bv'], 'L0_attn_Wo': _L0_attn_in['Wo'], 'L0_attn_bo': _L0_attn_in['bo'], 'L0_ffn_router_w': _L0_ffn_in['router_w'], 'L0_ffn_router_b': _L0_ffn_in['router_b'], 'L0_ffn_gate_w': _L0_ffn_in['gate_w'], 'L0_ffn_up_w': _L0_ffn_in['up_w'], 'L0_ffn_down_w': _L0_ffn_in['down_w'], 'L0_ffn_shared_gate_w': _L0_ffn_in['shared_gate_w'], 'L0_ffn_shared_up_w': _L0_ffn_in['shared_up_w'], 'L0_ffn_shared_down_w': _L0_ffn_in['shared_down_w'], 'L1_attn_wq': _L1_attn_in['wq'], 'L1_attn_wk': _L1_attn_in['wk'], 'L1_attn_wv': _L1_attn_in['wv'], 'L1_attn_wo': _L1_attn_in['wo'], 'L1_ffn_w_norm': _L1_ffn_in['w_norm'], 'L1_ffn_w_router': _L1_ffn_in['w_router'], 'L1_ffn_w_gate': _L1_ffn_in['w_gate'], 'L1_ffn_w_up': _L1_ffn_in['w_up'], 'L1_ffn_w_down': _L1_ffn_in['w_down'], 'L1_ffn_sw_gate': _L1_ffn_in['sw_gate'], 'L1_ffn_sw_up': _L1_ffn_in['sw_up'], 'L1_ffn_sw_down': _L1_ffn_in['sw_down'], 'L1_ffn_w_shared_gate': _L1_ffn_in['w_shared_gate']}
    _x0 = _d['L0_attn_x']
    _d['L0_attn_x'] = jax.random.normal(jax.random.fold_in(jax.random.key(seed), 1), (1, 1024, 256), dtype=_x0.dtype)
    del _x0
    return _d

def reference(L0_attn_x, L0_attn_Wq, L0_attn_bq, L0_attn_Wk, L0_attn_bk, L0_attn_Wv, L0_attn_bv, L0_attn_Wo, L0_attn_bo, L0_ffn_router_w, L0_ffn_router_b, L0_ffn_gate_w, L0_ffn_up_w, L0_ffn_down_w, L0_ffn_shared_gate_w, L0_ffn_shared_up_w, L0_ffn_shared_down_w, L1_attn_wq, L1_attn_wk, L1_attn_wv, L1_attn_wo, L1_ffn_w_norm, L1_ffn_w_router, L1_ffn_w_gate, L1_ffn_w_up, L1_ffn_w_down, L1_ffn_sw_gate, L1_ffn_sw_up, L1_ffn_sw_down, L1_ffn_w_shared_gate):

    def _L0_attn_ref(x, Wq, bq, Wk, bk, Wv, bv, Wo, bo):
        import jax, jax.numpy as jnp
        import numpy as np
        D_MODEL = 256
        N_HEADS = 16
        HEAD_DIM = D_MODEL // N_HEADS
        B, T = (2, 256)
        Bn, Tn, C = x.shape
        H, _, D = Wq.shape
        scale = D ** (-0.5)
        q = jnp.einsum('btc,hcd->bhtd', x, Wq) + bq[None, :, None, :]
        k = jnp.einsum('btc,hcd->bhtd', x, Wk) + bk[None, :, None, :]
        v = jnp.einsum('btc,hcd->bhtd', x, Wv) + bv[None, :, None, :]
        scores = jnp.einsum('bhtd,bhsd->bhts', q, k) * scale
        neg = jnp.finfo(scores.dtype).min
        causal = jnp.triu(jnp.full((Tn, Tn), neg, dtype=scores.dtype), k=1)
        probs = jax.nn.softmax(scores + causal, axis=-1)
        y = jnp.einsum('bhts,bhsd->bhtd', probs, v)
        y = y.transpose(0, 2, 1, 3).reshape(Bn, Tn, H * D)
        return y @ Wo + bo

    def _L0_ffn_ref(x, router_w, router_b, gate_w, up_w, down_w, shared_gate_w, shared_up_w, shared_down_w):
        import jax, jax.numpy as jnp
        import numpy as np
        B, S, H = (1, 64, 256)
        I = 192
        E = 32
        K = 4
        SCALE = 1.8
        b, s, h = x.shape
        xf = x.reshape(-1, h).astype(jnp.float32)
        logits = xf @ router_w.T + router_b
        top_vals, top_idx = jax.lax.top_k(logits, K)
        rw = jax.nn.softmax(top_vals, axis=-1) * SCALE
        combine = jnp.einsum('tke,tk->te', jax.nn.one_hot(top_idx, E, dtype=xf.dtype), rw)
        g = jax.nn.silu(jnp.einsum('th,eih->tei', xf, gate_w))
        u = jnp.einsum('th,eih->tei', xf, up_w)
        routed = jnp.einsum('tei,ehi,te->th', g * u, down_w, combine)
        sg = jax.nn.silu(xf @ shared_gate_w.T)
        su = xf @ shared_up_w.T
        shared = sg * su @ shared_down_w.T
        return (routed + shared).reshape(b, s, h)

    def _L1_attn_ref(x, wq, wk, wv, wo):
        import jax, jax.numpy as jnp
        import numpy as np
        D_MODEL = 256
        NUM_HEADS = 16
        D_K = D_MODEL // NUM_HEADS
        SEQ = 256
        BATCH = 2
        THETA = 10000.0

        def _rope_tables(seq_len, d_k, theta, dtype):
            pos = jnp.arange(seq_len, dtype=dtype)[:, None]
            inv = theta ** (-(jnp.arange(0, d_k, 2, dtype=dtype) / d_k))
            ang = pos * inv
            sin = jnp.repeat(jnp.sin(ang), 2, axis=1)
            cos = jnp.repeat(jnp.cos(ang), 2, axis=1)
            return (sin, cos)

        def _apply_rope(x, sin, cos):
            xp = x.reshape(x.shape[:-1] + (x.shape[-1] // 2, 2))
            swapped = jnp.stack((-xp[..., 1], xp[..., 0]), axis=-1).reshape(x.shape)
            return x * cos + swapped * sin
        B, S, D = x.shape
        H, dk = (NUM_HEADS, D_K)
        q = jnp.einsum('bsd,hkd->bhsk', x, wq.reshape(H, dk, D))
        k = jnp.einsum('bsd,hkd->bhsk', x, wk.reshape(H, dk, D))
        v = jnp.einsum('bsd,hkd->bhsk', x, wv.reshape(H, dk, D))
        sin, cos = _rope_tables(S, dk, THETA, x.dtype)
        q = _apply_rope(q, sin, cos)
        k = _apply_rope(k, sin, cos)
        scores = jnp.einsum('bhqk,bhsk->bhqs', q, k) / jnp.sqrt(jnp.asarray(dk, x.dtype))
        causal = jnp.triu(jnp.ones((S, S), dtype=bool), k=1)
        scores = jnp.where(causal, -jnp.inf, scores)
        attn = jax.nn.softmax(scores, axis=-1)
        out = jnp.einsum('bhqs,bhsv->bqhv', attn, v).reshape(B, S, H * dk)
        return jnp.einsum('bsf,df->bsd', out, wo)

    def _L1_ffn_ref(hidden_states, w_norm, w_router, w_gate, w_up, w_down, sw_gate, sw_up, sw_down, w_shared_gate):
        import jax, jax.numpy as jnp
        import numpy as np
        B, S, H = (2, 256, 256)
        E, K, F = (32, 4, 176)
        FS = 704
        EPS = 1e-06
        CAP = 128
        inp = hidden_states
        xf = inp.astype(jnp.float32)
        var = jnp.mean(xf * xf, axis=-1, keepdims=True)
        x = (w_norm * (xf * jax.lax.rsqrt(var + EPS))).astype(inp.dtype)
        Bq, Sq, Hq = x.shape
        x = x.reshape(-1, Hq)
        T = Bq * Sq
        logits = x @ w_router
        probs = jax.nn.softmax(logits.astype(jnp.float32), axis=-1)
        w_topk, sel = jax.lax.top_k(probs, K)
        w_topk = w_topk.astype(x.dtype)
        flat_e = sel.reshape(-1)
        order = jnp.argsort(flat_e)
        sorted_e = flat_e[order]
        counts = jnp.zeros((E,), jnp.int32).at[flat_e].add(1)
        starts = jnp.cumsum(counts) - counts
        pos = jnp.arange(T * K) - starts[sorted_e]
        tok = order // K
        valid = pos < CAP
        dest = jnp.where(valid, pos, CAP)
        buf = jnp.zeros((E, CAP + 1, Hq), x.dtype).at[sorted_e, dest].set(x[tok])
        buf = buf[:, :CAP]
        g = jnp.einsum('ech,ehf->ecf', buf, w_gate)
        u = jnp.einsum('ech,ehf->ecf', buf, w_up)
        y = jnp.einsum('ecf,efh->ech', jax.nn.silu(g) * u, w_down)
        wv = w_topk.reshape(-1)[order] * valid.astype(x.dtype)
        gath = y[sorted_e, jnp.minimum(pos, CAP - 1)]
        out = jnp.zeros((T, Hq), x.dtype).at[tok].add(gath * wv[:, None])
        sh = jax.nn.silu(x @ sw_gate) * (x @ sw_up) @ sw_down
        sh = jax.nn.sigmoid(x @ w_shared_gate) * sh
        out = out + sh
        return inp + out.reshape(Bq, Sq, Hq)
    x = L0_attn_x
    x = x + _layernorm(_L0_attn_ref(_layernorm(x, axis=-1), L0_attn_Wq, L0_attn_bq, L0_attn_Wk, L0_attn_bk, L0_attn_Wv, L0_attn_bv, L0_attn_Wo, L0_attn_bo), axis=-1)
    x = x + _layernorm(_L0_ffn_ref(_layernorm(x, axis=-1), L0_ffn_router_w, L0_ffn_router_b, L0_ffn_gate_w, L0_ffn_up_w, L0_ffn_down_w, L0_ffn_shared_gate_w, L0_ffn_shared_up_w, L0_ffn_shared_down_w), axis=-1)
    x = x + _layernorm(_L1_attn_ref(_layernorm(x, axis=-1), L1_attn_wq, L1_attn_wk, L1_attn_wv, L1_attn_wo), axis=-1)
    x = x + _layernorm(_L1_ffn_ref(_layernorm(x, axis=-1), L1_ffn_w_norm, L1_ffn_w_router, L1_ffn_w_gate, L1_ffn_w_up, L1_ffn_w_down, L1_ffn_sw_gate, L1_ffn_sw_up, L1_ffn_sw_down, L1_ffn_w_shared_gate), axis=-1)
    return x

_drawn_inputs = setup_inputs


def setup_inputs(seed=0):
    import zlib

    import numpy as np

    out = dict(_drawn_inputs(seed))
    spreads = {'L0_ffn_router_b': (0.0, 0.1)}
    factors = {'L0_attn_bq': 5.406,
     'L0_attn_bk': 8.0,
     'L1_ffn_w_norm': 8.0,
     'L1_ffn_w_router': 8.0,
     'L1_ffn_w_gate': 8.0,
     'L1_ffn_w_up': 8.0,
     'L1_ffn_w_down': 8.0,
     'L1_ffn_sw_gate': 8.0,
     'L1_ffn_sw_up': 8.0,
     'L1_ffn_sw_down': 8.0,
     'L1_ffn_w_shared_gate': 8.0}
    for name, (base, spread) in spreads.items():
        noise = np.random.default_rng([zlib.crc32(name.encode()), seed]).standard_normal(out[name].shape)
        drawn = base * np.exp(spread * noise) if base else spread * noise
        out[name] = jnp.asarray(drawn.astype(out[name].dtype))
    for name, factor in factors.items():
        out[name] = (out[name] * factor).astype(out[name].dtype)
    return out
```

```python
import numpy as np

import concourse.bass as bass
from concourse import mybir
from contextlib import ExitStack

F32 = mybir.dt.float32
BF16 = mybir.dt.bfloat16
I32 = mybir.dt.int32
U32 = mybir.dt.uint32
ALU = mybir.AluOpType
ACT = mybir.ActivationFunctionType
AX = mybir.AxisListType

P = 128
T = 1024
NT = T // P
D = 256
KD = D // P
H = 16
DH = D // H
HG = 4
NG = H // HG
CH = 512
NC = T // CH
TPC = CH // P
E = 32
K = 4
SCALE = DH ** -0.5
LN_EPS = 1e-5
RMS_EPS = 1e-6
BIG = 1.0e30
SKIP = float(1 << 20)
CAP = 128
PARTS = 3
Q_PART = (0, 0, 0, 1, 1, 2)
K_PART = (0, 1, 2, 0, 1, 0)
NPROD = len(Q_PART)
KQ = NPROD * DH
NSH = 2
KX = KQ + NSH

INTER = (192, 176)
CHUNK = (96, 88)
SHARED = (192, 704)
TILES = (64, 32)
E0 = (0, TILES[0])
R0 = (0, TILES[0] // 4)
NR = (E, E + 1)
RING = 4


def exp_steps():
    return [(c, b) for c in range(NC) for b in range(TPC * (c + 1))]


STEPS = exp_steps()
NSTEP = len(STEPS)


def max_units():
    units = []
    for i in range(NT):
        if i >= TPC:
            units += [(0, i, hh, 1, 0, CH) for hh in range(HG)]
        w = (i % TPC + 1) * P
        n = {1: 4, 2: 2, 3: 1, 4: 1}[w // P]
        units += [(1, i, hh, n, (i // TPC) * CH, w) for hh in range(0, HG, n)]
    return units


MAX_UNITS = max_units()
NMAX = len(MAX_UNITS)
UPG = NMAX + NC


class Chain:

    def __init__(self, eng, sem):
        self.eng, self.sem, self.n = eng, sem, 0

    def step(self, ins):
        self.n += 1
        ins.then_inc(self.sem, 1)

    def wait(self):
        self.eng.wait_ge(self.sem, self.n)

    def link(self, ins):
        self.step(ins)
        self.wait()


def build(nc, a, out):
    ctx = ExitStack()
    with ctx:
        sems = {}

        def S(name):
            if name not in sems:
                sems[name] = ctx.enter_context(nc.semaphore(name))
            return sems[name]

        def sb(name, shape, dt=F32):
            return ctx.enter_context(nc.sbuf_tensor(name, shape, dt))

        qk_parts = [nc.dram_tensor(f"qk_parts{L}", (2, KD, PARTS, P, T), BF16).ap() for L in range(2)]
        slot_rows = [nc.dram_tensor(f"slot_rows{L}", (TILES[L] * P, D), F32).ap() for L in range(2)]
        slot_out = [nc.dram_tensor(f"slot_out{L}", (TILES[L] * P, D), F32).ap() for L in range(2)]

        xres = sb("xres", [P, NT, D])
        xn = sb("xn", [P, NT, D])
        xT = sb("xT", [P, KD, T])
        hb = sb("hb", [P, NT, D])
        identf = sb("identf", [P, P])
        identb = sb("identb", [P, P], BF16)
        mask_q = sb("mask_q", [P, P], BF16)
        mask_k = sb("mask_k", [P, P], BF16)
        before = sb("before", [P, P], BF16)
        ones = sb("ones", [P, P], BF16)
        stats = sb("stats", [P, NT, 6])
        mv = sb("mv", [P, NT, 2])
        rstd = sb("rstd", [P, NT])
        msq = sb("msq", [P, NT])
        rs_half = sb("rs_half", [P, NT])
        rs_sq = sb("rs_sq", [P, NT])
        w_qkv = sb("w_qkv", [P, 3, KD, D])
        w_o = sb("w_o", [P, NG, D])
        bias_qk = sb("bias_qk", [P, 2, KD])
        bias_v = sb("bias_v", [P, D])
        bias_o = sb("bias_o", [P, D])
        cos_t = sb("cos_t", [P, T])
        sin_t = sb("sin_t", [P, T])
        V = sb("V", [P, NT, H, 32])
        w_sgu = sb("w_sgu", [P, KD, 2 * SHARED[1]])
        w_sdn = sb("w_sdn", [P, 8, D])
        w_rt = sb("w_rt", [P, KD, E + 1])
        b_rt = sb("b_rt", [P, E])
        w_nm = sb("w_nm", [P, D])
        QA = sb("QA", [P, H, T], BF16)
        KA = sb("KA", [P, H, T], BF16)
        X = sb("X", [P, 10240])
        qkf = X[:, 0:4096].rearrange("p (a m t) -> p a m t", a=2, m=KD)
        parts = X[:, 4096:10240].bitcast(BF16).rearrange("p (a m r t) -> p a m r t", a=2, m=KD, r=PARTS)
        probs = X[:, 0:4096].rearrange("p (n h t) -> p n h t", n=2, h=HG)
        pv_sb = X[:, 4096:5120].rearrange("p (n t) -> p n t", n=2)
        den = X[:, 5120:5632]
        rden = X[:, 5632:6144]
        yT = X[:, 6144:10240].rearrange("p (g t) -> p g t", g=NG)
        swapped = V[:, :, :, :].rearrange("p a b c -> p (a b c)")[:, 0:T]
        roped = V[:, :, :, :].rearrange("p a b c -> p (a b c)")[:, T:2 * T]
        mx = sb("mx", [P, 2, NT, HG])
        nb = sb("nb", [P, NT, NSH, HG], BF16)
        mT = sb("mT", [NSH * HG, T], BF16)
        acts = QA[:, :, :].rearrange("p h t -> p (h t)").bitcast(F32)
        KAf = KA[:, :, :].rearrange("p h t -> p (h t)").bitcast(F32)
        rows = X[:, 0:1024].rearrange("p (r n) -> p r n", r=RING)
        rowsT = X[:, 1024:1536].rearrange("p (r k n) -> p r k n", r=2, k=KD)
        eact = X[:, 1536:2048].rearrange("p (r n) -> p r n", r=2)
        esilu = X[:, 2048:2560].rearrange("p (r n) -> p r n", r=2)
        erows = X[:, 2560:3072].rearrange("p (r n) -> p r n", r=2)
        ssilu = X[:, 3072:4096].rearrange("p (r n) -> p r n", r=2)
        shout = X[:, 4096:6144].rearrange("p (t n) -> p t n", t=NT)
        gath = X[:, 6144:8192].rearrange("p (r k n) -> p r k n", r=2, k=K)
        onehot = X[:, 8192:9216].rearrange("p (t k e) -> p t k e", t=NT, k=K)
        prod = X[:, 9216:10240].rearrange("p (t k e) -> p t k e", t=NT, k=K)
        w_gu = KAf[:, 0:RING * 2 * KD * INTER[0]].rearrange("p (r n) -> p r n", r=RING)
        w_dn = KAf[:, RING * 768:RING * 768 + RING * 2 * D].rearrange("p (r n) -> p r n", r=RING)
        zeros = sb("zeros", [P, D])
        iota_e = sb("iota_e", [P, E])
        iota_t = sb("iota_t", [1, TILES[0]])
        lt_e = sb("lt_e", [P, E, E], BF16)
        lev = sb("lev", [P, NT])
        lg = sb("lg", [P, NT, E + 1])
        top = sb("top", [P, NT, 8])
        tix = sb("tix", [P, NT, 8], U32)
        tixf = sb("tixf", [P, NT, K])
        picked = sb("picked", [P, NT, E], BF16)
        gate = sb("gate", [P, NT, K])
        gall = sb("gall", [P, NT, E])
        gsum = sb("gsum", [P, NT])
        sgate = sb("sgate", [P, NT])
        cnt = sb("cnt", [P, E])
        ntile = sb("ntile", [P, E])
        tbeg = sb("tbeg", [P, E])
        tend = sb("tend", [P, E])
        big1 = X[:, 0:E * E]
        dest = sb("dest", [P, NT, E])
        slot = sb("slot", [P, NT, K])
        slot_i = sb("slot_i", [P, NT * K], I32)
        slot_g = sb("slot_g", [P, NT * K], I32)
        texp = X[0:1, 0:TILES[0]]
        texp_i = sb("texp_i", [1, TILES[0]], I32)
        tmap = X[0:1, 1024:1024 + TILES[0] * E]

        ps = ctx.enter_context(nc.psum_tensor("ps", [P, 8, CH], F32))

        block = ctx.enter_context(nc.Block())

        @block.sync
        def _(sp):
            sp.dma_start(xres[:, :, :], a["x"].rearrange("(t p) d -> p t d", p=P)).then_inc(S("x_in"), 16)

            def attention_weights(L):
                sp.dma_start(w_qkv[:, :, :, :], a[f"qkv{L}"].rearrange("a (k p) n -> p a k n", p=P))\
                  .then_inc(S(f"w_qkv{L}"), 16)
                wo = a[f"wo{L}"].rearrange("(g h d) n -> h d g n", g=NG, h=HG)
                if L == 0:
                    sp.wait_ge(S("wo_zero"), 1)
                for hh in range(HG):
                    sp.dma_start(w_o[32 * hh:32 * hh + DH, :, :], wo[hh]).then_inc(S(f"w_o{L}"), 16)

            def expert_constants(L):
                n = 2 * SHARED[L]
                sp.dma_start(w_sgu[:, :, 0:n], a[f"sgu{L}"]).then_inc(S(f"w_shared{L}"), 16)
                sp.dma_start(w_sdn[0:CHUNK[L], 0:SHARED[L] // CHUNK[L], :],
                             a[f"sdn{L}"].rearrange("(c p) n -> p c n", p=CHUNK[L])).then_inc(S(f"w_shared{L}"), 16)
                sp.dma_start(w_rt[:, :, 0:NR[L]], a[f"router{L}"].rearrange("(k p) n -> p k n", p=P))\
                  .then_inc(S(f"w_router{L}"), 16)

            attention_weights(0)
            sp.dma_start(bias_qk[:, :, :], a["bqk"]).then_inc(S("bias"), 16)
            for dst, name in ((bias_v, "bv"), (bias_o, "bo"), (b_rt, "router_b"), (w_nm, "w_norm")):
                n = dst.shape[1]
                sp.dma_start(dst[:, :], a[name].rearrange("(o n) -> o n", o=1).broadcast_to([P, n])).then_inc(S("bias"), 16)
            sp.dma_start(cos_t[:, :], a["cos"]).then_inc(S("rope"), 16)
            sp.dma_start(sin_t[:, :], a["sin"]).then_inc(S("rope"), 16)
            expert_constants(0)
            sp.wait_ge(S("zeros"), 1)
            for L in range(2):
                for i in range(0, TILES[L], 8):
                    sp.dma_start(slot_rows[L][i * P:(i + 8) * P, :].rearrange("(t p) d -> p t d", p=P),
                                 zeros[:, :].rearrange("p (o d) -> p o d", o=1).broadcast_to([P, 8, D]))\
                      .then_inc(S(f"slots_zero{L}"), 16)

            for L in range(2):
                if L == 1:
                    sp.wait_ge(S("attn_proj0"), NT)
                    attention_weights(1)
                for m in range(KD):
                    for j in range(2):
                        n = 2 * m + j
                        sp.wait_ge(S(f"parts_p3_{L}"), n + 1)
                        sp.dma_start(qk_parts[L][j, m].rearrange("r p t -> p r t"), parts[:, j, m, :, :])\
                          .then_inc(S(f"parts_out{L}"), 16)
                    sp.wait_ge(S(f"parts_out{L}"), 32 * (m + 1))
                    for r in range(NPROD):
                        for dst, j, part in ((QA, 0, Q_PART[r]), (KA, 1, K_PART[r])):
                            sp.dma_start(dst[DH * r:DH * (r + 1), 8 * m:8 * m + 8, :],
                                         qk_parts[L][j, m, part].rearrange("(h d) t -> d h t", d=DH))\
                              .then_inc(S(f"qa_rows{L}_{m}"), 16)
                for g in range(NG):
                    sp.wait_ge(S(f"mx_done{L}"), UPG * (g + 1))
                    for j in range(NSH):
                        sp.dma_start(QA[KQ + j:KQ + j + 1, HG * g:HG * (g + 1), :], mT[HG * j:HG * (j + 1), :])\
                          .then_inc(S(f"max_rows{L}"), 16)

                ng, nd = KD * 2 * INTER[L], 2 * D

                def weights_gu(i, r, e):
                    sp.dma_start(w_gu[:, r, 0:ng], a[f"gu{L}"][bass.ds(e, 1)].rearrange("o p n -> (o p) n"))\
                      .then_inc(S(f"w_gu_{r}"), 16)
                    sp.dma_start(w_dn[0:CHUNK[L], r, 0:nd], a[f"dn{L}"][bass.ds(e, 1)].rearrange("o p n -> (o p) n"))\
                      .then_inc(S(f"w_dn_{r}"), 16)

                def tile_in(i, r):
                    e = sp.value_load(texp_i[0:1, bass.ds(i, 1)], min_val=0, max_val=E - 1) if L == 0 else i
                    weights_gu(i, r, e)
                    sp.dma_start(rows[:, r, :], slot_rows[L][bass.ds(i * P, P), :]).then_inc(S(f"rows_{r}"), 16)

                sp.wait_ge(S(f"attn_proj{L}"), NT)
                sp.wait_ge(S(f"scattered{L}"), 16 * NT * K)
                if L == 0:
                    sp.wait_ge(S("tile_expert"), 1)
                def tile_out(i, r):
                    sp.wait_ge(S("e_sb"), E0[L] + i + 1)
                    sp.dma_start(slot_out[L][bass.ds(i * P, P), :], erows[:, r % 2, :])\
                      .then_inc(S(f"e_out_{r % 2}"), 16)

                for r in range(RING):
                    tile_in(r, r)
                with sp.Fori(RING, TILES[L] - RING + 1, RING) as i0:
                    for r in range(RING):
                        sp.wait_ge(S("e_down"), E0[L] + i0 + (r - RING + 1))
                        tile_in(i0 + r, r)
                        tile_out(i0 + (r - RING), r)
                for r in range(RING):
                    tile_out(TILES[L] - RING + r, r)
                if L == 0:
                    sp.wait_ge(S("sh_down0"), NT)
                    expert_constants(1)
            sp.wait_ge(S("final"), NT)
            sp.dma_start(out.rearrange("(t p) d -> p t d", p=P), xres[:, :, :]).then_inc(S("out"), 16)
            sp.wait_ge(S("out"), 16)

        @block.gpsimd
        def _(pool):
            ch = Chain(pool, S("pool_own"))
            ch.step(pool.memset(zeros[:, :], 0.0))
            pool.memset(w_o[:, :, :], 0.0).then_inc(S("wo_zero"), 1)
            for t in (identf, identb, mask_q, mask_k):
                ch.step(pool.memset(t[:, :], 0.0))
            for t in (before, ones):
                ch.step(pool.memset(t[:, :], 1.0))
            ch.step(pool.memset(lt_e[:, :, :], 1.0))
            ch.step(pool.iota(iota_e[:, :], pattern=[[1, E]], base=0, channel_multiplier=0,
                              allow_small_or_imprecise_dtypes=True))
            ch.step(pool.iota(iota_t[:, :], pattern=[[1, TILES[0]]], base=0, channel_multiplier=0,
                              allow_small_or_imprecise_dtypes=True))
            ch.step(pool.iota(lev[:, :], pattern=[[P, NT]], base=0, channel_multiplier=0,
                              allow_small_or_imprecise_dtypes=True))
            ch.wait()
            pool.memset(zeros[:, 0:1], 0.0).then_inc(S("zeros"), 1)
            for t in (identf, identb):
                ch.step(pool.affine_select(out=t[:, :], in_=t[:, :], compare_op=ALU.not_equal, fill=1.0,
                                           base=0, pattern=[[-1, P]], channel_multiplier=1))
            ch.step(pool.affine_select(out=mask_q[:, :], in_=mask_q[:, :], compare_op=ALU.is_ge, fill=-BIG,
                                       base=0, pattern=[[-1, P]], channel_multiplier=1))
            ch.step(pool.affine_select(out=mask_k[:, :], in_=mask_k[:, :], compare_op=ALU.is_ge, fill=-BIG,
                                       base=0, pattern=[[1, P]], channel_multiplier=-1))
            ch.step(pool.affine_select(out=before[:, :], in_=before[:, :], compare_op=ALU.is_ge, fill=0.0,
                                       base=-1, pattern=[[1, P]], channel_multiplier=-1))
            ch.step(pool.affine_select(out=lt_e[:, :, :], in_=lt_e[:, :, :], compare_op=ALU.is_ge, fill=0.0,
                                       base=-1, pattern=[[1, E], [-1, E]], channel_multiplier=0))
            ch.wait()
            pool.memset(KA[KQ:KX, :, :], 1.0).then_inc(S("consts"), 1)
            pool.wait_ge(S("consts"), 1)

            for L in range(2):
                if L == 1:
                    pool.wait_ge(S("e_down"), TILES[0])
                    pool.memset(KA[KQ:KX, :, :], 1.0).then_inc(S("k_ones1"), 1)
                    pool.wait_ge(S("k_ones1"), 1)
                if L == 1:
                    pool.wait_ge(S("parts_r1_1"), 2 * KD)
                ch.link(pool.memset(V[:, :, :, DH + 1:], 0.0))
                pool.memset(V[:, :, :, DH:DH + 1], 1.0).then_inc(S(f"v_pad{L}"), 1)

                pool.wait_ge(S(f"slots_zero{L}"), 16 * TILES[L] // 8)
                pool.wait_ge(S(f"slot_no{L}"), 1)
                for i in range(NT):
                    for k in range(K):
                        n = i * K + k
                        pool.indirect_dma_start(
                            out=slot_rows[L], out_offset=bass.IndirectOffsetOnAxis(ap=slot_i[:, n:n + 1], axis=0),
                            in_=xn[:, i, :], in_offset=None, bounds_check=TILES[L] * P - 1, oob_is_err=False)\
                            .then_inc(S(f"scattered{L}"), 16)
                for r in range(2):
                    pool.wait_ge(S(f"e_out_{r}"), 16 * (E0[L] + TILES[L]) // 2)
                for i in range(NT):
                    if i >= 2:
                        pool.wait_ge(S(f"summed{L}"), i - 1)
                    for k in range(K):
                        n = i * K + k
                        pool.indirect_dma_start(
                            out=gath[:, i % 2, k, :], out_offset=None, in_=slot_out[L],
                            in_offset=bass.IndirectOffsetOnAxis(ap=slot_g[:, n:n + 1], axis=0))\
                            .then_inc(S(f"gathered{L}_{i % 2}"), 16)

        @block.tensor
        def _(pe):
            pe.wait_ge(S("consts"), 1)

            def transposes(tag):
                for n in range(NC):
                    pe.wait_ge(S(f"xn_{tag}"), TPC * (n + 1))
                    for k in range(KD):
                        for i in range(TPC):
                            mm = pe.transpose(ps[:, KD * n + k, i * P:(i + 1) * P],
                                              xn[:, TPC * n + i, k * P:(k + 1) * P], identf[:, :])
                        mm.then_inc(S(f"xTp_{tag}"), 1)

            for L in range(2):
                transposes(f"a{L}")
                pe.wait_ge(S(f"w_qkv{L}"), 16)
                u = 0
                for m in range(KD):
                    for j in range(2):
                        for n in range(NC):
                            if m == 0:
                                pe.wait_ge(S(f"xT_a{L}"), KD * (n + 1))
                            if u >= 4:
                                pe.wait_ge(S(f"qk_sb{L}"), u - 3)
                            for k in range(KD):
                                mm = pe.matmul(ps[:, 4 + u % 4, :], w_qkv[:, j, k, m * P:(m + 1) * P],
                                               xT[:, k, n * CH:(n + 1) * CH], start=(k == 0), stop=(k == KD - 1))
                            mm.then_inc(S(f"qk_ps{L}"), 1)
                            u += 1
                for i in range(NT):
                    if i >= 4:
                        pe.wait_ge(S(f"v_sb{L}"), i - 3)
                    for k in range(KD):
                        mm = pe.matmul(ps[:, i % 4, 0:D], xT[:, k, i * P:(i + 1) * P], w_qkv[:, 2, k, :],
                                       start=(k == 0), stop=(k == KD - 1))
                    mm.then_inc(S(f"v_ps{L}"), 1)

                def max_unit(g, u):
                    n = UPG * g + u
                    if n >= 2:
                        pe.wait_ge(S(f"mx_done{L}"), n - 1)
                    bank = u % 2
                    if u < NMAX:
                        _, i, h0, nh, s0, w = MAX_UNITS[u]
                        for x in range(nh):
                            h = HG * g + h0 + x
                            diag = s0 + w == (i + 1) * P
                            mm = pe.matmul(ps[:, bank, x * w:(x + 1) * w], QA[0:KQ, h, i * P:(i + 1) * P],
                                           KA[0:KQ, h, s0:s0 + w], start=True, stop=not diag)
                            if diag:
                                mm = pe.matmul(ps[:, bank, (x + 1) * w - P:(x + 1) * w], identb[:, :], mask_q[:, :],
                                               start=False, stop=True)
                    else:
                        c = u - NMAX
                        pe.wait_ge(S(f"neg_max{L}"), g + 1)
                        for i in range(TPC):
                            mm = pe.matmul(ps[0:NSH * HG, bank, i * P:(i + 1) * P],
                                           nb[:, TPC * c + i, :, :].rearrange("p a h -> p (a h)"), identb[:, :],
                                           start=True, stop=True)
                    mm.then_inc(S(f"mx_ps{L}"), 1)

                def scores(g, s, p):
                    c, b = STEPS[s]
                    off = max(0, b * P - c * CH)
                    u = 2 * (NSTEP * g + s) + p
                    if s == 0 and p == 0:
                        pe.wait_ge(S(f"max_rows{L}"), 16 * NSH * (g + 1))
                    if u >= 2:
                        pe.wait_ge(S(f"exp{L}"), u - 1)
                    for x in range(2):
                        h = HG * g + 2 * p + x
                        bank = 4 + 2 * p + x
                        diag = b >= TPC * c
                        mm = pe.matmul(ps[:, bank, off:CH], KA[0:KX, h, b * P:(b + 1) * P],
                                       QA[0:KX, h, c * CH + off:(c + 1) * CH], start=True, stop=not diag)
                        if diag:
                            mm = pe.matmul(ps[:, bank, off:off + P], identb[:, :], mask_k[:, :], start=False, stop=True)
                    mm.then_inc(S(f"sc{L}"), 1)

                def weigh(g, s):
                    c, b = STEPS[s]
                    off = max(0, b * P - c * CH)
                    n = NC * g + c
                    st = NSTEP * g + s
                    pe.wait_ge(S(f"exp{L}"), 2 * st + 2)
                    if b == 0 and n >= 2:
                        pe.wait_ge(S(f"pv_sb{L}"), n - 1)
                    for x in range(HG):
                        mm = pe.matmul(ps[32 * x:32 * x + 32, 2 + c, off:CH], V[:, b, HG * g + x, :],
                                       probs[:, st % 2, x, off:CH], start=(b == 0), stop=(b == TPC * (c + 1) - 1))
                    mm.then_inc(S(f"pv{L}"), 1)

                pe.wait_ge(S(f"qa_rows{L}_0"), 16 * 2 * NPROD)
                pe.wait_ge(S(f"qk_sb{L}"), 8)
                pe.wait_ge(S(f"v_sb{L}"), NT)
                pe.wait_ge(S(f"v_pad{L}"), 1)
                if L == 1:
                    pe.wait_ge(S("k_ones1"), 1)
                for u in range(UPG):
                    max_unit(0, u)
                for g in range(NG):
                    if g == 1:
                        pe.wait_ge(S(f"qa_rows{L}_1"), 16 * 2 * NPROD)
                    nxt = list(range(UPG)) if g + 1 < NG else []
                    for s in range(NSTEP + 1):
                        if s < NSTEP:
                            scores(g, s, 0)
                            scores(g, s, 1)
                        if s >= 1:
                            weigh(g, s - 1)
                        todo = 4 if s < 10 else (0 if s == 10 else 1)
                        for _ in range(min(todo, len(nxt))):
                            max_unit(g + 1, nxt.pop(0))
                pe.wait_ge(S(f"w_o{L}"), 16 * HG)
                pe.wait_ge(S(f"exp{L}"), 2 * NSTEP * NG)
                for i in range(NT):
                    pe.wait_ge(S(f"yT{L}"), NC * NG - 1 if i < TPC else NC * NG)
                    if i >= 4:
                        pe.wait_ge(S(f"ao_sb{L}"), i - 3)
                    for g in range(NG):
                        mm = pe.matmul(ps[:, 4 + i % 4, 0:D], yT[:, g, i * P:(i + 1) * P], w_o[:, g, :],
                                       start=(g == 0), stop=(g == NG - 1))
                    mm.then_inc(S(f"attn_proj{L}"), 1)

                C = CHUNK[L]
                transposes(f"f{L}")
                pe.wait_ge(S(f"w_router{L}"), 16)
                pe.wait_ge(S(f"xT_f{L}"), KD * NC)
                pe.wait_ge(S(f"ao_sb{L}"), NT)
                for i in range(NT):
                    for k in range(KD):
                        mm = pe.matmul(ps[:, 4, i * NR[L]:(i + 1) * NR[L]], xT[:, k, i * P:(i + 1) * P],
                                       w_rt[:, k, 0:NR[L]], start=(k == 0), stop=(k == KD - 1))
                mm.then_inc(S(f"logits_ps{L}"), 1)

                pe.wait_ge(S(f"w_shared{L}"), 32)
                nsc = SHARED[L] // C

                def shared_up(u):
                    n, j = divmod(u, nsc)
                    if u >= 2:
                        pe.wait_ge(S(f"s_act{L}"), u - 1)
                    for x in range(2):
                        col = x * SHARED[L] + j * C
                        for k in range(KD):
                            mm = pe.matmul(ps[0:C, 2 * (u % 2) + x, :], w_sgu[:, k, col:col + C],
                                           xT[:, k, n * CH:(n + 1) * CH], start=(k == 0), stop=(k == KD - 1))
                    mm.then_inc(S(f"s_gu{L}"), 1)

                shared_up(0)
                shared_up(1)
                pe.wait_ge(S(f"picked{L}"), 1)
                for i in range(NT):
                    for j in range(i + 1):
                        mm = pe.matmul(ps[:, 5, i * E:(i + 1) * E], (ones if j < i else before)[:, :],
                                       picked[:, j, :], start=(j == 0), stop=(j == i))
                for j in range(NT):
                    mm = pe.matmul(ps[:, 5, NT * E:(NT + 1) * E], ones[:, :], picked[:, j, :],
                                   start=(j == 0), stop=(j == NT - 1))
                mm.then_inc(S(f"ranks{L}"), 1)
                for u in range(2, nsc * NC):
                    shared_up(u)
                actv = acts[:, 0:nsc * T].rearrange("p (c t) -> p c t", c=nsc)
                for i in range(NT):
                    pe.wait_ge(S(f"s_act{L}"), nsc * (i // TPC + 1))
                    if i >= 2:
                        pe.wait_ge(S(f"sh_sb{L}"), i - 1)
                    for j in range(nsc):
                        mm = pe.matmul(ps[:, 6 + i % 2, 0:D], actv[0:C, j, i * P:(i + 1) * P],
                                       w_sdn[0:C, j, :], start=(j == 0), stop=(j == nsc - 1))
                    mm.then_inc(S(f"sh_down{L}"), 1)

                I2 = INTER[L]

                def e_transpose(blk, r, first):
                    i = blk * RING + r
                    pe.wait_ge(S(f"rows_{r}"), 16 * (R0[L] + blk + 1))
                    if not (first and r < 2):
                        pe.wait_ge(S("rowsT"), E0[L] + i - 1)
                    for k in range(KD):
                        mm = pe.transpose(ps[:, r % 2, k * P:(k + 1) * P], rows[:, r, k * P:(k + 1) * P], identf[:, :])
                    mm.then_inc(S("e_tr"), 1)

                def e_up(blk, r, first):
                    i = blk * RING + r
                    pe.wait_ge(S("rowsT"), E0[L] + i + 1)
                    pe.wait_ge(S(f"w_gu_{r}"), 16 * (R0[L] + blk + 1))
                    if not (first and r < 2):
                        pe.wait_ge(S("e_act"), E0[L] + i - 1)
                    for x in range(2):
                        for j in range(2):
                            for k in range(KD):
                                col = (k * 2 + x) * I2 + j * C
                                mm = pe.matmul(ps[0:C, 2 + r % 2, (2 * x + j) * P:(2 * x + j + 1) * P],
                                               w_gu[:, r, col:col + C], rowsT[:, r % 2, k, :],
                                               start=(k == 0), stop=(k == KD - 1))
                    mm.then_inc(S("e_up"), 1)

                def e_down(blk, r, first):
                    i = blk * RING + r
                    pe.wait_ge(S("e_act"), E0[L] + i + 1)
                    pe.wait_ge(S(f"w_dn_{r}"), 16 * (R0[L] + blk + 1))
                    if not (first and r < 2):
                        pe.wait_ge(S("e_sb"), E0[L] + i - 1)
                    for j in range(2):
                        mm = pe.matmul(ps[:, 4 + r % 2, 0:D], eact[0:C, r % 2, j * P:(j + 1) * P],
                                       w_dn[0:C, r, j * D:(j + 1) * D], start=(j == 0), stop=(j == 1))
                    mm.then_inc(S("e_down"), 1)

                def e_block(blk, first, last):
                    for r in range(RING):
                        if not (last and r == RING - 1):
                            e_transpose(blk + (r + 1) // RING, (r + 1) % RING, first and r + 1 < RING)
                        e_up(blk, r, first)
                        if not (first and r == 0):
                            e_down(blk + (-1 if r == 0 else 0), (r - 1) % RING, first)

                pe.wait_ge(S(f"logits_sb{L}"), 1)
                pe.wait_ge(S(f"dest_done{L}"), 1)
                pe.wait_ge(S(f"s_act{L}"), nsc * NC)
                pe.wait_ge(S(f"sh_sb{L}"), NT)
                e_transpose(0, 0, True)
                e_block(0, True, False)
                with pe.Fori(1, TILES[L] // RING - 1) as blk:
                    e_block(blk, False, False)
                e_block(TILES[L] // RING - 1, False, True)
                e_down(TILES[L] // RING - 1, RING - 1, False)

        @block.scalar
        def _(act):
            for L in range(2):
                def xT_copy(tag):
                    for n in range(NC):
                        for k in range(KD):
                            u = KD * n + k
                            act.wait_ge(S(f"xTp_{tag}"), u + 1)
                            nc.scalar.activation(xT[:, k, n * CH:(n + 1) * CH], ps[:, u, :], ACT.Copy)\
                              .then_inc(S(f"xT_{tag}"), 1)

                xT_copy(f"a{L}")
                if L == 0:
                    act.wait_ge(S("bias"), 16 * 5)
                if L == 1:
                    act.wait_ge(S("summed0"), NT)
                for m in range(KD):
                    for j in range(2):
                        for n in range(NC):
                            u = (m * 2 + j) * NC + n
                            act.wait_ge(S(f"qk_ps{L}"), u + 1)
                            dst = qkf[:, j, m, n * CH:(n + 1) * CH]
                            if L == 0:
                                nc.scalar.activation(dst, ps[:, 4 + u % 4, :], ACT.Identity,
                                                     bias=bias_qk[:, j, m:m + 1]).then_inc(S(f"qk_sb{L}"), 1)
                            else:
                                nc.scalar.activation(dst, ps[:, 4 + u % 4, :], ACT.Copy).then_inc(S(f"qk_sb{L}"), 1)
                    for part in range(2):
                        for j in range(2):
                            n = 2 * m + j
                            if part == 0 and L == 0:
                                act.wait_ge(S(f"qk_sb{L}"), (n + 1) * NC)
                            if part == 0 and L == 1:
                                act.wait_ge(S("roped"), n + 1)
                            if part == 1:
                                act.wait_ge(S(f"parts_r1_{L}"), n + 1)
                            nc.scalar.activation(parts[:, j, m, part, :], qkf[:, j, m, :], ACT.Copy)\
                              .then_inc(S(f"parts_p{part + 1}_{L}"), 1)

                act.wait_ge(S(f"parts_out{L}"), 16 * 2 * KD)

                def exps(g, s, p):
                    c, b = STEPS[s]
                    off = max(0, b * P - c * CH)
                    st = NSTEP * g + s
                    act.wait_ge(S(f"sc{L}"), 2 * st + p + 1)
                    if p == 0 and st >= 2:
                        act.wait_ge(S(f"pv{L}"), st - 1)
                    nc.scalar.activation(probs[:, st % 2, 2 * p:2 * p + 2, off:CH], ps[:, 4 + 2 * p:6 + 2 * p, off:CH],
                                         ACT.Exp, scale=SCALE).then_inc(S(f"exp{L}"), 1)

                def pv_copy(n):
                    act.wait_ge(S(f"pv{L}"), NSTEP * (n // NC) + (TPC if n % NC == 0 else NSTEP))
                    if n >= 2:
                        act.wait_ge(S(f"yT{L}"), n - 1)
                    nc.scalar.activation(pv_sb[:, n % 2, :], ps[:, 2 + n % NC, :], ACT.Copy).then_inc(S(f"pv_sb{L}"), 1)

                for g in range(NG):
                    for s in range(NSTEP):
                        exps(g, s, 0)
                        exps(g, s, 1)
                        if s == 0 and g > 0:
                            pv_copy(NC * g - 1)
                        if s == TPC:
                            pv_copy(NC * g)
                pv_copy(NC * NG - 1)

                xT_copy(f"f{L}")
                C = CHUNK[L]
                nsc = SHARED[L] // C
                act.wait_ge(S(f"less_top{L}"), 1)
                nc.scalar.activation(gate[:, :, :], gate[:, :, :], ACT.Exp).then_inc(S(f"gate_exp{L}"), 1)
                if L == 1:
                    nc.scalar.activation(gall[:, :, :], gall[:, :, :], ACT.Exp).then_inc(S(f"gate_exp{L}"), 1)
                    nc.scalar.activation(sgate[:, :], lg[:, :, E], ACT.Tanh, scale=0.5).then_inc(S("sgate"), 1)
                for u in range(nsc * NC):
                    act.wait_ge(S(f"s_gu{L}"), u + 1)
                    if u >= 2:
                        act.wait_ge(S(f"s_act{L}"), u - 1)
                    nc.scalar.activation(ssilu[0:C, u % 2, :], ps[0:C, 2 * (u % 2), :], ACT.Silu)\
                      .then_inc(S(f"s_silu{L}"), 1)
                if L == 1:
                    act.wait_ge(S("sgate_done"), 1)
                for i in range(NT):
                    act.wait_ge(S(f"sh_down{L}"), i + 1)
                    nc.scalar.activation(shout[:, i, :], ps[:, 6 + i % 2, 0:D], ACT.Copy,
                                         scale=1.0 if L == 0 else sgate[:, i:i + 1]).then_inc(S(f"sh_sb{L}"), 1)

                def e_tile(blk, r, first):
                    i = blk * RING + r
                    act.wait_ge(S("e_tr"), E0[L] + i + 1)
                    if not (first and r < 2):
                        act.wait_ge(S("e_up"), E0[L] + i - 1)
                    nc.scalar.activation(rowsT[:, r % 2, :, :].rearrange("p k n -> p (k n)"),
                                         ps[:, r % 2, 0:D], ACT.Copy).then_inc(S("rowsT"), 1)

                def e_silu(blk, r, first):
                    i = blk * RING + r
                    act.wait_ge(S("e_up"), E0[L] + i + 1)
                    if not (first and r < 2):
                        act.wait_ge(S("e_act"), E0[L] + i - 1)
                    nc.scalar.activation(esilu[0:C, r % 2, :], ps[0:C, 2 + r % 2, 0:2 * P], ACT.Silu)\
                      .then_inc(S("e_silu"), 1)

                def e_block(blk, first, last):
                    for r in range(RING):
                        if not (last and r == RING - 1):
                            e_tile(blk + (r + 1) // RING, (r + 1) % RING, first and r + 1 < RING)
                        e_silu(blk, r, first)

                e_tile(0, 0, True)
                e_block(0, True, False)
                with act.Fori(1, TILES[L] // RING - 1) as blk:
                    e_block(blk, False, False)
                e_block(TILES[L] // RING - 1, False, True)

        @block.vector
        def _(dve):
            ch = Chain(dve, S("dve_own"))
            v = nc.vector

            def inv_sqrt(dst, src, eps, t0, t1):
                y, half, sq = dst[:, t0:t1], rs_half[:, t0:t1], rs_sq[:, t0:t1]
                ch.link(v.tensor_scalar(half, src, eps, None, ALU.add))
                ch.link(v.tensor_scalar(y.bitcast(I32), half.bitcast(I32), -0.5, float(0x5F3759DF), ALU.mult, ALU.add))
                ch.link(v.tensor_scalar(half, half, -0.5, None, ALU.mult))
                for _ in range(3):
                    ch.link(v.tensor_tensor(sq, y, y, ALU.mult))
                    ch.link(v.tensor_tensor(sq, sq, half, ALU.mult))
                    ch.link(v.scalar_tensor_tensor(y, sq, 1.5, y, ALU.add, ALU.mult))

            def row_stats(src, tiles):
                t0, t1 = tiles[0], tiles[-1] + 1
                for i in tiles:
                    ch.step(v.bn_stats(stats[:, i, :], src[:, i, :]))
                ch.wait()
                for i in tiles:
                    ch.step(v.bn_aggr(mv[:, i, :], stats[:, i, :]))
                ch.wait()
                inv_sqrt(rstd, mv[:, t0:t1, 1], LN_EPS, t0, t1)

            def norm(dst, src, i):
                return v.tensor_scalar(dst[:, i, :], src[:, i, :], mv[:, i, 0:1], rstd[:, i:i + 1],
                                       ALU.subtract, ALU.mult)

            halves = (list(range(0, TPC)), list(range(TPC, NT)))
            dve.wait_ge(S("x_in"), 16)
            for L in range(2):
                for tiles in halves:
                    row_stats(xres, tiles)
                    for i in tiles:
                        norm(xn, xres, i).then_inc(S(f"xn_a{L}"), 1)
                for m in range(KD):
                    for j in range(2):
                        n = 2 * m + j
                        q = qkf[:, j, m, :]
                        dve.wait_ge(S(f"qk_sb{L}"), (n + 1) * NC)
                        if L == 1:
                            if n == 0:
                                dve.wait_ge(S("rope"), 32)
                            swap = [x ^ 1 for x in range(32)]
                            ch.link(v.stream_shuffle(swapped, q, swap))
                            ch.step(v.tensor_tensor(swapped, swapped, sin_t[:, :], ALU.mult))
                            ch.link(v.tensor_tensor(roped, q, cos_t[:, :], ALU.mult))
                            v.tensor_tensor(q, roped, swapped, ALU.add).then_inc(S("roped"), 1)
                            dve.wait_ge(S("roped"), n + 1)
                    for j in range(2):
                        n = 2 * m + j
                        q = qkf[:, j, m, :]
                        dve.wait_ge(S(f"parts_p1_{L}"), n + 1)
                        v.tensor_tensor(q, q, parts[:, j, m, 0, :], ALU.subtract).then_inc(S(f"parts_r1_{L}"), 1)
                    for j in range(2):
                        n = 2 * m + j
                        dve.wait_ge(S(f"parts_p2_{L}"), n + 1)
                        v.tensor_tensor(parts[:, j, m, 2, :], qkf[:, j, m, :], parts[:, j, m, 1, :], ALU.subtract)\
                         .then_inc(S(f"parts_p3_{L}"), 1)
                if L == 0:
                    dve.wait_ge(S("bias"), 16 * 5)
                for i in range(NT):
                    dve.wait_ge(S(f"v_ps{L}"), i + 1)
                    dst = V[:, i, :, 0:DH]
                    src = ps[:, i % 4, 0:D].rearrange("p (h d) -> p h d", h=H)
                    if L == 0:
                        v.tensor_tensor(dst, src, bias_v[:, :].rearrange("p (h d) -> p h d", h=H), ALU.add)\
                         .then_inc(S(f"v_sb{L}"), 1)
                    else:
                        v.tensor_copy(dst, src).then_inc(S(f"v_sb{L}"), 1)

                def max_unit(g, u):
                    n = UPG * g + u
                    if u == NMAX:
                        ch.link(v.tensor_tensor(mx[:, 1, TPC:NT, :], mx[:, 1, TPC:NT, :], mx[:, 0, TPC:NT, :], ALU.max))
                        ch.link(v.tensor_scalar(nb[:, :, 0, :], mx[:, 1, :, :], -1.0, None, ALU.mult))
                        v.scalar_tensor_tensor(nb[:, :, 1, :], mx[:, 1, :, :], -1.0, nb[:, :, 0, :],
                                               ALU.mult, ALU.subtract).then_inc(S(f"neg_max{L}"), 1)
                        if g >= 1:
                            dve.wait_ge(S(f"max_rows{L}"), 16 * NSH * g)
                    dve.wait_ge(S(f"mx_ps{L}"), n + 1)
                    if u < NMAX:
                        part, i, h0, nh, _, w = MAX_UNITS[u]
                        ins = v.tensor_reduce(mx[:, part, i, h0:h0 + nh],
                                              ps[:, u % 2, 0:nh * w].rearrange("p (h w) -> p h w", h=nh), AX.X, ALU.max)
                        ins.then_inc(S(f"mx_done{L}"), 1)
                        if u == NMAX - 1:
                            dve.wait_ge(S(f"mx_done{L}"), n + 1)
                    else:
                        c = u - NMAX
                        v.tensor_copy(mT[:, c * CH:(c + 1) * CH], ps[0:NSH * HG, u % 2, :])\
                         .then_inc(S(f"mx_done{L}"), 1)

                def divide(n):
                    g, c = divmod(n, NC)
                    dve.wait_ge(S(f"pv_sb{L}"), n + 1)
                    ch.link(v.stream_shuffle(den, pv_sb[:, n % 2, :], [DH] * 32))
                    ch.link(v.reciprocal(rden, den))
                    v.tensor_tensor(yT[:, g, c * CH:(c + 1) * CH], pv_sb[:, n % 2, :], rden, ALU.mult)\
                     .then_inc(S(f"yT{L}"), 1)

                for u in range(UPG):
                    max_unit(0, u)
                for g in range(NG):
                    nxt = list(range(UPG)) if g + 1 < NG else []
                    for s in range(NSTEP + 1):
                        todo = 4 if s < 10 else (0 if s == 10 else 1)
                        for _ in range(min(todo, len(nxt))):
                            max_unit(g + 1, nxt.pop(0))
                        if s == 1 and g > 0:
                            divide(NC * g - 1)
                        if s == TPC + 2:
                            divide(NC * g)
                divide(NC * NG - 1)

                for tiles in halves:
                    for i in tiles:
                        dve.wait_ge(S(f"attn_proj{L}"), i + 1)
                        if L == 0:
                            v.tensor_tensor(hb[:, i, :], ps[:, 4 + i % 4, 0:D], bias_o[:, :], ALU.add)\
                             .then_inc(S(f"ao_sb{L}"), 1)
                        else:
                            v.tensor_copy(hb[:, i, :], ps[:, 4 + i % 4, 0:D]).then_inc(S(f"ao_sb{L}"), 1)
                    dve.wait_ge(S(f"ao_sb{L}"), tiles[-1] + 1)
                    row_stats(hb, tiles)
                    for i in tiles:
                        ch.step(norm(hb, hb, i))
                    ch.wait()
                    for i in tiles:
                        ch.step(v.tensor_tensor(xres[:, i, :], xres[:, i, :], hb[:, i, :], ALU.add))
                    ch.wait()
                    row_stats(xres, tiles)
                    if L == 0:
                        for i in tiles:
                            norm(xn, xres, i).then_inc(S(f"xn_f{L}"), 1)
                    else:
                        for i in tiles:
                            ch.step(norm(hb, xres, i))
                        ch.wait()
                        for i in tiles:
                            ch.step(v.bn_stats(stats[:, i, :], hb[:, i, :]))
                        ch.wait()
                        for i in tiles:
                            ch.step(v.bn_aggr(mv[:, i, :], stats[:, i, :]))
                        ch.wait()
                        t0, t1 = tiles[0], tiles[-1] + 1
                        ch.link(v.tensor_tensor(msq[:, t0:t1], mv[:, t0:t1, 0], mv[:, t0:t1, 0], ALU.mult))
                        ch.link(v.tensor_tensor(msq[:, t0:t1], msq[:, t0:t1], mv[:, t0:t1, 1], ALU.add))
                        inv_sqrt(msq, msq[:, t0:t1], RMS_EPS, t0, t1)
                        for i in tiles:
                            v.scalar_tensor_tensor(xn[:, i, :], hb[:, i, :], msq[:, i:i + 1], w_nm[:, :],
                                                   ALU.mult, ALU.mult).then_inc(S(f"xn_f{L}"), 1)

                dve.wait_ge(S(f"logits_ps{L}"), 1)
                lps = ps[:, 4, 0:NT * NR[L]].rearrange("p (t e) -> p t e", t=NT)
                if L == 0:
                    ins = v.tensor_tensor(lg[:, :, 0:E], lps,
                                          b_rt[:, :].rearrange("p (o e) -> p o e", o=1).broadcast_to([P, NT, E]), ALU.add)
                else:
                    ins = v.tensor_copy(lg[:, :, :], lps)
                ins.then_inc(S(f"logits_sb{L}"), 1)
                dve.wait_ge(S(f"logits_sb{L}"), 1)
                for i in range(NT):
                    ch.step(v.max(top[:, i, :], lg[:, i, 0:E]))
                ch.wait()
                for i in range(NT):
                    ch.step(v.max_index(tix[:, i, :], top[:, i, :], lg[:, i, 0:E]))
                ch.wait()
                ch.link(v.tensor_copy(tixf[:, :, :], tix[:, :, 0:K]))
                ch.link(v.tensor_tensor(
                    onehot, iota_e[:, :].rearrange("p (a b e) -> p a b e", a=1, b=1).broadcast_to([P, NT, K, E]),
                    tixf[:, :, :].rearrange("p t (k o) -> p t k o", o=1).broadcast_to([P, NT, K, E]), ALU.is_equal))
                with nc.allow_low_precision(reason="zeros and ones"):
                    v.tensor_reduce(picked[:, :, :], onehot.rearrange("p t k e -> p t e k"), AX.X, ALU.add)\
                     .then_inc(S(f"picked{L}"), 1)
                ins = v.tensor_tensor(gate[:, :, :], top[:, :, 0:K], top[:, :, 0:1].broadcast_to([P, NT, K]), ALU.subtract)
                if L == 1:
                    ch.step(ins)
                    ins = v.tensor_tensor(gall[:, :, :], lg[:, :, 0:E], top[:, :, 0:1].broadcast_to([P, NT, E]),
                                          ALU.subtract)
                    ch.wait()
                ins.then_inc(S(f"less_top{L}"), 1)

                dve.wait_ge(S(f"ranks{L}"), 1)
                rank = ps[:, 5, 0:NT * E].rearrange("p (t e) -> p t e", t=NT)
                if L == 0:
                    ch.link(v.tensor_copy(cnt[:, :], ps[:, 5, NT * E:(NT + 1) * E]))
                    levels = big1[:, 0:E * NT].rearrange("p (e t) -> p e t", e=E)
                    ch.link(v.tensor_tensor(levels, cnt[:, :].rearrange("p (e o) -> p e o", o=1).broadcast_to([P, E, NT]),
                                            lev[:, :].rearrange("p (o t) -> p o t", o=1).broadcast_to([P, E, NT]),
                                            ALU.is_gt))
                    ch.link(v.tensor_reduce(ntile[:, :], levels, AX.X, ALU.add))
                    sq = big1.rearrange("p (e f) -> p e f", e=E)
                    ch.link(v.tensor_tensor(sq, lt_e[:, :, :],
                                            ntile[:, :].rearrange("p (o f) -> p o f", o=1).broadcast_to([P, E, E]),
                                            ALU.mult))
                    ch.link(v.tensor_reduce(tbeg[:, :], sq, AX.X, ALU.add))
                    ch.step(v.tensor_tensor(tend[:, :], tbeg[:, :], ntile[:, :], ALU.add))
                    ch.link(v.tensor_scalar(tbeg[:, :], tbeg[:, :], float(P), None, ALU.mult))
                    v.tensor_tensor(dest[:, :, :], rank,
                                    tbeg[:, :].rearrange("p (o e) -> p o e", o=1).broadcast_to([P, NT, E]), ALU.add)\
                     .then_inc(S(f"dest_done{L}"), 1)
                else:
                    ch.step(v.tensor_scalar(dest[:, :, :], rank, CAP - 0.5, SKIP, ALU.is_gt, ALU.mult))
                    ch.link(v.tensor_scalar(tbeg[:, :], iota_e[:, :], float(CAP), None, ALU.mult))
                    ch.link(v.tensor_tensor(dest[:, :, :], dest[:, :, :], rank, ALU.add))
                    v.tensor_tensor(dest[:, :, :], dest[:, :, :],
                                    tbeg[:, :].rearrange("p (o e) -> p o e", o=1).broadcast_to([P, NT, E]), ALU.add)\
                     .then_inc(S(f"dest_done{L}"), 1)
                dve.wait_ge(S(f"dest_done{L}"), 1)
                for k in range(K):
                    ch.step(v.tensor_tensor(prod[:, :, k, :], onehot[:, :, k, :], dest[:, :, :], ALU.mult))
                ch.wait()
                ch.link(v.tensor_reduce(slot[:, :, :], prod, AX.X, ALU.add))
                v.tensor_copy(slot_i[:, :], slot[:, :, :].rearrange("p t k -> p (t k)")).then_inc(S(f"slot_no{L}"), 1)
                last_slot = float(TILES[L] * P - 1)
                if L == 1:
                    ch.step(v.tensor_scalar(prod[:, :, :, 0], slot[:, :, :], last_slot + 0.5, None, ALU.is_lt))
                ch.link(v.tensor_scalar(slot_g[:, :], slot[:, :, :].rearrange("p t k -> p (t k)"), last_slot, None, ALU.min))
                dve.wait_ge(S(f"gate_exp{L}"), 1 + L)
                ch.link(v.tensor_reduce(gsum[:, :], gate[:, :, :] if L == 0 else gall[:, :, :], AX.X, ALU.add))
                ch.link(v.reciprocal(gsum[:, :], gsum[:, :]))
                if L == 0:
                    ch.link(v.tensor_scalar(gsum[:, :], gsum[:, :], 1.8, None, ALU.mult))
                ch.link(v.tensor_tensor(gate[:, :, :], gate[:, :, :],
                                        gsum[:, :].rearrange("p (t o) -> p t o", o=1).broadcast_to([P, NT, K]), ALU.mult))
                if L == 1:
                    ch.link(v.tensor_tensor(gate[:, :, :], gate[:, :, :], prod[:, :, :, 0], ALU.mult))
                    dve.wait_ge(S("sgate"), 1)
                    v.tensor_scalar(sgate[:, :], sgate[:, :], 1.0, 0.5, ALU.add, ALU.mult).then_inc(S("sgate_done"), 1)
                if L == 0:
                    m3 = tmap.rearrange("p (i e) -> p i e", i=TILES[0])
                    ch.link(v.tensor_tensor(
                        m3, iota_t[:, :].rearrange("p (i o) -> p i o", o=1).broadcast_to([1, TILES[0], E]),
                        tend[0:1, :].rearrange("p (o e) -> p o e", o=1).broadcast_to([1, TILES[0], E]), ALU.is_ge))
                    ch.link(v.tensor_reduce(texp, m3, AX.X, ALU.add))
                    v.tensor_scalar(texp_i[:, :], texp, float(E - 1), None, ALU.min).then_inc(S("tile_expert"), 1)

                C = CHUNK[L]
                nsc = SHARED[L] // C
                actv = acts[:, 0:nsc * T].rearrange("p (c t) -> p c t", c=nsc)
                for u in range(nsc * NC):
                    n, j = divmod(u, nsc)
                    dve.wait_ge(S(f"s_silu{L}"), u + 1)
                    v.tensor_tensor(actv[0:C, j, n * CH:(n + 1) * CH], ps[0:C, 2 * (u % 2) + 1, :],
                                    ssilu[0:C, u % 2, :], ALU.mult).then_inc(S(f"s_act{L}"), 1)

                def e_mult(blk, r, first):
                    i = blk * RING + r
                    dve.wait_ge(S("e_silu"), E0[L] + i + 1)
                    if not (first and r < 2):
                        dve.wait_ge(S("e_down"), E0[L] + i - 1)
                    v.tensor_tensor(eact[0:C, r % 2, :], ps[0:C, 2 + r % 2, 2 * P:4 * P], esilu[0:C, r % 2, :],
                                    ALU.mult).then_inc(S("e_act"), 1)

                def e_copy(blk, r, first):
                    i = blk * RING + r
                    dve.wait_ge(S("e_down"), E0[L] + i + 1)
                    if not (first and r < 2):
                        dve.wait_ge(S(f"e_out_{r % 2}"), 16 * (E0[L] // 2 + 2 * blk + r // 2))
                    v.tensor_copy(erows[:, r % 2, :], ps[:, 4 + r % 2, 0:D]).then_inc(S("e_sb"), 1)

                def e_block(blk, first):
                    for r in range(RING):
                        e_mult(blk, r, first)
                        if not (first and r == 0):
                            e_copy(blk + (-1 if r == 0 else 0), (r - 1) % RING, first)

                e_block(0, True)
                with dve.Fori(1, TILES[L] // RING) as blk:
                    e_block(blk, False)
                e_copy(TILES[L] // RING - 1, RING - 1, False)

                dve.wait_ge(S(f"sh_sb{L}"), NT)
                for i in range(NT):
                    dve.wait_ge(S(f"gathered{L}_{i % 2}"), 16 * K * (i // 2 + 1))
                    for k in range(K):
                        ins = v.scalar_tensor_tensor(shout[:, i, :], gath[:, i % 2, k, :], gate[:, i, k:k + 1],
                                                     shout[:, i, :], ALU.mult, ALU.add)
                        if k < K - 1:
                            ch.link(ins)
                    ins.then_inc(S(f"summed{L}"), 1)
                    dve.wait_ge(S(f"summed{L}"), i + 1)
                    if L == 1:
                        ch.link(v.tensor_tensor(shout[:, i, :], shout[:, i, :], hb[:, i, :], ALU.add))
                    row_stats(shout, [i])
                    ch.link(norm(shout, shout, i))
                    ins = v.tensor_tensor(xres[:, i, :], xres[:, i, :], shout[:, i, :], ALU.add)
                    if L == 0:
                        ch.link(ins)
                    else:
                        ins.then_inc(S("final"), 1)


def kernel(**inputs):
    import concourse.bacc as bacc
    from concourse.bass_utils import run_bass_kernel_spmd

    g = {k: np.asarray(v) for k, v in inputs.items()}
    d = {}
    d["x"] = g["L0_attn_x"].reshape(T, D)
    d["qkv0"] = np.stack([g[f"L0_attn_{n}"].transpose(1, 0, 2).reshape(D, D) for n in ("Wq", "Wk", "Wv")])
    d["qkv1"] = np.stack([g[f"L1_attn_{n}"].T for n in ("wq", "wk", "wv")])
    d["wo0"] = g["L0_attn_Wo"]
    d["wo1"] = g["L1_attn_wo"].T
    d["bqk"] = np.stack([g[f"L0_attn_{n}"].reshape(KD, P) for n in ("bq", "bk")]).transpose(2, 0, 1)
    d["bv"] = g["L0_attn_bv"].reshape(D)
    d["bo"] = g["L0_attn_bo"]
    d["router_b"] = g["L0_ffn_router_b"]
    d["w_norm"] = g["L1_ffn_w_norm"]
    d["router0"] = g["L0_ffn_router_w"].T
    d["router1"] = np.concatenate([g["L1_ffn_w_router"], g["L1_ffn_w_shared_gate"]], axis=1)

    def up(gate, upw):
        both = np.stack([gate, upw], axis=-2)
        s = both.shape
        both = both.reshape(s[:-3] + (KD, P) + s[-2:])
        n = both.ndim
        return both.transpose(tuple(range(n - 4)) + (n - 3, n - 4, n - 2, n - 1))

    def down(w, c):
        return w.reshape(E, -1, c, D).transpose(0, 2, 1, 3).reshape(E, c, -1)

    d["gu0"] = up(g["L0_ffn_gate_w"].transpose(0, 2, 1), g["L0_ffn_up_w"].transpose(0, 2, 1)).reshape(E, P, -1)
    d["gu1"] = up(g["L1_ffn_w_gate"], g["L1_ffn_w_up"]).reshape(E, P, -1)
    d["dn0"] = down(g["L0_ffn_down_w"].transpose(0, 2, 1), CHUNK[0])
    d["dn1"] = down(g["L1_ffn_w_down"], CHUNK[1])
    d["sgu0"] = up(g["L0_ffn_shared_gate_w"].T, g["L0_ffn_shared_up_w"].T).reshape(P, KD, -1)
    d["sgu1"] = up(g["L1_ffn_sw_gate"], g["L1_ffn_sw_up"]).reshape(P, KD, -1)
    d["sdn0"] = g["L0_ffn_shared_down_w"].T
    d["sdn1"] = g["L1_ffn_sw_down"]
    pos = np.arange(T, dtype=np.float32)[:, None]
    inv = (np.float32(10000.0) ** (-(np.arange(0, DH, 2, dtype=np.float32) / np.float32(DH)))).astype(np.float32)
    ang = np.repeat(pos * inv, 2, axis=1)
    sign = np.where(np.arange(DH) % 2 == 0, -1.0, 1.0).astype(np.float32)
    d["cos"] = np.tile(np.cos(ang).T, (P // DH, 1)).astype(np.float32)
    d["sin"] = np.tile((np.sin(ang) * sign).T, (P // DH, 1)).astype(np.float32)

    nc = bacc.Bacc("TRN2", target_bir_lowering=False, num_devices=1)
    arrays, args = {}, {}
    for name, x in d.items():
        x = np.ascontiguousarray(x)
        arrays[f"in_{name}"] = x
        args[name] = nc.dram_tensor(f"in_{name}", x.shape, mybir.dt.from_np(x.dtype), kind="ExternalInput").ap()
    out = nc.dram_tensor("out_x", (T, D), F32, kind="ExternalOutput").ap()
    build(nc, args, out)
    r = run_bass_kernel_spmd(nc, [arrays], core_ids=[0])
    return r.results[0]["out_x"].reshape(1, T, D)
```

```python
import numpy as np

import concourse.bass as bass
from concourse import mybir
from contextlib import ExitStack

F32 = mybir.dt.float32
BF16 = mybir.dt.bfloat16
I32 = mybir.dt.int32
U32 = mybir.dt.uint32
ALU = mybir.AluOpType
ACT = mybir.ActivationFunctionType
AX = mybir.AxisListType

P = 128
T = 1024
NT = T // P
D = 256
KD = D // P
H = 16
DH = D // H
HG = 4
NG = H // HG
CH = 512
NC = T // CH
TPC = CH // P
E = 32
K = 4
SCALE = DH ** -0.5
LN_EPS = 1e-5
RMS_EPS = 1e-6
BIG = 1.0e30
SKIP = float(1 << 20)
CAP = 128
PARTS = 3
Q_PARTS = ((0, 3, 0), (3, 3, 1), (6, 1, 2))
K_PARTS = ((0, 3), (3, 3), (6, 1))
NPROD = 7
KQ = NPROD * DH
NSH = 2
KX = KQ + NSH
ONES_AT = KQ // 32 * 32

INTER = (192, 176)
SHARED = (192, 704)
HALF = P // 2
FULL = 1
SFULL = tuple(w // P for w in SHARED)
UPC = 2 * FULL + 1
EW = KD * UPC * P + D
TILES = (64, 32)
E0 = (0, TILES[0])
R0 = (0, TILES[0] // 4)
NR = (E, E + 1)
RING = 4
SLOTS_AT = D
GATES_AT = D + K
TOKEN_AT = D + 2 * K
W = TOKEN_AT + 1


def exp_steps():
    return [(c, b) for c in range(NC) for b in range(TPC * (c + 1))]


STEPS = exp_steps()
NSTEP = len(STEPS)


def max_units():
    units = []
    for i in range(NT):
        if i >= TPC:
            units += [(0, i, hh, 1, 0, CH) for hh in range(HG)]
        w = (i % TPC + 1) * P
        n = {1: 4, 2: 2, 3: 1, 4: 1}[w // P]
        units += [(1, i, hh, n, (i // TPC) * CH, w) for hh in range(0, HG, n)]
    return units


MAX_UNITS = max_units()
NMAX = len(MAX_UNITS)
RB = 3
PB = 3


def schedule():
    out = [("max", 0, u) for u in range(NMAX)] + [("rows", 0, c) for c in range(NC)]
    last = NG * NSTEP
    for st in range(last + 2):
        g, s = divmod(st, NSTEP)
        more = [("max", g + 1, u) for u in range(NMAX)][4 * s:4 * s + 4] if g + 1 < NG else []
        if g + 1 < NG and s == NSTEP - 2:
            more += [("rows", g + 1, c) for c in range(NC)]
        if s == TPC + 3 and g < NG:
            more.append(("turn", NC * g))
        if s == 3 and 0 < g < NG:
            more.append(("turn", NC * g - 1))
        for p in range(2):
            if st < last:
                out.append(("score", st, p))
            out += more[:1]
            more = more[1:]
        if st >= 2:
            out.append(("weigh", st - 2))
        out += more
    return out + [("turn", NC * NG - 1)]


SCHEDULE = schedule()
UNITS = [x for x in SCHEDULE if x[0] in ("max", "rows", "turn")]
UNIT_NO = {x: n for n, x in enumerate(UNITS)}
EMPTIED = [sum(y[0] != "rows" for y in UNITS[:n + 1]) for n in range(len(UNITS))]
ROWS_DONE = [sum(y[0] == "rows" for y in UNITS[:n + 1]) for n in range(len(UNITS))]
DIAGONAL = [b >= TPC * c for c, b in STEPS]


def masked_steps(st):
    g, s = divmod(st, NSTEP)
    return g * sum(DIAGONAL) + sum(DIAGONAL[:s + 1])


NORMS = (("attention0a", TPC), ("attention0b", TPC), ("output0", NT), ("experts0", NT), ("sum0", NT),
         ("attention1", NT), ("output1", NT), ("experts1", NT), ("sum1", NT))
SCALED = {name: n + 1 for n, (name, _) in enumerate(NORMS)}
NORMED = {name: sum(t for _, t in NORMS[:n]) for n, (name, _) in enumerate(NORMS)}


DVE_PARTS = ((0, 0), (0, 1))
POOL_PARTS = ((1, 0), (1, 1))


class Chain:

    def __init__(self, eng, sem):
        self.eng, self.sem, self.n = eng, sem, 0

    def step(self, ins):
        self.n += 1
        ins.then_inc(self.sem, 1)

    def wait(self, back=0):
        self.eng.wait_ge(self.sem, self.n - back)

    def link(self, ins):
        self.step(ins)
        self.wait()


def build(nc, a, out):
    ctx = ExitStack()
    with ctx:
        sems = {}

        def S(name):
            if name not in sems:
                sems[name] = ctx.enter_context(nc.semaphore(name))
            return sems[name]

        def left(L, m, j, part):
            who, those = ("pool", POOL_PARTS) if (m, j) in POOL_PARTS else ("dve", DVE_PARTS)
            return S(f"left{part}_{who}"), len(those) * L + those.index((m, j)) + 1

        def take_part(eng, L, m, j, part):
            eng.wait_ge(S(f"parts_p{part}_{L}"), 2 * m + j + 1)
            q = qkf[:, j, m, :]
            eng.tensor_tensor(q if part == 1 else parts[:, j, m, 2, :], q, parts[:, j, m, part - 1, :], ALU.subtract)\
               .then_inc(left(L, m, j, part)[0], 1)

        def sb(name, shape, dt=F32):
            return ctx.enter_context(nc.sbuf_tensor(name, shape, dt))

        qk_parts = [nc.dram_tensor(f"qk_parts{L}", (2, PARTS, DH, H, T), BF16).ap() for L in range(2)]
        slot_rows = [nc.dram_tensor(f"slot_rows{L}", (TILES[L] * P, W), F32).ap() for L in range(2)]
        acc = [[nc.dram_tensor(f"acc{L}_{x}", (T + P, D), F32).ap() for x in range(2)] for L in range(2)]

        xres = sb("xres", [P, NT, D])
        xn = sb("xn", [P, NT, W])
        xT = sb("xT", [P, KD, T])
        hb = sb("hb", [P, NT, D])
        identf = sb("identf", [P, P])
        identb = sb("identb", [P, P], BF16)
        mask_q = sb("mask_q", [P, P], BF16)
        before = sb("before", [P, P], BF16)
        ones = sb("ones", [P, P], BF16)
        stats = sb("stats", [P, NT, 6])
        mv = sb("mv", [P, NT, 2])
        rstd = sb("rstd", [P, NT])
        shift = sb("shift", [P, NT])
        ones_row = sb("ones_row", [1, P])
        msq = sb("msq", [P, NT])
        rs_half = sb("rs_half", [P, NT])
        rs_sq = sb("rs_sq", [P, NT])
        w_qkv = sb("w_qkv", [P, 3, KD, D])
        w_o = sb("w_o", [P, KD, D])
        bias_qk = sb("bias_qk", [P, 2, KD])
        bias_v = sb("bias_v", [P, D])
        bias_o = sb("bias_o", [P, D])
        cos_t = sb("cos_t", [P, T])
        sin_t = sb("sin_t", [P, T])
        V = sb("V", [P, NT, H, 32])
        w_sgu = sb("w_sgu", [P, KD, 2 * SHARED[1]])
        w_sdn = sb("w_sdn", [P, SFULL[1] + 1, D])
        w_rt = sb("w_rt", [P, KD, E + 1])
        b_rt = sb("b_rt", [P, E])
        w_nm = sb("w_nm", [P, D])
        QA = sb("QA", [P, H, T], BF16)
        KA = sb("KA", [P, H, T], BF16)
        X = sb("X", [P, 10240])
        qkf = X[:, 0:4096].rearrange("p (a m t) -> p a m t", a=2, m=KD)
        parts = X[:, 4096:10240].bitcast(BF16).rearrange("p (a m r t) -> p a m r t", a=2, m=KD, r=PARTS)
        probs = X[:, 0:PB * 2048].rearrange("p (n h t) -> p n h t", n=PB, h=HG)
        pv_sb = X[:, PB * 2048:PB * 2048 + 1024].rearrange("p (n t) -> p n t", n=2)
        y = X[:, PB * 2048 + 1024:PB * 2048 + 3072].rearrange("p (t n) -> p t n", t=NT)
        swapped = V[:, :, :, :].rearrange("p a b c -> p (a b c)")[:, 0:2 * T].rearrange("p (a t) -> p a t", a=2)
        by_cos = V[:, :, :, :].rearrange("p a b c -> p (a b c)")[:, 2 * T:4 * T].rearrange("p (a t) -> p a t", a=2)
        rden = sb("rden", [P, 2, TPC, HG])
        mx = sb("mx", [P, 2, NT, HG])
        nb = sb("nb", [P, NT, NSH, HG], BF16)
        mT = sb("mT", [NSH * HG, T], BF16)
        acts = QA[:, :, :].rearrange("p h t -> p (h t)").bitcast(F32)
        KAf = KA[:, :, :].rearrange("p h t -> p (h t)").bitcast(F32)
        rows = X[:, 0:RING * W].rearrange("p (r n) -> p r n", r=RING)
        rowsT = X[:, 1088:1600].rearrange("p (r k n) -> p r k n", r=2, k=KD)
        eact = X[:, 1600:2112].rearrange("p (r n) -> p r n", r=2)
        esilu = X[:, 2112:2624].rearrange("p (r n) -> p r n", r=2)
        erows = X[:, 2624:3136].rearrange("p (r n) -> p r n", r=2)
        ssilu = X[:, 3072:4096].rearrange("p (r n) -> p r n", r=2)
        shout = X[:, 4096:6144].rearrange("p (t n) -> p t n", t=NT)
        sum_odd = X[:, 6144:8192].rearrange("p (t n) -> p t n", t=NT)
        onehot = X[:, 8192:9216].rearrange("p (t k e) -> p t k e", t=NT, k=K)
        prod = X[:, 9216:10240].rearrange("p (t k e) -> p t k e", t=NT, k=K)
        w_ex = KAf[:, 0:RING * EW].rearrange("p (r n) -> p r n", r=RING)
        w_rest = KAf[:, RING * EW:RING * (EW + D)].rearrange("p (r n) -> p r n", r=RING)
        empty = sb("empty", [P, W])
        own_first = sb("own_first", [P, RING])
        pause = sb("pause", [P, RING])
        own = sb("own", [P, RING])
        mine = sb("mine", [P, RING, K])
        egate = sb("egate", [P, RING])
        token = sb("token", [P, RING], I32)
        iota_e = sb("iota_e", [P, E])
        iota_t = sb("iota_t", [1, TILES[0]])
        lt_e = sb("lt_e", [P, E, E], BF16)
        lev = sb("lev", [P, NT])
        lg = sb("lg", [P, NT, E + 1])
        top = sb("top", [P, NT, 8])
        tix = sb("tix", [P, NT, 8], U32)
        tixf = sb("tixf", [P, NT, K])
        picked = sb("picked", [P, NT, E], BF16)
        gate = sb("gate", [P, NT, K])
        gall = sb("gall", [P, NT, E])
        gsum = sb("gsum", [P, NT])
        sgate = sb("sgate", [P, NT])
        cnt = sb("cnt", [P, E])
        ntile = sb("ntile", [P, E])
        tbeg = sb("tbeg", [P, E])
        tend = sb("tend", [P, E])
        big1 = X[:, 0:E * E]
        dest = sb("dest", [P, NT, E])
        slot = sb("slot", [P, NT, K])
        slot_i = sb("slot_i", [P, NT * K], I32)
        texp = X[0:1, 0:TILES[0]]
        texp_i = sb("texp_i", [1, TILES[0]], I32)
        tmap = X[0:1, 1024:1024 + TILES[0] * E]

        ps = ctx.enter_context(nc.psum_tensor("ps", [P, 8, CH], F32))

        block = ctx.enter_context(nc.Block())

        @block.sync
        def _(sp):
            xt = a["x"].rearrange("(t p) d -> p t d", p=P)
            for n in range(NC):
                sp.dma_start(xres[:, n * TPC:(n + 1) * TPC, :], xt[:, n * TPC:(n + 1) * TPC, :])\
                  .then_inc(S(f"x_in{n}"), 16)

            def attention_weights(L):
                sp.dma_start(w_qkv[:, :, :, :], a[f"qkv{L}"].rearrange("a (k p) n -> p a k n", p=P))\
                  .then_inc(S(f"w_qkv{L}"), 16)

            def output_weights(L):
                sp.dma_start(w_o[:, :, :], a[f"wo{L}"].rearrange("(k p) n -> p k n", p=P)).then_inc(S(f"w_o{L}"), 16)

            def row_of(dst, name, sem):
                n = dst.shape[1]
                sp.dma_start(dst[:, :], a[name].rearrange("(o n) -> o n", o=1).broadcast_to([P, n])).then_inc(sem, 16)

            def expert_constants(L):
                n, f = (2 * SFULL[L] + 1) * P, SFULL[L]
                sp.dma_start(w_rt[:, :, 0:NR[L]], a[f"router{L}"].rearrange("(k p) n -> p k n", p=P))\
                  .then_inc(S(f"w_router{L}"), 16)
                sp.dma_start(w_sgu[:, :, 0:n], a[f"sgu{L}"]).then_inc(S(f"w_shared{L}"), 16)
                sp.dma_start(w_sdn[:, 0:f, :], a[f"sdn{L}"][0:f * P, :].rearrange("(c p) n -> p c n", p=P))\
                  .then_inc(S(f"w_shared{L}"), 16)
                sp.dma_start(w_sdn[0:SHARED[L] - f * P, f, :], a[f"sdn{L}"][f * P:SHARED[L], :])\
                  .then_inc(S(f"w_shared{L}"), 16)

            def empty_slots(L, i):
                sp.dma_start(slot_rows[L][i * P:(i + 8) * P, :].rearrange("(t p) d -> p t d", p=P),
                             empty[:, :].rearrange("p (o d) -> p o d", o=1).broadcast_to([P, 8, W]))\
                  .then_inc(S(f"slots_empty{L}"), 16)

            def zero_sums(L):
                sp.dma_start(acc[L][0][T:T + P, :], empty[:, 0:D]).then_inc(S(f"acc_start{L}"), 16)
                sp.dma_start(acc[L][1].rearrange("(t p) d -> p t d", p=P),
                             empty[:, 0:D].rearrange("p (o d) -> p o d", o=1).broadcast_to([P, NT + 1, D]))\
                  .then_inc(S(f"acc_start{L}"), 16)

            attention_weights(0)
            sp.dma_start(bias_qk[:, :, :], a["bqk"]).then_inc(S("bias_qkv"), 16)
            row_of(bias_v, "bv", S("bias_qkv"))

            for L in range(2):
                if L == 1:
                    sp.wait_ge(S("attn_proj0"), NT)
                    attention_weights(1)
                for m in range(KD):
                    for part in range(PARTS):
                        for j in range(2):
                            if part < 2:
                                sp.wait_ge(S(f"parts_p{part + 1}_{L}"), 2 * m + j + 1)
                            else:
                                sp.wait_ge(*left(L, m, j, 2))
                            sp.dma_start(qk_parts[L][j, part, :, 8 * m:8 * (m + 1), :].rearrange("d h t -> h d t"),
                                         parts[:, j, m, part, :]).then_inc(S(f"parts_out{L}"), 16)
                    sp.wait_ge(S(f"parts_out{L}"), 16 * 2 * PARTS * (m + 1))
                    if m == 0:
                        sp.wait_ge(S(f"k_ones{L}"), 1)
                    for g in range(2 * m, 2 * m + 2):
                        hs = slice(HG * g, HG * (g + 1))
                        for r, n, part in Q_PARTS:
                            src = qk_parts[L][0, part:part + 1, :, hs, :].rearrange("o d h t -> o d (h t)")
                            sp.dma_start(QA[DH * r:DH * (r + n), hs, :].rearrange("p h t -> p (h t)"),
                                         src.broadcast_to([n, DH, HG * T])).then_inc(S(f"qa_rows{L}_{g}"), 16)
                        for r, n in K_PARTS:
                            src = qk_parts[L][1, 0:n, :, hs, :].rearrange("r d h t -> (r d) (h t)")
                            sp.dma_start(KA[DH * r:DH * (r + n), hs, :].rearrange("p h t -> p (h t)"), src)\
                              .then_inc(S(f"qa_rows{L}_{g}"), 16)
                if L == 0:
                    row_of(bias_o, "bo", S("bias_o"))
                    row_of(b_rt, "router_b", S("bias_o"))
                    row_of(w_nm, "w_norm", S("bias_o"))
                    sp.dma_start(cos_t[:, :], a["cos"]).then_inc(S("rope"), 16)
                    sp.dma_start(sin_t[:, :], a["sin"]).then_inc(S("rope"), 16)
                    expert_constants(0)
                    sp.wait_ge(S("empty"), 1)
                output_weights(L)
                for g in range(NG):
                    sp.wait_ge(S(f"maxT{L}"), NC * (g + 1))
                    for j in range(NSH):
                        sp.dma_start(QA[KQ + j:KQ + j + 1, HG * g:HG * (g + 1), :], mT[HG * j:HG * (j + 1), :])\
                          .then_inc(S(f"max_rows{L}"), 16)
                    if L == 0:
                        for i in range(16 * g, 16 * g + 16, 8):
                            empty_slots(0, i)
                        empty_slots(1, 8 * g)
                if L == 0:
                    zero_sums(0)
                    zero_sums(1)

                rest = INTER[L] - P

                def weights_in(r, e):
                    sp.dma_start(w_ex[:, r, :], a[f"ex{L}"][bass.ds(e, 1)].rearrange("o p n -> (o p) n"))\
                      .then_inc(S(f"w_ex_{r}"), 16)
                    sp.dma_start(w_rest[0:rest, r, :], a[f"dn{L}"][bass.ds(e, 1)].rearrange("o p n -> (o p) n"))\
                      .then_inc(S(f"w_rest_{r}"), 16)

                def experts_of(i):
                    if L == 1:
                        return [i + r for r in range(RING)]
                    return [sp.value_load(texp_i[0:1, bass.ds(i + r, 1)], min_val=0, max_val=E - 1)
                            for r in range(RING)]

                sp.wait_ge(S(f"attn_proj{L}"), NT)
                if L == 0:
                    sp.wait_ge(S("tile_expert"), 1)
                for r, e in enumerate(experts_of(0)):
                    weights_in(r, e)
                sp.wait_ge(S(f"sh_sb{L}"), NT)
                sp.dma_start(acc[L][0][0:T, :].rearrange("(t p) d -> p t d", p=P), shout).then_inc(S(f"acc_start{L}"), 16)
                with sp.Fori(RING, TILES[L] - RING + 1, RING) as i0:
                    for r, e in enumerate(experts_of(i0)):
                        sp.wait_ge(S("e_down"), E0[L] + i0 + (r - RING + 1))
                        weights_in(r, e)
                for x in range(2):
                    sp.wait_ge(S(f"added_{x}"), 16 * (E0[L] + TILES[L]) // 2)
                for n in range(NC):
                    for x, dst in enumerate((shout, sum_odd)):
                        sp.dma_start(dst[:, n * TPC:(n + 1) * TPC, :],
                                     acc[L][x][n * CH:(n + 1) * CH, :].rearrange("(t p) d -> p t d", p=P))\
                          .then_inc(S(f"sums_in{L}_{n}"), 16)
                if L == 0:
                    expert_constants(1)
            for n in range(NC):
                sp.wait_ge(S("final"), TPC * (n + 1))
                sp.dma_start(out.rearrange("(t p) d -> p t d", p=P)[:, n * TPC:(n + 1) * TPC, :],
                             xres[:, n * TPC:(n + 1) * TPC, :]).then_inc(S("out"), 16)
            sp.wait_ge(S("out"), 16 * NC)

        @block.gpsimd
        def _(pool):
            ch = Chain(pool, S("pool_own"))
            ch.step(pool.memset(empty[:, 0:TOKEN_AT], 0.0))
            ch.step(pool.iota(empty[:, TOKEN_AT:W].bitcast(I32), pattern=[[0, 1]], base=T, channel_multiplier=1))
            for i in range(NT):
                ch.step(pool.iota(xn[:, i, TOKEN_AT:W].bitcast(I32), pattern=[[0, 1]], base=i * P, channel_multiplier=1))
            ch.step(pool.iota(own_first[:, :], pattern=[[P, RING]], base=0, channel_multiplier=1,
                              allow_small_or_imprecise_dtypes=True))
            for t in (identf, identb, mask_q):
                ch.step(pool.memset(t[:, :], 0.0))
            for t in (before, ones, ones_row):
                ch.step(pool.memset(t[:, :], 1.0))
            ch.step(pool.memset(lt_e[:, :, :], 1.0))
            ch.step(pool.iota(iota_e[:, :], pattern=[[1, E]], base=0, channel_multiplier=0,
                              allow_small_or_imprecise_dtypes=True))
            ch.step(pool.iota(iota_t[:, :], pattern=[[1, TILES[0]]], base=0, channel_multiplier=0,
                              allow_small_or_imprecise_dtypes=True))
            ch.step(pool.iota(lev[:, :], pattern=[[P, NT]], base=0, channel_multiplier=0,
                              allow_small_or_imprecise_dtypes=True))
            ch.wait()
            pool.memset(empty[:, 0:1], 0.0).then_inc(S("empty"), 1)
            for t in (identf, identb):
                ch.step(pool.affine_select(out=t[:, :], in_=t[:, :], compare_op=ALU.not_equal, fill=1.0,
                                           base=0, pattern=[[-1, P]], channel_multiplier=1))
            ch.step(pool.affine_select(out=mask_q[:, :], in_=mask_q[:, :], compare_op=ALU.is_ge, fill=-BIG,
                                       base=0, pattern=[[-1, P]], channel_multiplier=1))
            ch.step(pool.affine_select(out=before[:, :], in_=before[:, :], compare_op=ALU.is_ge, fill=0.0,
                                       base=-1, pattern=[[1, P]], channel_multiplier=-1))
            ch.step(pool.affine_select(out=lt_e[:, :, :], in_=lt_e[:, :, :], compare_op=ALU.is_ge, fill=0.0,
                                       base=-1, pattern=[[1, E], [-1, E]], channel_multiplier=0))
            ch.wait()
            pool.memset(empty[:, 0:1], 0.0).then_inc(S("consts"), 1)
            pool.wait_ge(S("consts"), 1)

            for L in range(2):
                if L == 1:
                    pool.wait_ge(S("e_down"), TILES[0])
                    pool.wait_ge(S("e_seen"), TILES[0])
                pool.memset(KA[ONES_AT:KX, :, :], 1.0).then_inc(S(f"k_ones{L}"), 1)
                pool.wait_ge(S(f"k_ones{L}"), 1)
                for m in range(KD):
                    if L == 1:
                        if m == 0:
                            pool.wait_ge(S("rope"), 32)
                        for j in range(2):
                            n = 2 * m + j
                            pool.wait_ge(S(f"qk_sb{L}"), (n + 1) * NC)
                            if m == 1:
                                pool.wait_ge(S("roped"), n - 1)
                            pool.tensor_tensor(by_cos[:, j, :], qkf[:, j, m, :], cos_t[:, :], ALU.mult)\
                                .then_inc(S("by_cos"), 1)
                    for part in (1, 2):
                        for j in range(2):
                            if (m, j) in POOL_PARTS:
                                take_part(pool, L, m, j, part)
                if L == 1:
                    pool.wait_ge(S("roped"), 2 * KD)
                ch.link(pool.memset(V[:, :, :, DH + 1:], 0.0))
                pool.memset(V[:, :, :, DH:DH + 1], 1.0).then_inc(S(f"v_pad{L}"), 1)
                for st in range(NG * NSTEP):
                    c, b = STEPS[st % NSTEP]
                    if not DIAGONAL[st % NSTEP]:
                        continue
                    off = b * P - c * CH
                    block_p = probs[:, st % PB, :, off:off + P]
                    pool.wait_ge(S(f"exp{L}"), 2 * st + 2)
                    pool.affine_select(out=block_p, in_=block_p, compare_op=ALU.is_ge, fill=0.0, base=0,
                                       pattern=[[0, HG], [1, P]], channel_multiplier=-1).then_inc(S(f"masked{L}"), 1)

                pool.wait_ge(S(f"slots_empty{L}"), 16 * TILES[L] // 8)
                pool.wait_ge(S(f"slot_no{L}"), 1)
                for i in range(NT):
                    for k in range(K):
                        n = i * K + k
                        pool.indirect_dma_start(
                            out=slot_rows[L], out_offset=bass.IndirectOffsetOnAxis(ap=slot_i[:, n:n + 1], axis=0),
                            in_=xn[:, i, :], in_offset=None, bounds_check=TILES[L] * P - 1, oob_is_err=False)\
                            .then_inc(S(f"scattered{L}"), 16)
                def add_rows(blk, r):
                    i = blk * RING + r
                    pool.wait_ge(S("e_sb"), E0[L] + i + 1)
                    pool.tensor_tensor(pause[:, r:r + 1], empty[:, 0:1], empty[:, 1:2], ALU.add).then_inc(S("e_seen"), 1)
                    pool.wait_ge(S(f"acc_start{L}"), 16 * 3)
                    pool.indirect_dma_start(
                        out=acc[L][r % 2], out_offset=bass.IndirectOffsetOnAxis(ap=token[:, r:r + 1], axis=0),
                        in_=erows[:, r % 2, :], in_offset=None,
                        compute_op=ALU.add).then_inc(S(f"added_{r % 2}"), 16)

                for r in range(RING):
                    add_rows(0, r)
                with pool.Fori(1, TILES[L] // RING) as blk:
                    for r in range(RING):
                        add_rows(blk, r)

        @block.tensor
        def _(pe):
            pe.wait_ge(S("consts"), 1)

            def transposes(tag, src, ready):
                for n in range(NC):
                    pe.wait_ge(*ready[n])
                    for k in range(KD):
                        for i in range(TPC):
                            mm = pe.transpose(ps[:, KD * n + k, i * P:(i + 1) * P],
                                              src[:, TPC * n + i, k * P:(k + 1) * P], identf[:, :])
                        mm.then_inc(S(f"xTp_{tag}"), 1)

            for L in range(2):
                first = NORMED["attention0a" if L == 0 else "attention1"]
                transposes(f"a{L}", xn, [(S("normed"), first + TPC * (n + 1)) for n in range(NC)])
                pe.wait_ge(S(f"w_qkv{L}"), 16)
                u = 0
                for m in range(KD):
                    for j in range(2):
                        for n in range(NC):
                            if m == 0:
                                pe.wait_ge(S(f"xT_a{L}"), KD * (n + 1))
                            if u >= 4:
                                pe.wait_ge(S(f"qk_sb{L}"), u - 3)
                            for k in range(KD):
                                mm = pe.matmul(ps[:, 4 + u % 4, :], w_qkv[:, j, k, m * P:(m + 1) * P],
                                               xT[:, k, n * CH:(n + 1) * CH], start=(k == 0), stop=(k == KD - 1))
                            mm.then_inc(S(f"qk_ps{L}"), 1)
                            u += 1
                if L == 0:
                    pe.wait_ge(S("bias_qkv"), 32)
                for i in range(NT):
                    pe.wait_ge(S(f"qk_sb{L}"), 5 + i // 2)
                    dst = ps[:, 4 + i // 2, i % 2 * D:(i % 2 + 1) * D]
                    for k in range(KD):
                        mm = pe.matmul(dst, xT[:, k, i * P:(i + 1) * P], w_qkv[:, 2, k, :],
                                       start=(k == 0), stop=(k == KD - 1 and L == 1))
                    if L == 0:
                        mm = pe.matmul(dst, ones_row[:, :], bias_v[0:1, :], start=False, stop=True)
                    mm.then_inc(S(f"v_ps{L}"), 1)

                def unit(x):
                    n = UNIT_NO[x]
                    bank = n % RB
                    if n >= RB:
                        if UNITS[n - RB][0] == "rows":
                            pe.wait_ge(S(f"maxT{L}"), ROWS_DONE[n - RB])
                        else:
                            pe.wait_ge(S(f"unit_out{L}"), EMPTIED[n - RB])
                    if x[0] == "max":
                        _, g, u = x
                        _, i, h0, nh, s0, w = MAX_UNITS[u]
                        for j in range(nh):
                            h = HG * g + h0 + j
                            diag = s0 + w == (i + 1) * P
                            mm = pe.matmul(ps[:, bank, j * w:(j + 1) * w], QA[0:KQ, h, i * P:(i + 1) * P],
                                           KA[0:KQ, h, s0:s0 + w], start=True, stop=not diag)
                            if diag:
                                mm = pe.matmul(ps[:, bank, (j + 1) * w - P:(j + 1) * w], identb[:, :], mask_q[:, :],
                                               start=False, stop=True)
                    elif x[0] == "rows":
                        _, g, c = x
                        pe.wait_ge(S(f"neg_max{L}"), g + 1)
                        for i in range(TPC):
                            mm = pe.matmul(ps[0:NSH * HG, bank, i * P:(i + 1) * P],
                                           nb[:, TPC * c + i, :, :].rearrange("p a h -> p (a h)"), identb[:, :],
                                           start=True, stop=True)
                    else:
                        pe.wait_ge(S(f"pv_sb{L}"), x[1] + 1)
                        for i in range(TPC):
                            mm = pe.transpose(ps[:, bank, i * P:(i + 1) * P], pv_sb[:, x[1] % 2, i * P:(i + 1) * P],
                                              identf[:, :])
                    mm.then_inc(S(f"unit{L}"), 1)

                def scores(st, p):
                    g, s = divmod(st, NSTEP)
                    c, b = STEPS[s]
                    off = max(0, b * P - c * CH)
                    if s == 0 and p == 0:
                        pe.wait_ge(S(f"max_rows{L}"), 16 * NSH * (g + 1))
                    if st >= 1:
                        pe.wait_ge(S(f"exp{L}"), 2 * st + p - 1)
                    for x in range(2):
                        h = HG * g + 2 * p + x
                        mm = pe.matmul(ps[:, 4 + 2 * p + x, off:CH], KA[0:KX, h, b * P:(b + 1) * P],
                                       QA[0:KX, h, c * CH + off:(c + 1) * CH], start=True, stop=True)
                    mm.then_inc(S(f"sc{L}"), 1)

                def weigh(st):
                    g, s = divmod(st, NSTEP)
                    c, b = STEPS[s]
                    off = max(0, b * P - c * CH)
                    n = NC * g + c
                    pe.wait_ge(S(f"exp{L}"), 2 * st + 2)
                    if DIAGONAL[s]:
                        pe.wait_ge(S(f"masked{L}"), masked_steps(st))
                    if b == 0 and n >= 1:
                        pe.wait_ge(S(f"pv_sb{L}"), n)
                    for x in range(HG):
                        mm = pe.matmul(ps[32 * x:32 * x + 32, RB, off:CH], V[:, b, HG * g + x, :],
                                       probs[:, st % PB, x, off:CH], start=(b == 0), stop=(b == TPC * (c + 1) - 1))
                    mm.then_inc(S(f"pv{L}"), 1)

                for x in SCHEDULE:
                    if x[0] == "max" and x[2] == 0:
                        pe.wait_ge(S(f"qa_rows{L}_{x[1]}"), 16 * (len(Q_PARTS) + len(K_PARTS)))
                    if x == ("score", 0, 0):
                        pe.wait_ge(S(f"v_sb{L}"), NT)
                        pe.wait_ge(S(f"v_pad{L}"), 1)
                        pe.wait_ge(S(f"k_ones{L}"), 1)
                    if x[0] == "score":
                        scores(*x[1:])
                    elif x[0] == "weigh":
                        weigh(x[1])
                    else:
                        unit(x)
                units_out = (S(f"unit_out{L}"), EMPTIED[-1])
                transposes(f"y{L}", y, [units_out] * NC)
                pe.wait_ge(S(f"w_o{L}"), 16)
                pe.wait_ge(S(f"exp{L}"), 2 * NSTEP * NG)
                if L == 0:
                    pe.wait_ge(S("bias_o"), 48)
                for i in range(NT):
                    pe.wait_ge(S(f"xT_y{L}"), KD * (i // TPC + 1))
                    dst = ps[:, 4 + i // 2, i % 2 * D:(i % 2 + 1) * D]
                    for k in range(KD):
                        mm = pe.matmul(dst, xT[:, k, i * P:(i + 1) * P], w_o[:, k, :],
                                       start=(k == 0), stop=(k == KD - 1 and L == 1))
                    if L == 0:
                        mm = pe.matmul(dst, ones_row[:, :], bias_o[0:1, :], start=False, stop=True)
                    mm.then_inc(S(f"attn_proj{L}"), 1)

                xn_done = (S("normed"), NORMED["experts0"]) if L == 0 else (S("xn_f1"), 0)
                transposes(f"f{L}", xn, [(xn_done[0], xn_done[1] + TPC * (n + 1)) for n in range(NC)])
                pe.wait_ge(S(f"w_router{L}"), 16)
                for i in range(NT):
                    if i % TPC == 0:
                        pe.wait_ge(S(f"xT_f{L}"), KD * (i // TPC + 1))
                    for k in range(KD):
                        mm = pe.matmul(ps[:, 4, i * NR[L]:(i + 1) * NR[L]], xT[:, k, i * P:(i + 1) * P],
                                       w_rt[:, k, 0:NR[L]], start=(k == 0), stop=(k == KD - 1))
                mm.then_inc(S(f"logits_ps{L}"), 1)

                pe.wait_ge(S(f"w_shared{L}"), 48)
                srest, erest = SHARED[L] - SFULL[L] * P, INTER[L] - P
                nsc = SFULL[L] + 1

                def shared_up(u):
                    n, j = divmod(u, nsc)
                    if u >= 2:
                        pe.wait_ge(S(f"s_act{L}"), u - 1)
                    for x in range(2 if j < SFULL[L] else 1):
                        col = (x * SFULL[L] + j if j < SFULL[L] else 2 * SFULL[L]) * P
                        for k in range(KD):
                            mm = pe.matmul(ps[:, 2 * (u % 2) + x, :], w_sgu[:, k, col:col + P],
                                           xT[:, k, n * CH:(n + 1) * CH], start=(k == 0), stop=(k == KD - 1))
                    mm.then_inc(S(f"s_gu{L}"), 1)

                shared_up(0)
                shared_up(1)
                pe.wait_ge(S(f"picked{L}"), 1)
                for i in range(NT):
                    for j in range(i + 1):
                        mm = pe.matmul(ps[:, 5, i * E:(i + 1) * E], (ones if j < i else before)[:, :],
                                       picked[:, j, :], start=(j == 0), stop=(j == i))
                for j in range(NT):
                    mm = pe.matmul(ps[:, 5, NT * E:(NT + 1) * E], ones[:, :], picked[:, j, :],
                                   start=(j == 0), stop=(j == NT - 1))
                mm.then_inc(S(f"ranks{L}"), 1)
                for u in range(2, nsc * NC):
                    shared_up(u)
                actv = acts[:, 0:nsc * T].rearrange("p (c t) -> p c t", c=nsc)
                for i in range(NT):
                    pe.wait_ge(S(f"s_act{L}"), nsc * (i // TPC + 1))
                    if i >= 2:
                        pe.wait_ge(S(f"sh_sb{L}"), i - 1)
                    for j in range(nsc):
                        rows_j = P if j < SFULL[L] else srest
                        mm = pe.matmul(ps[:, 6 + i % 2, 0:D], actv[0:rows_j, j, i * P:(i + 1) * P],
                                       w_sdn[0:rows_j, j, :], start=(j == 0), stop=(j == nsc - 1))
                    mm.then_inc(S(f"sh_down{L}"), 1)

                def e_transpose(blk, r, first):
                    i = blk * RING + r
                    pe.wait_ge(S(f"rows_{r}"), 16 * (R0[L] + blk + 1))
                    if not (first and r < 2):
                        pe.wait_ge(S("rowsT"), E0[L] + i - 1)
                    for k in range(KD):
                        mm = pe.transpose(ps[:, r % 2, k * P:(k + 1) * P], rows[:, r, k * P:(k + 1) * P], identf[:, :])
                    mm.then_inc(S("e_tr"), 1)

                def e_up(blk, r, first):
                    i = blk * RING + r
                    pe.wait_ge(S("rowsT"), E0[L] + i + 1)
                    pe.wait_ge(S(f"w_ex_{r}"), 16 * (R0[L] + blk + 1))
                    if not (first and r < 2):
                        pe.wait_ge(S("e_act"), 2 * (E0[L] + i - 1))
                    for m in range(UPC):
                        for k in range(KD):
                            col = (k * UPC + m) * P
                            mm = pe.matmul(ps[:, 2 + r % 2, m * P:(m + 1) * P], w_ex[:, r, col:col + P],
                                           rowsT[:, r % 2, k, :], start=(k == 0), stop=(k == KD - 1))
                    mm.then_inc(S("e_up"), 1)

                def e_down(blk, r, first):
                    i = blk * RING + r
                    pe.wait_ge(S("e_act"), 2 * (E0[L] + i) + 2)
                    pe.wait_ge(S(f"w_rest_{r}"), 16 * (R0[L] + blk + 1))
                    if not (first and r < 2):
                        pe.wait_ge(S("e_sb"), E0[L] + i - 1)
                    pe.matmul(ps[:, 4 + r % 2, 0:D], eact[:, r % 2, 0:P], w_ex[:, r, KD * UPC * P:EW],
                              start=True, stop=False)
                    mm = pe.matmul(ps[:, 4 + r % 2, 0:D], eact[0:erest, r % 2, P:2 * P], w_rest[0:erest, r, :],
                                   start=False, stop=True)
                    mm.then_inc(S("e_down"), 1)

                def e_block(blk, first, last):
                    for r in range(RING):
                        if not (last and r == RING - 1):
                            e_transpose(blk + (r + 1) // RING, (r + 1) % RING, first and r + 1 < RING)
                        e_up(blk, r, first)
                        if not (first and r == 0):
                            e_down(blk + (-1 if r == 0 else 0), (r - 1) % RING, first)

                pe.wait_ge(S(f"logits_sb{L}"), 1)
                pe.wait_ge(S(f"dest_done{L}"), 1)
                pe.wait_ge(S(f"s_act{L}"), nsc * NC)
                pe.wait_ge(S(f"sh_sb{L}"), NT)
                e_transpose(0, 0, True)
                e_block(0, True, False)
                with pe.Fori(1, TILES[L] // RING - 1) as blk:
                    e_block(blk, False, False)
                e_block(TILES[L] // RING - 1, False, True)
                e_down(TILES[L] // RING - 1, RING - 1, False)

        @block.scalar
        def _(act):
            for L in range(2):
                def xT_copy(tag):
                    for n in range(NC):
                        for k in range(KD):
                            u = KD * n + k
                            act.wait_ge(S(f"xTp_{tag}"), u + 1)
                            nc.scalar.activation(xT[:, k, n * CH:(n + 1) * CH], ps[:, u, :], ACT.Copy)\
                              .then_inc(S(f"xT_{tag}"), 1)

                def norm(i, dst, src):
                    nc.scalar.activation(dst, src, ACT.Identity, bias=shift[:, i:i + 1], scale=rstd[:, i:i + 1])\
                      .then_inc(S("normed"), 1)

                for n in range(NC):
                    act.wait_ge(S("scaled"), SCALED["attention0a"] + n if L == 0 else SCALED["attention1"])
                    for i in range(TPC * n, TPC * (n + 1)):
                        norm(i, xn[:, i, 0:D], xres[:, i, :])
                xT_copy(f"a{L}")
                if L == 0:
                    act.wait_ge(S("bias_qkv"), 32)
                if L == 1:
                    act.wait_ge(S("summed0"), NC)
                for m in range(KD):
                    for j in range(2):
                        for n in range(NC):
                            u = (m * 2 + j) * NC + n
                            act.wait_ge(S(f"qk_ps{L}"), u + 1)
                            dst = qkf[:, j, m, n * CH:(n + 1) * CH]
                            if L == 0:
                                nc.scalar.activation(dst, ps[:, 4 + u % 4, :], ACT.Identity,
                                                     bias=bias_qk[:, j, m:m + 1]).then_inc(S(f"qk_sb{L}"), 1)
                            else:
                                nc.scalar.activation(dst, ps[:, 4 + u % 4, :], ACT.Copy).then_inc(S(f"qk_sb{L}"), 1)
                    for part in range(2):
                        for j in range(2):
                            n = 2 * m + j
                            if part == 0 and L == 0:
                                act.wait_ge(S(f"qk_sb{L}"), (n + 1) * NC)
                            if part == 0 and L == 1:
                                act.wait_ge(S("roped"), n + 1)
                            if part == 1:
                                act.wait_ge(*left(L, m, j, 1))
                            nc.scalar.activation(parts[:, j, m, part, :], qkf[:, j, m, :], ACT.Copy)\
                              .then_inc(S(f"parts_p{part + 1}_{L}"), 1)

                if L == 1:
                    act.wait_ge(S("roped"), 2 * KD)
                for i in range(NT):
                    act.wait_ge(S(f"v_ps{L}"), i // 2 * 2 + 2)
                    nc.scalar.activation(V[:, i, :, 0:DH],
                                         ps[:, 4 + i // 2, i % 2 * D:(i % 2 + 1) * D].rearrange("p (h d) -> p h d", h=H),
                                         ACT.Copy).then_inc(S(f"v_sb{L}"), 1)

                act.wait_ge(S(f"parts_out{L}"), 16 * 2 * KD * PARTS)

                def exps(st, p):
                    c, b = STEPS[st % NSTEP]
                    off = max(0, b * P - c * CH)
                    act.wait_ge(S(f"sc{L}"), 2 * st + p + 1)
                    if p == 0 and st >= PB:
                        act.wait_ge(S(f"pv{L}"), st - PB + 1)
                    nc.scalar.activation(probs[:, st % PB, 2 * p:2 * p + 2, off:CH], ps[:, 4 + 2 * p:6 + 2 * p, off:CH],
                                         ACT.Exp, scale=SCALE).then_inc(S(f"exp{L}"), 1)

                def pv_copy(n):
                    g, c = divmod(n, NC)
                    act.wait_ge(S(f"pv{L}"), NSTEP * g + (TPC if c == 0 else NSTEP))
                    if n >= 2:
                        act.wait_ge(S(f"unit{L}"), UNIT_NO[("turn", n - 2)] + 1)
                    nc.scalar.activation(pv_sb[:, n % 2, :], ps[:, RB, :], ACT.Copy).then_inc(S(f"pv_sb{L}"), 1)

                for x in SCHEDULE:
                    if x[0] == "score":
                        exps(*x[1:])
                    elif x[0] == "rows":
                        _, g, c = x
                        act.wait_ge(S(f"unit{L}"), UNIT_NO[x] + 1)
                        if g >= 1:
                            act.wait_ge(S(f"max_rows{L}"), 16 * NSH * g)
                        nc.scalar.activation(mT[:, c * CH:(c + 1) * CH], ps[0:NSH * HG, UNIT_NO[x] % RB, :],
                                             ACT.Copy).then_inc(S(f"maxT{L}"), 1)
                    elif x[0] == "weigh":
                        g, s = divmod(x[1], NSTEP)
                        if s in (TPC - 1, NSTEP - 1):
                            pv_copy(NC * g + (s == NSTEP - 1))
                xT_copy(f"y{L}")
                act.wait_ge(S("scaled"), SCALED[f"output{L}"])
                for i in range(NT):
                    norm(i, hb[:, i, :], ps[:, 4 + i // 2, i % 2 * D:(i % 2 + 1) * D])
                act.wait_ge(S("scaled"), SCALED[f"experts{L}"])
                for i in range(NT):
                    norm(i, xn[:, i, 0:D] if L == 0 else hb[:, i, :], xres[:, i, :])

                xT_copy(f"f{L}")
                srest, erest = SHARED[L] - SFULL[L] * P, INTER[L] - P
                nsc = SFULL[L] + 1
                act.wait_ge(S(f"less_top{L}"), 1)
                nc.scalar.activation(gate[:, :, :], gate[:, :, :], ACT.Exp).then_inc(S(f"gate_exp{L}"), 1)
                if L == 1:
                    nc.scalar.activation(gall[:, :, :], gall[:, :, :], ACT.Exp).then_inc(S(f"gate_exp{L}"), 1)
                    nc.scalar.activation(sgate[:, :], lg[:, :, E], ACT.Tanh, scale=0.5).then_inc(S("sgate"), 1)
                for u in range(nsc * NC):
                    act.wait_ge(S(f"s_gu{L}"), u + 1)
                    if u >= 2:
                        act.wait_ge(S(f"s_act{L}"), u - 1)
                    if u % nsc < SFULL[L]:
                        ins = nc.scalar.activation(ssilu[:, u % 2, :], ps[:, 2 * (u % 2), :], ACT.Silu)
                    else:
                        ins = nc.scalar.activation(ssilu[HALF:HALF + srest, u % 2, :], ps[0:srest, 2 * (u % 2), :],
                                                   ACT.Silu)
                    ins.then_inc(S(f"s_silu{L}"), 1)
                if L == 0:
                    for i in range(NT):
                        act.wait_ge(S("sh_down0"), i + 1)
                        nc.scalar.activation(shout[:, i, :], ps[:, 6 + i % 2, 0:D], ACT.Copy).then_inc(S("sh_sb0"), 1)

                def e_tile(blk, r, first):
                    i = blk * RING + r
                    act.wait_ge(S("e_tr"), E0[L] + i + 1)
                    if not (first and r < 2):
                        act.wait_ge(S("e_up"), E0[L] + i - 1)
                    nc.scalar.activation(rowsT[:, r % 2, :, :].rearrange("p k n -> p (k n)"),
                                         ps[:, r % 2, 0:D], ACT.Copy).then_inc(S("rowsT"), 1)

                def e_silu(blk, r, first):
                    i = blk * RING + r
                    act.wait_ge(S("e_up"), E0[L] + i + 1)
                    if not (first and r < 2):
                        act.wait_ge(S("e_act"), 2 * (E0[L] + i - 1))
                    nc.scalar.activation(esilu[:, r % 2, 0:P], ps[:, 2 + r % 2, 0:P], ACT.Silu).then_inc(S("e_silu"), 1)
                    nc.scalar.activation(esilu[HALF:HALF + erest, r % 2, P:2 * P], ps[0:erest, 2 + r % 2, 2 * P:3 * P],
                                         ACT.Silu).then_inc(S("e_silu"), 1)

                def rows_in(blk, r):
                    act.dma_start(rows[:, r, :], slot_rows[L][bass.ds((blk * RING + r) * P, P), :])\
                       .then_inc(S(f"rows_{r}"), 16)

                def e_block(blk, first, last):
                    for r in range(RING):
                        if not (last and r == RING - 1):
                            e_tile(blk + (r + 1) // RING, (r + 1) % RING, first and r + 1 < RING)
                        e_silu(blk, r, first)
                        if not last:
                            act.wait_ge(S("e_tr"), E0[L] + blk * RING + r + 1)
                            act.wait_ge(S("e_pick"), 2 * (E0[L] + blk * RING + r) + 2)
                            rows_in(blk + 1, r)

                act.wait_ge(S(f"scattered{L}"), 16 * NT * K)
                if L == 0:
                    act.wait_ge(S("tile_expert"), 1)
                for r in range(RING):
                    rows_in(0, r)
                e_tile(0, 0, True)
                e_block(0, True, False)
                with act.Fori(1, TILES[L] // RING - 1) as blk:
                    e_block(blk, False, False)
                e_block(TILES[L] // RING - 1, False, True)
                act.wait_ge(S("scaled"), SCALED[f"sum{L}"])
                for i in range(NT):
                    norm(i, shout[:, i, :], shout[:, i, :])

        @block.vector
        def _(dve):
            ch = Chain(dve, S("dve_own"))
            v = nc.vector

            def inv_sqrt(dst, src, eps, t0, t1):
                y, half, sq = dst[:, t0:t1], rs_half[:, t0:t1], rs_sq[:, t0:t1]
                ch.link(v.tensor_scalar(half, src, eps, None, ALU.add))
                ch.link(v.tensor_scalar(y.bitcast(I32), half.bitcast(I32), -0.5, float(0x5F3759DF), ALU.mult, ALU.add))
                ch.link(v.tensor_scalar(half, half, -0.5, None, ALU.mult))
                for _ in range(3):
                    ch.link(v.tensor_tensor(sq, y, y, ALU.mult))
                    ch.link(v.tensor_tensor(sq, sq, half, ALU.mult))
                    ch.link(v.scalar_tensor_tensor(y, sq, 1.5, y, ALU.add, ALU.mult))

            def scales(t0, t1):
                ch.wait()
                for i in range(t0, t1):
                    ch.step(v.bn_aggr(mv[:, i, :], stats[:, i, :]))
                ch.wait()
                inv_sqrt(rstd, mv[:, t0:t1, 1], LN_EPS, t0, t1)
                v.scalar_tensor_tensor(shift[:, t0:t1], mv[:, t0:t1, 0], -1.0, rstd[:, t0:t1], ALU.mult, ALU.mult)\
                 .then_inc(S("scaled"), 1)

            def add_normed(stage, src, last=False):
                for i in range(NT):
                    dve.wait_ge(S("normed"), NORMED[stage] + i + 1)
                    ins = v.tensor_tensor(xres[:, i, :], xres[:, i, :], src[:, i, :], ALU.add)
                    if last:
                        ins.then_inc(S("final"), 1)
                        continue
                    ch.step(ins)
                    if i >= 1:
                        ch.wait(back=1 if i == 1 else 2)
                        ch.step(v.bn_stats(stats[:, i - 1, :], xres[:, i - 1, :]))
                if not last:
                    ch.wait(back=1)
                    ch.step(v.bn_stats(stats[:, NT - 1, :], xres[:, NT - 1, :]))
                    scales(0, NT)

            halves = (list(range(0, TPC)), list(range(TPC, NT)))
            for L in range(2):
                for n in range(NC if L == 0 else 0):
                    dve.wait_ge(S(f"x_in{n}"), 16)
                    for i in halves[n]:
                        ch.step(v.bn_stats(stats[:, i, :], xres[:, i, :]))
                    scales(TPC * n, TPC * (n + 1))
                for m in range(KD):
                    for j in range(2 if L == 1 else 0):
                        n = 2 * m + j
                        q = qkf[:, j, m, :]
                        dve.wait_ge(S(f"qk_sb{L}"), (n + 1) * NC)
                        if n == 0:
                            dve.wait_ge(S("rope"), 32)
                        swap = [x ^ 1 for x in range(32)]
                        ch.link(v.stream_shuffle(swapped[:, j, :], q, swap))
                        ch.link(v.tensor_tensor(swapped[:, j, :], swapped[:, j, :], sin_t[:, :], ALU.mult))
                        dve.wait_ge(S("by_cos"), n + 1)
                        v.tensor_tensor(q, by_cos[:, j, :], swapped[:, j, :], ALU.add).then_inc(S("roped"), 1)
                    for part in (1, 2):
                        for j in range(2):
                            if (m, j) in DVE_PARTS:
                                take_part(dve, L, m, j, part)

                for x in UNITS:
                    n = UNIT_NO[x]
                    if x[0] == "rows":
                        continue
                    dve.wait_ge(S(f"unit{L}"), n + 1)
                    if x[0] == "max":
                        _, g, u = x
                        part, i, h0, nh, _, w = MAX_UNITS[u]
                        v.tensor_reduce(mx[:, part, i, h0:h0 + nh],
                                        ps[:, n % RB, 0:nh * w].rearrange("p (h w) -> p h w", h=nh), AX.X, ALU.max)\
                         .then_inc(S(f"unit_out{L}"), 1)
                        if u == NMAX - 1:
                            dve.wait_ge(S(f"unit_out{L}"), EMPTIED[n])
                            ch.link(v.tensor_tensor(mx[:, 1, TPC:NT, :], mx[:, 1, TPC:NT, :], mx[:, 0, TPC:NT, :],
                                                    ALU.max))
                            ch.link(v.tensor_scalar(nb[:, :, 0, :], mx[:, 1, :, :], -1.0, None, ALU.mult))
                            v.scalar_tensor_tensor(nb[:, :, 1, :], mx[:, 1, :, :], -1.0, nb[:, :, 0, :],
                                                   ALU.mult, ALU.subtract).then_inc(S(f"neg_max{L}"), 1)
                    else:
                        g, c = divmod(x[1], NC)
                        t = ps[:, n % RB, :].rearrange("p (i h d) -> p i h d", i=TPC, h=HG)
                        ch.link(v.reciprocal(rden[:, c, :, :], t[:, :, :, DH]))
                        v.tensor_tensor(
                            y[:, TPC * c:TPC * (c + 1), HG * DH * g:HG * DH * (g + 1)].rearrange(
                                "p i (h d) -> p i h d", h=HG),
                            t[:, :, :, 0:DH],
                            rden[:, c, :, :].rearrange("p i (h o) -> p i h o", o=1).broadcast_to([P, TPC, HG, DH]),
                            ALU.mult).then_inc(S(f"unit_out{L}"), 1)

                for i in range(NT):
                    dve.wait_ge(S(f"attn_proj{L}"), i // 2 * 2 + 2)
                    ch.step(v.bn_stats(stats[:, i, :], ps[:, 4 + i // 2, i % 2 * D:(i % 2 + 1) * D]))
                scales(0, NT)
                add_normed(f"output{L}", hb)
                if L == 1:
                    dve.wait_ge(S("scaled"), SCALED["experts1"])
                    ch.link(v.tensor_tensor(msq[:, :], rstd[:, :], rstd[:, :], ALU.mult))
                    ch.link(v.tensor_tensor(msq[:, :], msq[:, :], mv[:, :, 1], ALU.mult))
                    inv_sqrt(msq, msq[:, :], RMS_EPS, 0, NT)
                    for i in range(NT):
                        dve.wait_ge(S("normed"), NORMED["experts1"] + i + 1)
                        v.scalar_tensor_tensor(xn[:, i, 0:D], hb[:, i, :], msq[:, i:i + 1], w_nm[:, :],
                                               ALU.mult, ALU.mult).then_inc(S("xn_f1"), 1)

                if L == 0:
                    dve.wait_ge(S("bias_o"), 48)
                dve.wait_ge(S(f"logits_ps{L}"), 1)
                lps = ps[:, 4, 0:NT * NR[L]].rearrange("p (t e) -> p t e", t=NT)
                if L == 0:
                    ins = v.tensor_tensor(lg[:, :, 0:E], lps,
                                          b_rt[:, :].rearrange("p (o e) -> p o e", o=1).broadcast_to([P, NT, E]), ALU.add)
                else:
                    ins = v.tensor_copy(lg[:, :, :], lps)
                ins.then_inc(S(f"logits_sb{L}"), 1)
                dve.wait_ge(S(f"logits_sb{L}"), 1)
                for i in range(NT):
                    ch.step(v.max(top[:, i, :], lg[:, i, 0:E]))
                ch.wait()
                for i in range(NT):
                    ch.step(v.max_index(tix[:, i, :], top[:, i, :], lg[:, i, 0:E]))
                ch.wait()
                ch.link(v.tensor_copy(tixf[:, :, :], tix[:, :, 0:K]))
                ch.link(v.tensor_tensor(
                    onehot, iota_e[:, :].rearrange("p (a b e) -> p a b e", a=1, b=1).broadcast_to([P, NT, K, E]),
                    tixf[:, :, :].rearrange("p t (k o) -> p t k o", o=1).broadcast_to([P, NT, K, E]), ALU.is_equal))
                with nc.allow_low_precision(reason="zeros and ones"):
                    v.tensor_reduce(picked[:, :, :], onehot.rearrange("p t k e -> p t e k"), AX.X, ALU.add)\
                     .then_inc(S(f"picked{L}"), 1)
                ins = v.tensor_tensor(gate[:, :, :], top[:, :, 0:K], top[:, :, 0:1].broadcast_to([P, NT, K]), ALU.subtract)
                if L == 1:
                    ch.step(ins)
                    ins = v.tensor_tensor(gall[:, :, :], lg[:, :, 0:E], top[:, :, 0:1].broadcast_to([P, NT, E]),
                                          ALU.subtract)
                    ch.wait()
                ins.then_inc(S(f"less_top{L}"), 1)

                dve.wait_ge(S(f"ranks{L}"), 1)
                rank = ps[:, 5, 0:NT * E].rearrange("p (t e) -> p t e", t=NT)
                if L == 0:
                    ch.link(v.tensor_copy(cnt[:, :], ps[:, 5, NT * E:(NT + 1) * E]))
                    levels = big1[:, 0:E * NT].rearrange("p (e t) -> p e t", e=E)
                    ch.link(v.tensor_tensor(levels, cnt[:, :].rearrange("p (e o) -> p e o", o=1).broadcast_to([P, E, NT]),
                                            lev[:, :].rearrange("p (o t) -> p o t", o=1).broadcast_to([P, E, NT]),
                                            ALU.is_gt))
                    ch.link(v.tensor_reduce(ntile[:, :], levels, AX.X, ALU.add))
                    sq = big1.rearrange("p (e f) -> p e f", e=E)
                    ch.link(v.tensor_tensor(sq, lt_e[:, :, :],
                                            ntile[:, :].rearrange("p (o f) -> p o f", o=1).broadcast_to([P, E, E]),
                                            ALU.mult))
                    ch.link(v.tensor_reduce(tbeg[:, :], sq, AX.X, ALU.add))
                    ch.step(v.tensor_tensor(tend[:, :], tbeg[:, :], ntile[:, :], ALU.add))
                    ch.link(v.tensor_scalar(tbeg[:, :], tbeg[:, :], float(P), None, ALU.mult))
                    v.tensor_tensor(dest[:, :, :], rank,
                                    tbeg[:, :].rearrange("p (o e) -> p o e", o=1).broadcast_to([P, NT, E]), ALU.add)\
                     .then_inc(S(f"dest_done{L}"), 1)
                else:
                    ch.step(v.tensor_scalar(dest[:, :, :], rank, CAP - 0.5, SKIP, ALU.is_gt, ALU.mult))
                    ch.link(v.tensor_scalar(tbeg[:, :], iota_e[:, :], float(CAP), None, ALU.mult))
                    ch.link(v.tensor_tensor(dest[:, :, :], dest[:, :, :], rank, ALU.add))
                    v.tensor_tensor(dest[:, :, :], dest[:, :, :],
                                    tbeg[:, :].rearrange("p (o e) -> p o e", o=1).broadcast_to([P, NT, E]), ALU.add)\
                     .then_inc(S(f"dest_done{L}"), 1)
                dve.wait_ge(S(f"dest_done{L}"), 1)
                ch.link(v.tensor_tensor(prod, onehot, dest[:, :, :].rearrange("p t (o e) -> p t o e", o=1)
                                        .broadcast_to([P, NT, K, E]), ALU.mult))
                ch.link(v.tensor_reduce(slot[:, :, :], prod, AX.X, ALU.add))
                ch.step(v.tensor_copy(slot_i[:, :], slot[:, :, :].rearrange("p t k -> p (t k)")))
                ch.step(v.tensor_copy(xn[:, :, SLOTS_AT:GATES_AT], slot[:, :, :]))
                ch.step(v.tensor_copy(own[:, :], own_first[:, :]))
                dve.wait_ge(S(f"gate_exp{L}"), 1 + L)
                ch.link(v.tensor_reduce(gsum[:, :], gate[:, :, :] if L == 0 else gall[:, :, :], AX.X, ALU.add))
                ch.link(v.reciprocal(gsum[:, :], gsum[:, :]))
                if L == 0:
                    ch.link(v.tensor_scalar(gsum[:, :], gsum[:, :], 1.8, None, ALU.mult))
                v.tensor_tensor(xn[:, :, GATES_AT:TOKEN_AT], gate[:, :, :],
                                gsum[:, :].rearrange("p (t o) -> p t o", o=1).broadcast_to([P, NT, K]), ALU.mult)\
                 .then_inc(S(f"slot_no{L}"), 1)
                if L == 1:
                    dve.wait_ge(S("sgate"), 1)
                    ch.link(v.tensor_scalar(sgate[:, :], sgate[:, :], 1.0, 0.5, ALU.add, ALU.mult))
                if L == 0:
                    m3 = tmap.rearrange("p (i e) -> p i e", i=TILES[0])
                    ch.link(v.tensor_tensor(
                        m3, iota_t[:, :].rearrange("p (i o) -> p i o", o=1).broadcast_to([1, TILES[0], E]),
                        tend[0:1, :].rearrange("p (o e) -> p o e", o=1).broadcast_to([1, TILES[0], E]), ALU.is_ge))
                    ch.link(v.tensor_reduce(texp, m3, AX.X, ALU.add))
                    v.tensor_scalar(texp_i[:, :], texp, float(E - 1), None, ALU.min).then_inc(S("tile_expert"), 1)

                srest, erest = SHARED[L] - SFULL[L] * P, INTER[L] - P
                nsc = SFULL[L] + 1
                actv = acts[:, 0:nsc * T].rearrange("p (c t) -> p c t", c=nsc)
                for u in range(nsc * NC):
                    n, j = divmod(u, nsc)
                    dve.wait_ge(S(f"s_silu{L}"), u + 1)
                    if j < SFULL[L]:
                        ins = v.tensor_tensor(actv[:, j, n * CH:(n + 1) * CH], ps[:, 2 * (u % 2) + 1, :],
                                              ssilu[:, u % 2, :], ALU.mult)
                    else:
                        up = slice(HALF, HALF + srest)
                        ins = v.tensor_tensor(actv[0:srest, j, n * CH:(n + 1) * CH], ps[up, 2 * (u % 2), :],
                                              ssilu[up, u % 2, :], ALU.mult)
                    ins.then_inc(S(f"s_act{L}"), 1)
                if L == 1:
                    for i in range(NT):
                        dve.wait_ge(S("sh_down1"), i + 1)
                        v.scalar_tensor_tensor(shout[:, i, :], ps[:, 6 + i % 2, 0:D], sgate[:, i:i + 1], hb[:, i, :],
                                               ALU.mult, ALU.add).then_inc(S("sh_sb1"), 1)

                def e_pick(blk, r, first):
                    i = blk * RING + r
                    dve.wait_ge(S(f"rows_{r}"), 16 * (R0[L] + blk + 1))
                    if not (first and L == 0):
                        dve.wait_ge(S(f"added_{r % 2}"), 16 * (E0[L] // 2 + 2 * blk + r // 2 - 1))
                        dve.wait_ge(S("e_seen"), E0[L] + i - RING + 1)
                    v.scalar_tensor_tensor(mine[:, r, :], rows[:, r, SLOTS_AT:GATES_AT], own[:, r:r + 1],
                                           rows[:, r, GATES_AT:TOKEN_AT], ALU.is_equal, ALU.mult).then_inc(S("e_pick"), 1)
                    v.tensor_copy(token[:, r:r + 1], rows[:, r, TOKEN_AT:W].bitcast(I32)).then_inc(S("e_pick"), 1)

                def e_gate(blk, r):
                    i = blk * RING + r
                    dve.wait_ge(S("e_pick"), 2 * (E0[L] + i) + 2)
                    v.tensor_reduce(egate[:, r:r + 1], mine[:, r, :], AX.X, ALU.add).then_inc(S("e_gate"), 1)

                def e_mult(blk, r, first):
                    i = blk * RING + r
                    dve.wait_ge(S("e_silu"), 2 * (E0[L] + i) + 2)
                    if not (first and r < 2):
                        dve.wait_ge(S("e_down"), E0[L] + i - 1)
                    v.tensor_tensor(eact[:, r % 2, 0:P], ps[:, 2 + r % 2, P:2 * P], esilu[:, r % 2, 0:P], ALU.mult)\
                     .then_inc(S("e_act"), 1)
                    up = slice(HALF, HALF + erest)
                    v.tensor_tensor(eact[0:erest, r % 2, P:2 * P], ps[up, 2 + r % 2, 2 * P:3 * P],
                                    esilu[up, r % 2, P:2 * P], ALU.mult).then_inc(S("e_act"), 1)

                def e_out(blk, r, first):
                    i = blk * RING + r
                    dve.wait_ge(S("e_down"), E0[L] + i + 1)
                    dve.wait_ge(S("e_gate"), E0[L] + i + 1)
                    if not (first and r < 2 and L == 0):
                        dve.wait_ge(S(f"added_{r % 2}"), 16 * (E0[L] // 2 + 2 * blk + r // 2))
                    v.tensor_scalar(erows[:, r % 2, :], ps[:, 4 + r % 2, 0:D], egate[:, r:r + 1], None, ALU.mult)\
                     .then_inc(S("e_sb"), 1)

                def e_block(blk, first, last):
                    for r in range(RING):
                        e_pick(blk, r, first)
                        e_mult(blk, r, first)
                        e_gate(blk, r)
                        if not (first and r == 0):
                            e_out(blk + (-1 if r == 0 else 0), (r - 1) % RING, first)
                    if not last:
                        v.tensor_scalar(own[:, :], own[:, :], float(RING * P), None, ALU.add).then_inc(S("own"), 1)
                        dve.wait_ge(S("own"), L * (TILES[0] // RING - 1) + blk + 1)

                last = TILES[L] // RING - 1
                e_block(0, True, False)
                with dve.Fori(1, last) as blk:
                    e_block(blk, False, False)
                e_block(last, False, True)
                e_out(last, RING - 1, False)

                for n, tiles in enumerate(halves):
                    dve.wait_ge(S(f"sums_in{L}_{n}"), 32)
                    t0, t1 = tiles[0], tiles[-1] + 1
                    v.tensor_tensor(shout[:, t0:t1, :], shout[:, t0:t1, :], sum_odd[:, t0:t1, :], ALU.add)\
                     .then_inc(S(f"summed{L}"), 1)
                    dve.wait_ge(S(f"summed{L}"), n + 1)
                    for i in tiles:
                        ch.step(v.bn_stats(stats[:, i, :], shout[:, i, :]))
                scales(0, NT)
                add_normed(f"sum{L}", shout, last=(L == 1))


def kernel(**inputs):
    import concourse.bacc as bacc
    from concourse.bass_utils import run_bass_kernel_spmd

    g = {k: np.asarray(v) for k, v in inputs.items()}
    d = {}
    d["x"] = g["L0_attn_x"].reshape(T, D)
    d["qkv0"] = np.stack([g[f"L0_attn_{n}"].transpose(1, 0, 2).reshape(D, D) for n in ("Wq", "Wk", "Wv")])
    d["qkv1"] = np.stack([g[f"L1_attn_{n}"].T for n in ("wq", "wk", "wv")])
    d["wo0"] = g["L0_attn_Wo"]
    d["wo1"] = g["L1_attn_wo"].T
    d["bqk"] = np.stack([g[f"L0_attn_{n}"].reshape(KD, P) for n in ("bq", "bk")]).transpose(2, 0, 1)
    d["bv"] = g["L0_attn_bv"].reshape(D)
    d["bo"] = g["L0_attn_bo"]
    d["router_b"] = g["L0_ffn_router_b"]
    d["w_norm"] = g["L1_ffn_w_norm"]
    d["router0"] = g["L0_ffn_router_w"].T
    d["router1"] = np.concatenate([g["L1_ffn_w_router"], g["L1_ffn_w_shared_gate"]], axis=1)

    def up(gate, upw):
        n = gate.shape[-1] // P * P
        fill = [(0, 0)] * (gate.ndim - 1) + [(0, HALF - (gate.shape[-1] - n))]
        both = np.concatenate([gate[..., :n], upw[..., :n], np.pad(gate[..., n:], fill), np.pad(upw[..., n:], fill)],
                              axis=-1)
        return np.swapaxes(both.reshape(both.shape[:-2] + (KD, P, both.shape[-1])), -3, -2)

    def expert(gate, upw, down):
        return np.concatenate([up(gate, upw).reshape(E, P, -1), down[:, :P]], axis=-1)

    down0 = g["L0_ffn_down_w"].transpose(0, 2, 1)
    d["ex0"] = expert(g["L0_ffn_gate_w"].transpose(0, 2, 1), g["L0_ffn_up_w"].transpose(0, 2, 1), down0)
    d["ex1"] = expert(g["L1_ffn_w_gate"], g["L1_ffn_w_up"], g["L1_ffn_w_down"])
    d["dn0"] = down0[:, P:]
    d["dn1"] = g["L1_ffn_w_down"][:, P:]
    d["sgu0"] = up(g["L0_ffn_shared_gate_w"].T, g["L0_ffn_shared_up_w"].T)
    d["sgu1"] = up(g["L1_ffn_sw_gate"], g["L1_ffn_sw_up"])
    d["sdn0"] = g["L0_ffn_shared_down_w"].T
    d["sdn1"] = g["L1_ffn_sw_down"]
    pos = np.arange(T, dtype=np.float32)[:, None]
    inv = (np.float32(10000.0) ** (-(np.arange(0, DH, 2, dtype=np.float32) / np.float32(DH)))).astype(np.float32)
    ang = np.repeat(pos * inv, 2, axis=1)
    sign = np.where(np.arange(DH) % 2 == 0, -1.0, 1.0).astype(np.float32)
    d["cos"] = np.tile(np.cos(ang).T, (P // DH, 1)).astype(np.float32)
    d["sin"] = np.tile((np.sin(ang) * sign).T, (P // DH, 1)).astype(np.float32)

    nc = bacc.Bacc("TRN2", target_bir_lowering=False, num_devices=1)
    arrays, args = {}, {}
    for name, x in d.items():
        x = np.ascontiguousarray(x)
        arrays[f"in_{name}"] = x
        args[name] = nc.dram_tensor(f"in_{name}", x.shape, mybir.dt.from_np(x.dtype), kind="ExternalInput").ap()
    out = nc.dram_tensor("out_x", (T, D), F32, kind="ExternalOutput").ap()
    build(nc, args, out)
    r = run_bass_kernel_spmd(nc, [arrays], core_ids=[0])
    return r.results[0]["out_x"].reshape(1, T, D)
```

```python
import numpy as np

import concourse.bass as bass
from concourse import mybir
from contextlib import ExitStack

F32 = mybir.dt.float32
BF16 = mybir.dt.bfloat16
I32 = mybir.dt.int32
U32 = mybir.dt.uint32
ALU = mybir.AluOpType
ACT = mybir.ActivationFunctionType
AX = mybir.AxisListType

P = 128
T = 1024
NT = T // P
D = 256
KD = D // P
H = 16
DH = D // H
HG = 4
NG = H // HG
CH = 512
NC = T // CH
TPC = CH // P
E = 32
K = 4
SCALE = DH ** -0.5
LN_EPS = 1e-5
RMS_EPS = 1e-6
BIG = 1.0e30
SKIP = float(1 << 20)
CAP = 128
PARTS = 3
Q_PARTS = (0, 0, 0, 1, 1, 1, 2)
K_PARTS = (0, 1, 2, 0, 1, 2, 0)
HM = H // KD
NPROD = 7
KQ = NPROD * DH
NSH = 2
KX = KQ + NSH
ONES_AT = KQ // 32 * 32

INTER = (192, 176)
SHARED = (192, 704)
HALF = P // 2
FULL = 1
SFULL = tuple(w // P for w in SHARED)
UPC = 2 * FULL + 1
EW = KD * UPC * P + D
TILES = (64, 32)
E0 = (0, TILES[0])
R0 = (0, TILES[0] // 4)
NR = (E, E + 1)
SLOT_TILES = ((0, 2), (2, NT))
RING = 4
SLOTS_AT = D
GATES_AT = D + K
TOKEN_AT = D + 2 * K
W = TOKEN_AT + 1


def exp_steps():
    out = [(0, b) for b in range(TPC)]
    for b in range(TPC):
        out += [(1, b), (1, TPC + b)]
    return out


STEPS = exp_steps()
NSTEP = len(STEPS)


def max_units():
    units = []
    for i in range(NT):
        if i >= TPC:
            units += [(0, i, hh, 1, 0, CH) for hh in range(HG)]
        w = (i % TPC + 1) * P
        n = {1: 4, 2: 2, 3: 1, 4: 1}[w // P]
        units += [(1, i, hh, n, (i // TPC) * CH, w) for hh in range(0, HG, n)]
    return units


MAX_UNITS = max_units()
NMAX = len(MAX_UNITS)
CHUNK_UNITS = [sum(u[1] < TPC * (c + 1) for u in MAX_UNITS) for c in range(NC)]
RB = 3
PB = 3


OWN_RATE, NEXT_RATE = 4, (5, 4, 4, 4)
OWN_AHEAD, NEXT_AHEAD = 10, 10
ROWS_AT = (6, NSTEP - 2)


def schedule():
    rest = [("max", 0, u) for u in range(CHUNK_UNITS[0], NMAX)] + [("rows", 0, 1)]
    out = [("max", 0, u) for u in range(CHUNK_UNITS[0])] + [("rows", 0, 0)] + rest[:OWN_AHEAD]
    rest = rest[OWN_AHEAD:]
    last = NG * NSTEP
    for st in range(last + 2):
        g, s = divmod(st, NSTEP)
        if s == 0 and g + 1 < NG:
            nxt = [("max", g + 1, u) for u in range(NMAX)]
        more = []
        if g == 0 and s < TPC:
            more = rest[:OWN_RATE]
            rest = rest[OWN_RATE:]
            if s == TPC - 1:
                more += rest + nxt[:NEXT_AHEAD]
                nxt = nxt[NEXT_AHEAD:]
        elif g + 1 < NG:
            more = nxt[:NEXT_RATE[g]]
            nxt = nxt[len(more):]
        if g + 1 < NG:
            for c in range(NC):
                if s == ROWS_AT[c]:
                    more.append(("rows", g + 1, c))
        if s == TPC + 3 and g < NG:
            more.append(("turn", NC * g))
        if s == 3 and 0 < g < NG:
            more.append(("turn", NC * g - 1))
        for p in range(2):
            if st < last:
                out.append(("score", st, p))
            out += more[:1]
            more = more[1:]
        if st >= 2:
            out.append(("weigh", st - 2))
        out += more
    return out + [("turn", NC * NG - 1)]


SCHEDULE = schedule()
UNITS = [x for x in SCHEDULE if x[0] in ("max", "rows", "turn")]
UNIT_NO = {x: n for n, x in enumerate(UNITS)}
EMPTIED = [sum(y[0] != "rows" for y in UNITS[:n + 1]) for n in range(len(UNITS))]
ROWS_DONE = [sum(y[0] == "rows" for y in UNITS[:n + 1]) for n in range(len(UNITS))]
DIAGONAL = [b >= TPC * c for c, b in STEPS]


def masked_steps(st):
    g, s = divmod(st, NSTEP)
    return g * sum(DIAGONAL) + sum(DIAGONAL[:s + 1])


NORMS = (("attention0a", TPC), ("attention0b", TPC), ("output0", NT), ("experts0", TPC), ("sum0", NT),
         ("attention1", TPC), ("output1", NT), ("experts1", NT), ("sum1", NT))
SCALED = {name: n + 1 for n, (name, _) in enumerate(NORMS)}
NORMED = {name: sum(t for _, t in NORMS[:n]) for n, (name, _) in enumerate(NORMS)}


DVE_PARTS = ((0, 0), (0, 1))
POOL_PARTS = ((1, 0), (1, 1))

TURNS = tuple(f"{x}{L}" for L in range(2) for x in ("a", "y", "f"))


def turned(tag):
    return KD * TURNS.index(tag)


class Chain:

    def __init__(self, eng, sem):
        self.eng, self.sem, self.n = eng, sem, 0

    def step(self, ins):
        self.n += 1
        ins.then_inc(self.sem, 1)

    def wait(self, back=0):
        self.eng.wait_ge(self.sem, self.n - back)

    def link(self, ins):
        self.step(ins)
        self.wait()


def build(nc, a, out):
    ctx = ExitStack()
    with ctx:
        sems = {}

        def S(name):
            if name not in sems:
                sems[name] = ctx.enter_context(nc.semaphore(name))
            return sems[name]

        def left(L, m, j, part):
            who, those = ("pool", POOL_PARTS) if (m, j) in POOL_PARTS else ("dve", DVE_PARTS)
            return S(f"left{part}_{who}"), len(those) * L + those.index((m, j)) + 1

        def max_rows(eng, L, g, c):
            for j in range(NSH):
                eng.dma_start(QA[KQ + j:KQ + j + 1, HG * g:HG * (g + 1), c * CH:(c + 1) * CH],
                              mT[HG * j:HG * (j + 1), c * CH:(c + 1) * CH]).then_inc(S(f"max_rows{L}_{c}"), 16)

        def take_part(eng, L, m, j, part):
            eng.wait_ge(S(f"parts_p{part}_{L}"), 2 * m + j + 1)
            q = qkf[:, j, m, :]
            eng.tensor_tensor(q if part == 1 else parts[:, j, m, 2, :], q, parts[:, j, m, part - 1, :], ALU.subtract)\
               .then_inc(left(L, m, j, part)[0], 1)

        def sb(name, shape, dt=F32):
            return ctx.enter_context(nc.sbuf_tensor(name, shape, dt))

        slot_rows = [nc.dram_tensor(f"slot_rows{L}", (TILES[L] * P, W), F32).ap() for L in range(2)]
        acc = [[nc.dram_tensor(f"acc{L}_{x}", (T + P, D), F32).ap() for x in range(2)] for L in range(2)]

        xres = sb("xres", [P, NT, D])
        xn = sb("xn", [P, NT, W])
        xT = sb("xT", [P, KD, T])
        hb = sb("hb", [P, NT, D])
        identf = sb("identf", [P, P])
        identb = sb("identb", [P, P], BF16)
        mask_q = sb("mask_q", [P, P], BF16)
        before = sb("before", [P, P], BF16)
        ones = sb("ones", [P, P], BF16)
        stats = sb("stats", [P, NT, 6])
        mv = sb("mv", [P, NT, 2])
        rstd = sb("rstd", [P, NT])
        shift = sb("shift", [P, NT])
        ones_row = sb("ones_row", [1, P])
        msq = sb("msq", [P, NT])
        rs_half = sb("rs_half", [P, NT])
        rs_sq = sb("rs_sq", [P, NT])
        rs_big = sb("rs_big", [P, NT])
        w_qkv = sb("w_qkv", [P, 3, KD, D])
        w_o = sb("w_o", [P, KD, D])
        bias_qk = sb("bias_qk", [P, 2, KD])
        bias_v = sb("bias_v", [P, D])
        bias_o = sb("bias_o", [P, D])
        cos_t = sb("cos_t", [P, T])
        sin_t = sb("sin_t", [P, T])
        V = sb("V", [P, NT, H, 32])
        w_sgu = sb("w_sgu", [P, KD, 2 * SHARED[1]])
        w_sdn = sb("w_sdn", [P, SFULL[1] + 1, D])
        w_rt = sb("w_rt", [P, KD, E + 1])
        b_rt = sb("b_rt", [P, E])
        w_nm = sb("w_nm", [P, D])
        QA = sb("QA", [P, H, T], BF16)
        KA = sb("KA", [P, H, T], BF16)
        X = sb("X", [P, 10240])
        qkf = X[:, 0:4096].rearrange("p (a m t) -> p a m t", a=2, m=KD)
        parts = X[:, 4096:10240].bitcast(BF16).rearrange("p (a m r t) -> p a m r t", a=2, m=KD, r=PARTS)
        probs = X[:, 0:PB * 2048].rearrange("p (n h t) -> p n h t", n=PB, h=HG)
        pv_sb = X[:, PB * 2048:PB * 2048 + 1024].rearrange("p (n t) -> p n t", n=2)
        y = X[:, PB * 2048 + 1024:PB * 2048 + 3072].rearrange("p (t n) -> p t n", t=NT)
        swapped = V[:, :, :, :].rearrange("p a b c -> p (a b c)")[:, 0:2 * T].rearrange("p (a t) -> p a t", a=2)
        by_cos = V[:, :, :, :].rearrange("p a b c -> p (a b c)")[:, 2 * T:4 * T].rearrange("p (a t) -> p a t", a=2)
        rden = sb("rden", [P, 2, TPC, HG])
        mx = sb("mx", [P, 2, NT, HG])
        nb = sb("nb", [P, NT, NSH, HG], BF16)
        mT = sb("mT", [NSH * HG, T], BF16)
        acts = QA[:, :, :].rearrange("p h t -> p (h t)").bitcast(F32)
        KAf = KA[:, :, :].rearrange("p h t -> p (h t)").bitcast(F32)
        rows = X[:, 0:RING * W].rearrange("p (r n) -> p r n", r=RING)
        rowsT = X[:, 1088:1600].rearrange("p (r k n) -> p r k n", r=2, k=KD)
        eact = X[:, 1600:2112].rearrange("p (r n) -> p r n", r=2)
        esilu = X[:, 2112:2624].rearrange("p (r n) -> p r n", r=2)
        erows = X[:, 2624:3136].rearrange("p (r n) -> p r n", r=2)
        ssilu = X[:, 3072:4096].rearrange("p (r n) -> p r n", r=2)
        shout = X[:, 4096:6144].rearrange("p (t n) -> p t n", t=NT)
        sum_odd = X[:, 6144:8192].rearrange("p (t n) -> p t n", t=NT)
        onehot = X[:, 8192:9216].rearrange("p (t k e) -> p t k e", t=NT, k=K)
        prod = X[:, 9216:10240].rearrange("p (t k e) -> p t k e", t=NT, k=K)
        w_ex = KAf[:, 0:RING * EW].rearrange("p (r n) -> p r n", r=RING)
        w_rest = KAf[:, RING * EW:RING * (EW + D)].rearrange("p (r n) -> p r n", r=RING)
        empty = sb("empty", [P, W])
        own_first = sb("own_first", [P, RING])
        pause = sb("pause", [P, RING])
        own = sb("own", [P, RING])
        mine = sb("mine", [P, RING, K])
        egate = sb("egate", [P, RING])
        token = sb("token", [P, RING], I32)
        iota_e = sb("iota_e", [P, E])
        iota_t = sb("iota_t", [1, TILES[0]])
        upto = sb("upto", [E, 2, E], BF16)
        upto_n = sb("upto_n", [E, 2 * E], BF16)
        lev = sb("lev", [P, NT])
        lg = sb("lg", [P, NT, E + 1])
        top = sb("top", [P, NT, 8])
        tix = sb("tix", [P, NT, 8], U32)
        tixf = sb("tixf", [P, NT, K])
        picked = sb("picked", [P, NT, E], BF16)
        gate = sb("gate", [P, NT, K])
        gall = sb("gall", [P, NT, E])
        gsum = sb("gsum", [P, NT])
        sgate = sb("sgate", [P, NT])
        cnt = sb("cnt", [E, 1])
        levels = sb("levels", [E, NT])
        ntile = sb("ntile", [E, 1])
        tbeg = sb("tbeg", [P, E])
        tend = sb("tend", [1, E])
        dest = sb("dest", [P, NT, E])
        slot = sb("slot", [P, NT, K])
        slot_i = sb("slot_i", [P, NT * K], I32)
        texp = X[0:1, 0:TILES[0]]
        texp_i = sb("texp_i", [1, TILES[0]], I32)
        tmap = X[0:1, 1024:1024 + TILES[0] * E]

        ps = ctx.enter_context(nc.psum_tensor("ps", [P, 8, CH], F32))

        block = ctx.enter_context(nc.Block())

        @block.sync
        def _(sp):
            xt = a["x"].rearrange("(t p) d -> p t d", p=P)
            for n in range(NC):
                sp.dma_start(xres[:, n * TPC:(n + 1) * TPC, :], xt[:, n * TPC:(n + 1) * TPC, :])\
                  .then_inc(S(f"x_in{n}"), 16)

            def attention_weights(L):
                sp.dma_start(w_qkv[:, :, :, :], a[f"qkv{L}"].rearrange("a (k p) n -> p a k n", p=P))\
                  .then_inc(S(f"w_qkv{L}"), 16)

            def output_weights(L):
                sp.dma_start(w_o[:, :, :], a[f"wo{L}"].rearrange("(k p) n -> p k n", p=P)).then_inc(S(f"w_o{L}"), 16)

            def row_of(dst, name, sem):
                n = dst.shape[1]
                sp.dma_start(dst[:, :], a[name].rearrange("(o n) -> o n", o=1).broadcast_to([P, n])).then_inc(sem, 16)

            def expert_constants(L):
                n, f = (2 * SFULL[L] + 1) * P, SFULL[L]
                sp.dma_start(w_rt[:, :, 0:NR[L]], a[f"router{L}"].rearrange("(k p) n -> p k n", p=P))\
                  .then_inc(S(f"w_router{L}"), 16)
                sp.dma_start(w_sgu[:, :, 0:n], a[f"sgu{L}"]).then_inc(S(f"w_shared{L}"), 16)
                sp.dma_start(w_sdn[:, 0:f, :], a[f"sdn{L}"][0:f * P, :].rearrange("(c p) n -> p c n", p=P))\
                  .then_inc(S(f"w_shared{L}"), 16)
                sp.dma_start(w_sdn[0:SHARED[L] - f * P, f, :], a[f"sdn{L}"][f * P:SHARED[L], :])\
                  .then_inc(S(f"w_shared{L}"), 16)

            def empty_slots(L, i):
                sp.dma_start(slot_rows[L][i * P:(i + 8) * P, :].rearrange("(t p) d -> p t d", p=P),
                             empty[:, :].rearrange("p (o d) -> p o d", o=1).broadcast_to([P, 8, W]))\
                  .then_inc(S(f"slots_empty{L}"), 16)

            def zero_sums(L):
                sp.dma_start(acc[L][0][T:T + P, :], empty[:, 0:D]).then_inc(S(f"acc_start{L}"), 16)
                sp.dma_start(acc[L][1].rearrange("(t p) d -> p t d", p=P),
                             empty[:, 0:D].rearrange("p (o d) -> p o d", o=1).broadcast_to([P, NT + 1, D]))\
                  .then_inc(S(f"acc_start{L}"), 16)

            attention_weights(0)
            sp.dma_start(bias_qk[:, :, :], a["bqk"]).then_inc(S("bias_qkv"), 16)
            row_of(bias_v, "bv", S("bias_qkv"))

            for L in range(2):
                if L == 1:
                    sp.wait_ge(S("attn_proj0"), NT)
                    attention_weights(1)
                sp.wait_ge(S(f"k_ones{L}"), 1)
                for m in range(KD):
                    for part in range(PARTS):
                        for j, (dst, those) in enumerate(((QA, Q_PARTS), (KA, K_PARTS))):
                            if part < 2:
                                sp.wait_ge(S(f"parts_p{part + 1}_{L}"), 2 * m + j + 1)
                            else:
                                sp.wait_ge(*left(L, m, j, 2))
                            for r in range(NPROD):
                                if those[r] == part:
                                    sp.dma_start(dst[DH * r:DH * (r + 1), HM * m:HM * (m + 1), :],
                                                 parts[:, j, m, part, :]).then_inc(S(f"qa_rows{L}_{m}"), 16)
                for g in range(NG):
                    for c in range(NC if g else 0):
                        sp.wait_ge(S(f"maxT{L}"), NC * g + c + 1)
                        max_rows(sp, L, g, c)
                        if g == 1 and c == 0:
                            output_weights(L)
                            if L == 0:
                                row_of(bias_o, "bo", S("bias_o"))
                                row_of(b_rt, "router_b", S("bias_o"))
                                row_of(w_nm, "w_norm", S("bias_o"))
                                sp.dma_start(cos_t[:, :], a["cos"]).then_inc(S("rope"), 16)
                                sp.dma_start(sin_t[:, :], a["sin"]).then_inc(S("rope"), 16)
                                expert_constants(0)
                                sp.wait_ge(S("empty"), 1)
                    if L == 0 and g >= 1:
                        for i in range(g - 1, sum(TILES) // 8, NG - 1):
                            empty_slots(*((0, 8 * i) if 8 * i < TILES[0] else (1, 8 * i - TILES[0])))
                if L == 0:
                    zero_sums(0)
                    zero_sums(1)

                rest = INTER[L] - P

                def weights_in(r, e):
                    sp.dma_start(w_ex[:, r, :], a[f"ex{L}"][bass.ds(e, 1)].rearrange("o p n -> (o p) n"))\
                      .then_inc(S(f"w_ex_{r}"), 16)
                    sp.dma_start(w_rest[0:rest, r, :], a[f"dn{L}"][bass.ds(e, 1)].rearrange("o p n -> (o p) n"))\
                      .then_inc(S(f"w_rest_{r}"), 16)

                def expert_of(i):
                    return i if L == 1 else sp.value_load(texp_i[0:1, bass.ds(i, 1)], min_val=0, max_val=E - 1)

                sp.wait_ge(S(f"attn_proj{L}"), NT)
                if L == 0:
                    sp.wait_ge(S("tile_expert"), 1)
                for r in range(RING):
                    weights_in(r, expert_of(r))
                sp.wait_ge(S(f"sh_sb{L}"), NT)
                sp.dma_start(acc[L][0][0:T, :].rearrange("(t p) d -> p t d", p=P), shout).then_inc(S(f"acc_start{L}"), 16)
                with sp.Fori(RING, TILES[L] - RING + 1, RING) as i0:
                    for r in range(RING):
                        e = expert_of(i0 + r)
                        sp.wait_ge(S("e_down"), E0[L] + i0 + (r - RING + 1))
                        weights_in(r, e)
                for x, dst in enumerate((shout, sum_odd)):
                    sp.wait_ge(S(f"added_{x}"), 16 * (E0[L] + TILES[L]) // 2)
                    for n in range(NC):
                        sp.dma_start(dst[:, n * TPC:(n + 1) * TPC, :],
                                     acc[L][x][n * CH:(n + 1) * CH, :].rearrange("(t p) d -> p t d", p=P))\
                          .then_inc(S(f"sums_in{L}_{n}"), 16)
                if L == 0:
                    expert_constants(1)
            for n in range(NC):
                sp.wait_ge(S("final"), TPC * (n + 1))
                sp.dma_start(out.rearrange("(t p) d -> p t d", p=P)[:, n * TPC:(n + 1) * TPC, :],
                             xres[:, n * TPC:(n + 1) * TPC, :]).then_inc(S("out"), 16)
            sp.wait_ge(S("out"), 16 * NC)

        @block.gpsimd
        def _(pool):
            ch = Chain(pool, S("pool_own"))
            ch.step(pool.memset(empty[:, 0:TOKEN_AT], 0.0))
            ch.step(pool.iota(empty[:, TOKEN_AT:W].bitcast(I32), pattern=[[0, 1]], base=T, channel_multiplier=1))
            for i in range(NT):
                ch.step(pool.iota(xn[:, i, TOKEN_AT:W].bitcast(I32), pattern=[[0, 1]], base=i * P, channel_multiplier=1))
            ch.step(pool.iota(own_first[:, :], pattern=[[P, RING]], base=0, channel_multiplier=1,
                              allow_small_or_imprecise_dtypes=True))
            for t in (identf, identb, mask_q):
                ch.step(pool.memset(t[:, :], 0.0))
            for t in (before, ones, ones_row):
                ch.step(pool.memset(t[:, :], 1.0))
            ch.step(pool.memset(upto[:, :, :], 1.0))
            ch.step(pool.iota(iota_e[:, :], pattern=[[1, E]], base=0, channel_multiplier=0,
                              allow_small_or_imprecise_dtypes=True))
            ch.step(pool.iota(iota_t[:, :], pattern=[[1, TILES[0]]], base=0, channel_multiplier=0,
                              allow_small_or_imprecise_dtypes=True))
            ch.step(pool.iota(lev[:, :], pattern=[[P, NT]], base=0, channel_multiplier=0,
                              allow_small_or_imprecise_dtypes=True))
            ch.wait()
            pool.memset(empty[:, 0:1], 0.0).then_inc(S("empty"), 1)
            for t in (identf, identb):
                ch.step(pool.affine_select(out=t[:, :], in_=t[:, :], compare_op=ALU.not_equal, fill=1.0,
                                           base=0, pattern=[[-1, P]], channel_multiplier=1))
            ch.step(pool.affine_select(out=mask_q[:, :], in_=mask_q[:, :], compare_op=ALU.is_ge, fill=-BIG,
                                       base=0, pattern=[[-1, P]], channel_multiplier=1))
            ch.step(pool.affine_select(out=before[:, :], in_=before[:, :], compare_op=ALU.is_ge, fill=0.0,
                                       base=-1, pattern=[[1, P]], channel_multiplier=-1))
            for x in range(2):
                ch.step(pool.affine_select(out=upto[:, x, :], in_=upto[:, x, :], compare_op=ALU.is_ge, fill=0.0,
                                           base=x - 1, pattern=[[1, E]], channel_multiplier=-1))
            ch.wait()
            pool.memset(empty[:, 0:1], 0.0).then_inc(S("consts"), 1)
            pool.wait_ge(S("consts"), 1)

            for L in range(2):
                if L == 1:
                    pool.wait_ge(S("e_down"), TILES[0])
                    pool.wait_ge(S("e_seen"), TILES[0])
                pool.memset(KA[ONES_AT:KX, :, :], 1.0).then_inc(S(f"k_ones{L}"), 1)
                pool.wait_ge(S(f"k_ones{L}"), 1)
                for m in range(KD):
                    if L == 1:
                        if m == 0:
                            pool.wait_ge(S("rope"), 32)
                        for j in range(2):
                            n = 2 * m + j
                            pool.wait_ge(S(f"qk_sb{L}"), (n + 1) * NC)
                            if m == 1:
                                pool.wait_ge(S("roped"), n - 1)
                            pool.tensor_tensor(by_cos[:, j, :], qkf[:, j, m, :], cos_t[:, :], ALU.mult)\
                                .then_inc(S("by_cos"), 1)
                    for part in (1, 2):
                        for j in range(2):
                            if (m, j) in POOL_PARTS:
                                take_part(pool, L, m, j, part)
                if L == 1:
                    pool.wait_ge(S("roped"), 2 * KD)
                ch.link(pool.memset(V[:, :, :, DH + 1:], 0.0))
                pool.memset(V[:, :, :, DH:DH + 1], 1.0).then_inc(S(f"v_pad{L}"), 1)
                for st in range(NG * NSTEP):
                    c, b = STEPS[st % NSTEP]
                    if not DIAGONAL[st % NSTEP]:
                        continue
                    off = b * P - c * CH
                    block_p = probs[:, st % PB, :, off:off + P]
                    pool.wait_ge(S(f"exp{L}"), 2 * st + 2)
                    pool.affine_select(out=block_p, in_=block_p, compare_op=ALU.is_ge, fill=0.0, base=0,
                                       pattern=[[0, HG], [1, P]], channel_multiplier=-1).then_inc(S(f"masked{L}"), 1)

                pool.wait_ge(S(f"slots_empty{L}"), 16 * TILES[L] // 8)
                for i in range(NT):
                    for c, (t0, _) in enumerate(SLOT_TILES):
                        if i == t0:
                            pool.wait_ge(S(f"slot_no{L}"), 2 * (c + 1))
                    for k in range(K):
                        n = i * K + k
                        pool.indirect_dma_start(
                            out=slot_rows[L], out_offset=bass.IndirectOffsetOnAxis(ap=slot_i[:, n:n + 1], axis=0),
                            in_=xn[:, i, :], in_offset=None, bounds_check=TILES[L] * P - 1, oob_is_err=False)\
                            .then_inc(S(f"scattered{L}"), 16)
                def add_rows(blk, r):
                    i = blk * RING + r
                    pool.wait_ge(S("e_sb"), E0[L] + i + 1)
                    pool.tensor_tensor(pause[:, r:r + 1], empty[:, 0:1], empty[:, 1:2], ALU.add).then_inc(S("e_seen"), 1)
                    pool.wait_ge(S(f"acc_start{L}"), 16 * 3)
                    pool.indirect_dma_start(
                        out=acc[L][r % 2], out_offset=bass.IndirectOffsetOnAxis(ap=token[:, r:r + 1], axis=0),
                        in_=erows[:, r % 2, :], in_offset=None,
                        compute_op=ALU.add).then_inc(S(f"added_{r % 2}"), 16)

                for r in range(RING):
                    add_rows(0, r)
                with pool.Fori(1, TILES[L] // RING) as blk:
                    for r in range(RING):
                        add_rows(blk, r)

        @block.tensor
        def _(pe):
            pe.wait_ge(S("consts"), 1)

            def turn_out(tag, n):
                return S("xT_act" if n == 0 else "xT_dve"), turned(tag) + KD

            def transposes(tag, src, ready):
                for n in range(NC):
                    pe.wait_ge(*ready[n])
                    for k in range(KD):
                        for i in range(TPC):
                            mm = pe.transpose(ps[:, KD * n + k, i * P:(i + 1) * P],
                                              src[:, TPC * n + i, k * P:(k + 1) * P], identf[:, :])
                        mm.then_inc(S("turned"), 1)

            for L in range(2):
                first = NORMED["attention0a" if L == 0 else "attention1"]
                transposes(f"a{L}", xn, [(S("normed"), first + TPC),
                                         (S("normed"), first + NT) if L == 0 else (S("normed_dve"), NT)])
                pe.wait_ge(S(f"w_qkv{L}"), 16)
                u = 0
                for m in range(KD):
                    for j in range(2):
                        for n in range(NC):
                            if m == 0:
                                pe.wait_ge(*turn_out(f"a{L}", n))
                            if u >= 4:
                                pe.wait_ge(S(f"qk_sb{L}"), u - 3)
                            for k in range(KD):
                                mm = pe.matmul(ps[:, 4 + u % 4, :], w_qkv[:, j, k, m * P:(m + 1) * P],
                                               xT[:, k, n * CH:(n + 1) * CH], start=(k == 0), stop=(k == KD - 1))
                            mm.then_inc(S(f"qk_ps{L}"), 1)
                            u += 1
                if L == 0:
                    pe.wait_ge(S("bias_qkv"), 32)
                for i in range(NT):
                    pe.wait_ge(S(f"qk_sb{L}"), 5 + i // 2)
                    dst = ps[:, 4 + i // 2, i % 2 * D:(i % 2 + 1) * D]
                    for k in range(KD):
                        mm = pe.matmul(dst, xT[:, k, i * P:(i + 1) * P], w_qkv[:, 2, k, :],
                                       start=(k == 0), stop=(k == KD - 1 and L == 1))
                    if L == 0:
                        mm = pe.matmul(dst, ones_row[:, :], bias_v[0:1, :], start=False, stop=True)
                    mm.then_inc(S(f"v_ps{L}"), 1)

                def unit(x):
                    n = UNIT_NO[x]
                    bank = n % RB
                    if n >= RB:
                        if UNITS[n - RB][0] == "rows":
                            pe.wait_ge(S(f"maxT{L}"), ROWS_DONE[n - RB])
                        else:
                            pe.wait_ge(S(f"unit_out{L}"), EMPTIED[n - RB])
                    if x[0] == "max":
                        _, g, u = x
                        _, i, h0, nh, s0, w = MAX_UNITS[u]
                        for j in range(nh):
                            h = HG * g + h0 + j
                            diag = s0 + w == (i + 1) * P
                            mm = pe.matmul(ps[:, bank, j * w:(j + 1) * w], QA[0:KQ, h, i * P:(i + 1) * P],
                                           KA[0:KQ, h, s0:s0 + w], start=True, stop=not diag)
                            if diag:
                                mm = pe.matmul(ps[:, bank, (j + 1) * w - P:(j + 1) * w], identb[:, :], mask_q[:, :],
                                               start=False, stop=True)
                    elif x[0] == "rows":
                        _, g, c = x
                        pe.wait_ge(S(f"neg_max{L}"), NC * g + c + 1)
                        for i in range(TPC):
                            mm = pe.matmul(ps[0:NSH * HG, bank, i * P:(i + 1) * P],
                                           nb[:, TPC * c + i, :, :].rearrange("p a h -> p (a h)"), identb[:, :],
                                           start=True, stop=True)
                    else:
                        pe.wait_ge(S(f"pv_sb{L}"), x[1] + 1)
                        for i in range(TPC):
                            mm = pe.transpose(ps[:, bank, i * P:(i + 1) * P], pv_sb[:, x[1] % 2, i * P:(i + 1) * P],
                                              identf[:, :])
                    mm.then_inc(S(f"unit{L}"), 1)

                def scores(st, p):
                    g, s = divmod(st, NSTEP)
                    c, b = STEPS[s]
                    off = max(0, b * P - c * CH)
                    if b == 0 and p == 0:
                        pe.wait_ge(S(f"max_rows{L}_{c}"), 16 * NSH * (g + 1))
                    if st >= 1:
                        pe.wait_ge(S(f"exp{L}"), 2 * st + p - 1)
                    for x in range(2):
                        h = HG * g + 2 * p + x
                        mm = pe.matmul(ps[:, 4 + 2 * p + x, off:CH], KA[0:KX, h, b * P:(b + 1) * P],
                                       QA[0:KX, h, c * CH + off:(c + 1) * CH], start=True, stop=True)
                    mm.then_inc(S(f"sc{L}"), 1)

                def weigh(st):
                    g, s = divmod(st, NSTEP)
                    c, b = STEPS[s]
                    off = max(0, b * P - c * CH)
                    n = NC * g + c
                    pe.wait_ge(S(f"exp{L}"), 2 * st + 2)
                    if DIAGONAL[s]:
                        pe.wait_ge(S(f"masked{L}"), masked_steps(st))
                    if b == 0 and n >= 1:
                        pe.wait_ge(S(f"pv_sb{L}"), n)
                    for x in range(HG):
                        mm = pe.matmul(ps[32 * x:32 * x + 32, RB, off:CH], V[:, b, HG * g + x, :],
                                       probs[:, st % PB, x, off:CH], start=(b == 0), stop=(b == TPC * (c + 1) - 1))
                    mm.then_inc(S(f"pv{L}"), 1)

                for x in SCHEDULE:
                    if x[0] == "max" and x[2] == 0:
                        pe.wait_ge(S(f"qa_rows{L}_{HG * x[1] // HM}"), 16 * 2 * NPROD)
                    if x == ("score", 0, 0):
                        pe.wait_ge(S(f"v_sb{L}"), NT)
                        pe.wait_ge(S(f"v_pad{L}"), 1)
                        pe.wait_ge(S(f"k_ones{L}"), 1)
                    if x[0] == "score":
                        scores(*x[1:])
                    elif x[0] == "weigh":
                        weigh(x[1])
                    else:
                        unit(x)
                units_out = (S(f"unit_out{L}"), EMPTIED[-1])
                transposes(f"y{L}", y, [units_out] * NC)
                pe.wait_ge(S(f"w_o{L}"), 16)
                pe.wait_ge(S(f"exp{L}"), 2 * NSTEP * NG)
                if L == 0:
                    pe.wait_ge(S("bias_o"), 48)
                for i in range(NT):
                    if i % TPC == 0:
                        pe.wait_ge(*turn_out(f"y{L}", i // TPC))
                    dst = ps[:, 4 + i // 2, i % 2 * D:(i % 2 + 1) * D]
                    for k in range(KD):
                        mm = pe.matmul(dst, xT[:, k, i * P:(i + 1) * P], w_o[:, k, :],
                                       start=(k == 0), stop=(k == KD - 1 and L == 1))
                    if L == 0:
                        mm = pe.matmul(dst, ones_row[:, :], bias_o[0:1, :], start=False, stop=True)
                    mm.then_inc(S(f"attn_proj{L}"), 1)

                transposes(f"f{L}", xn, [(S("normed"), NORMED["experts0"] + TPC), (S("normed_dve"), TPC)] if L == 0
                           else [(S("xn_f1"), TPC), (S("xn_f1"), NT)])
                pe.wait_ge(S(f"w_router{L}"), 16)
                for i in range(NT):
                    if i % TPC == 0:
                        pe.wait_ge(*turn_out(f"f{L}", i // TPC))
                    for k in range(KD):
                        mm = pe.matmul(ps[:, 4 + i // TPC, i % TPC * NR[L]:(i % TPC + 1) * NR[L]],
                                       xT[:, k, i * P:(i + 1) * P], w_rt[:, k, 0:NR[L]],
                                       start=(k == 0), stop=(k == KD - 1))
                    if i % TPC == TPC - 1:
                        mm.then_inc(S(f"logits_ps{L}"), 1)

                pe.wait_ge(S(f"w_shared{L}"), 48)
                srest, erest = SHARED[L] - SFULL[L] * P, INTER[L] - P
                nsc = SFULL[L] + 1

                def shared_up(u):
                    n, j = divmod(u, nsc)
                    if u >= 2:
                        pe.wait_ge(S(f"s_act{L}"), u - 1)
                    for x in range(2 if j < SFULL[L] else 1):
                        col = (x * SFULL[L] + j if j < SFULL[L] else 2 * SFULL[L]) * P
                        for k in range(KD):
                            mm = pe.matmul(ps[:, 2 * (u % 2) + x, :], w_sgu[:, k, col:col + P],
                                           xT[:, k, n * CH:(n + 1) * CH], start=(k == 0), stop=(k == KD - 1))
                    mm.then_inc(S(f"s_gu{L}"), 1)

                shared_up(0)
                if L == 1:
                    shared_up(1)
                pe.wait_ge(S(f"picked{L}"), NC)
                if L == 0:
                    for j in range(NT):
                        mm = pe.matmul(ps[0:E, 5, 0:1], picked[:, j, :], ones[:, 0:1], start=(j == 0), stop=(j == NT - 1))
                    mm.then_inc(S("counts"), 1)
                for i in range(NT):
                    for j in range(i + 1):
                        mm = pe.matmul(ps[:, 4, i * E:(i + 1) * E], (ones if j < i else before)[:, :],
                                       picked[:, j, :], start=(j == 0), stop=(j == i))
                mm.then_inc(S(f"ranks{L}"), 1)
                if L == 0:
                    pe.wait_ge(S("upto_n"), 1)
                    pe.matmul(ps[:, 5, E:3 * E], ones[0:E, :], upto_n[:, :], start=True, stop=True)\
                      .then_inc(S("begins"), 1)
                    shared_up(1)
                for u in range(2, nsc * NC):
                    shared_up(u)
                actv = acts[:, 0:nsc * T].rearrange("p (c t) -> p c t", c=nsc)
                for i in range(NT):
                    pe.wait_ge(S(f"s_act{L}"), nsc * (i // TPC + 1))
                    if i >= 2:
                        pe.wait_ge(S(f"sh_sb{L}"), i - 1)
                    for j in range(nsc):
                        rows_j = P if j < SFULL[L] else srest
                        mm = pe.matmul(ps[:, 6 + i % 2, 0:D], actv[0:rows_j, j, i * P:(i + 1) * P],
                                       w_sdn[0:rows_j, j, :], start=(j == 0), stop=(j == nsc - 1))
                    mm.then_inc(S(f"sh_down{L}"), 1)

                def e_transpose(blk, r, first):
                    i = blk * RING + r
                    pe.wait_ge(S(f"rows_{r}"), 16 * (R0[L] + blk + 1))
                    if not (first and r < 2):
                        pe.wait_ge(S("rowsT"), E0[L] + i - 1)
                    for k in range(KD):
                        mm = pe.transpose(ps[:, r % 2, k * P:(k + 1) * P], rows[:, r, k * P:(k + 1) * P], identf[:, :])
                    mm.then_inc(S("e_tr"), 1)

                def e_up(blk, r, first):
                    i = blk * RING + r
                    pe.wait_ge(S("rowsT"), E0[L] + i + 1)
                    pe.wait_ge(S(f"w_ex_{r}"), 16 * (R0[L] + blk + 1))
                    if not (first and r < 2):
                        pe.wait_ge(S("e_act"), 2 * (E0[L] + i - 1))
                    for m in range(UPC):
                        for k in range(KD):
                            col = (k * UPC + m) * P
                            mm = pe.matmul(ps[:, 2 + r % 2, m * P:(m + 1) * P], w_ex[:, r, col:col + P],
                                           rowsT[:, r % 2, k, :], start=(k == 0), stop=(k == KD - 1))
                    mm.then_inc(S("e_up"), 1)

                def e_down(blk, r, first):
                    i = blk * RING + r
                    pe.wait_ge(S("e_act"), 2 * (E0[L] + i) + 2)
                    pe.wait_ge(S(f"w_rest_{r}"), 16 * (R0[L] + blk + 1))
                    if not (first and r < 2):
                        pe.wait_ge(S("e_sb"), E0[L] + i - 1)
                    pe.matmul(ps[:, 4 + r % 2, 0:D], eact[:, r % 2, 0:P], w_ex[:, r, KD * UPC * P:EW],
                              start=True, stop=False)
                    mm = pe.matmul(ps[:, 4 + r % 2, 0:D], eact[0:erest, r % 2, P:2 * P], w_rest[0:erest, r, :],
                                   start=False, stop=True)
                    mm.then_inc(S("e_down"), 1)

                def e_block(blk, first, last):
                    for r in range(RING):
                        if not (last and r == RING - 1):
                            e_transpose(blk + (r + 1) // RING, (r + 1) % RING, first and r + 1 < RING)
                        e_up(blk, r, first)
                        if not (first and r == 0):
                            e_down(blk + (-1 if r == 0 else 0), (r - 1) % RING, first)

                pe.wait_ge(S(f"dest_done{L}"), 1)
                pe.wait_ge(S(f"s_act{L}"), nsc * NC)
                pe.wait_ge(S(f"sh_sb{L}"), NT)
                e_transpose(0, 0, True)
                e_block(0, True, False)
                with pe.Fori(1, TILES[L] // RING - 1) as blk:
                    e_block(blk, False, False)
                e_block(TILES[L] // RING - 1, False, True)
                e_down(TILES[L] // RING - 1, RING - 1, False)

        @block.scalar
        def _(act):
            for L in range(2):
                def xT_copy(tag):
                    for k in range(KD):
                        act.wait_ge(S("turned"), NC * turned(tag) + k + 1)
                        nc.scalar.activation(xT[:, k, 0:CH], ps[:, k, :], ACT.Copy).then_inc(S("xT_act"), 1)

                def norm(i, dst, src):
                    nc.scalar.activation(dst, src, ACT.Identity, bias=shift[:, i:i + 1], scale=rstd[:, i:i + 1])\
                      .then_inc(S("normed"), 1)

                for n in range(NC if L == 0 else 1):
                    act.wait_ge(S("scaled"), SCALED["attention0a"] + n if L == 0 else SCALED["attention1"])
                    for i in range(TPC * n, TPC * (n + 1)):
                        norm(i, xn[:, i, 0:D], xres[:, i, :])
                xT_copy(f"a{L}")
                if L == 0:
                    act.wait_ge(S("bias_qkv"), 32)
                if L == 1:
                    act.wait_ge(S("summed0"), NC)
                for m in range(KD):
                    for j in range(2):
                        for n in range(NC):
                            u = (m * 2 + j) * NC + n
                            act.wait_ge(S(f"qk_ps{L}"), u + 1)
                            dst = qkf[:, j, m, n * CH:(n + 1) * CH]
                            if L == 0:
                                nc.scalar.activation(dst, ps[:, 4 + u % 4, :], ACT.Identity,
                                                     bias=bias_qk[:, j, m:m + 1]).then_inc(S(f"qk_sb{L}"), 1)
                            else:
                                nc.scalar.activation(dst, ps[:, 4 + u % 4, :], ACT.Copy).then_inc(S(f"qk_sb{L}"), 1)
                    for part in range(2):
                        for j in range(2):
                            n = 2 * m + j
                            if part == 0 and L == 0:
                                act.wait_ge(S(f"qk_sb{L}"), (n + 1) * NC)
                            if part == 0 and L == 1:
                                act.wait_ge(S("roped"), n + 1)
                            if part == 1:
                                act.wait_ge(*left(L, m, j, 1))
                            nc.scalar.activation(parts[:, j, m, part, :], qkf[:, j, m, :], ACT.Copy)\
                              .then_inc(S(f"parts_p{part + 1}_{L}"), 1)

                if L == 1:
                    act.wait_ge(S("roped"), 2 * KD)
                for i in range(NT):
                    act.wait_ge(S(f"v_ps{L}"), i // 2 * 2 + 2)
                    nc.scalar.activation(V[:, i, :, 0:DH],
                                         ps[:, 4 + i // 2, i % 2 * D:(i % 2 + 1) * D].rearrange("p (h d) -> p h d", h=H),
                                         ACT.Copy).then_inc(S(f"v_sb{L}"), 1)

                for m in range(KD):
                    act.wait_ge(S(f"qa_rows{L}_{m}"), 16 * 2 * NPROD)

                def exps(st, p):
                    c, b = STEPS[st % NSTEP]
                    off = max(0, b * P - c * CH)
                    act.wait_ge(S(f"sc{L}"), 2 * st + p + 1)
                    if p == 0 and st >= PB:
                        act.wait_ge(S(f"pv{L}"), st - PB + 1)
                    nc.scalar.activation(probs[:, st % PB, 2 * p:2 * p + 2, off:CH], ps[:, 4 + 2 * p:6 + 2 * p, off:CH],
                                         ACT.Exp, scale=SCALE).then_inc(S(f"exp{L}"), 1)

                def pv_copy(n):
                    g, c = divmod(n, NC)
                    act.wait_ge(S(f"pv{L}"), NSTEP * g + (TPC if c == 0 else NSTEP))
                    if n >= 2:
                        act.wait_ge(S(f"unit{L}"), UNIT_NO[("turn", n - 2)] + 1)
                    nc.scalar.activation(pv_sb[:, n % 2, :], ps[:, RB, :], ACT.Copy).then_inc(S(f"pv_sb{L}"), 1)

                for x in SCHEDULE:
                    if x[0] == "score":
                        exps(*x[1:])
                    elif x[0] == "rows":
                        _, g, c = x
                        act.wait_ge(S(f"unit{L}"), UNIT_NO[x] + 1)
                        if g >= 1:
                            act.wait_ge(S(f"max_rows{L}_{c}"), 16 * NSH * g)
                        nc.scalar.activation(mT[:, c * CH:(c + 1) * CH], ps[0:NSH * HG, UNIT_NO[x] % RB, :],
                                             ACT.Copy).then_inc(S(f"maxT{L}"), 1)
                        if g == 0:
                            act.wait_ge(S(f"maxT{L}"), c + 1)
                            max_rows(act, L, 0, c)
                    elif x[0] == "weigh":
                        g, s = divmod(x[1], NSTEP)
                        if s in (TPC - 1, NSTEP - 1):
                            pv_copy(NC * g + (s == NSTEP - 1))
                xT_copy(f"y{L}")
                act.wait_ge(S("scaled"), SCALED[f"output{L}"])
                for i in range(NT):
                    norm(i, hb[:, i, :], ps[:, 4 + i // 2, i % 2 * D:(i % 2 + 1) * D])
                act.wait_ge(S("scaled"), SCALED[f"experts{L}"])
                for i in range(TPC if L == 0 else NT):
                    norm(i, xn[:, i, 0:D] if L == 0 else hb[:, i, :], xres[:, i, :])

                xT_copy(f"f{L}")
                srest, erest = SHARED[L] - SFULL[L] * P, INTER[L] - P
                nsc = SFULL[L] + 1
                act.wait_ge(S(f"less_top{L}"), 1 + L)
                nc.scalar.activation(gate[:, :, :], gate[:, :, :], ACT.Exp).then_inc(S(f"gate_exp{L}"), 1)
                if L == 1:
                    nc.scalar.activation(gall[:, :, :], gall[:, :, :], ACT.Exp).then_inc(S(f"gate_exp{L}"), 1)
                    nc.scalar.activation(sgate[:, :], lg[:, :, E], ACT.Tanh, scale=0.5).then_inc(S("sgate"), 1)
                for u in range(nsc * NC):
                    act.wait_ge(S(f"s_gu{L}"), u + 1)
                    if u >= 2:
                        act.wait_ge(S(f"s_act{L}"), u - 1)
                    if u % nsc < SFULL[L]:
                        ins = nc.scalar.activation(ssilu[:, u % 2, :], ps[:, 2 * (u % 2), :], ACT.Silu)
                    else:
                        ins = nc.scalar.activation(ssilu[HALF:HALF + srest, u % 2, :], ps[0:srest, 2 * (u % 2), :],
                                                   ACT.Silu)
                    ins.then_inc(S(f"s_silu{L}"), 1)
                if L == 0:
                    for i in range(NT):
                        act.wait_ge(S("sh_down0"), i + 1)
                        nc.scalar.activation(shout[:, i, :], ps[:, 6 + i % 2, 0:D], ACT.Copy).then_inc(S("sh_sb0"), 1)

                def e_tile(blk, r, first):
                    i = blk * RING + r
                    act.wait_ge(S("e_tr"), E0[L] + i + 1)
                    if not (first and r < 2):
                        act.wait_ge(S("e_up"), E0[L] + i - 1)
                    nc.scalar.activation(rowsT[:, r % 2, :, :].rearrange("p k n -> p (k n)"),
                                         ps[:, r % 2, 0:D], ACT.Copy).then_inc(S("rowsT"), 1)

                def e_silu(blk, r, first):
                    i = blk * RING + r
                    act.wait_ge(S("e_up"), E0[L] + i + 1)
                    if not (first and r < 2):
                        act.wait_ge(S("e_act"), 2 * (E0[L] + i - 1))
                    nc.scalar.activation(esilu[:, r % 2, 0:P], ps[:, 2 + r % 2, 0:P], ACT.Silu).then_inc(S("e_silu"), 1)
                    nc.scalar.activation(esilu[HALF:HALF + erest, r % 2, P:2 * P], ps[0:erest, 2 + r % 2, 2 * P:3 * P],
                                         ACT.Silu).then_inc(S("e_silu"), 1)

                def rows_in(blk, r):
                    act.dma_start(rows[:, r, :], slot_rows[L][bass.ds((blk * RING + r) * P, P), :])\
                       .then_inc(S(f"rows_{r}"), 16)

                def e_block(blk, first, last):
                    for r in range(RING):
                        if not (last and r == RING - 1):
                            e_tile(blk + (r + 1) // RING, (r + 1) % RING, first and r + 1 < RING)
                        e_silu(blk, r, first)
                        if not last:
                            act.wait_ge(S("e_tr"), E0[L] + blk * RING + r + 1)
                            act.wait_ge(S("e_pick"), 2 * (E0[L] + blk * RING + r) + 2)
                            rows_in(blk + 1, r)

                act.wait_ge(S(f"scattered{L}"), 16 * NT * K)
                if L == 0:
                    act.wait_ge(S("tile_expert"), 1)
                for r in range(RING):
                    rows_in(0, r)
                e_tile(0, 0, True)
                e_block(0, True, False)
                with act.Fori(1, TILES[L] // RING - 1) as blk:
                    e_block(blk, False, False)
                e_block(TILES[L] // RING - 1, False, True)
                act.wait_ge(S("scaled"), SCALED[f"sum{L}"])
                for i in range(NT):
                    norm(i, shout[:, i, :], shout[:, i, :])

        @block.vector
        def _(dve):
            ch = Chain(dve, S("dve_own"))
            v = nc.vector

            def inv_sqrt(dst, src, eps, t0, t1):
                y, half, sq, big = (t[:, t0:t1] for t in (dst, rs_half, rs_sq, rs_big))
                ch.step(v.tensor_scalar(sq, src, eps, None, ALU.add))
                ch.link(v.tensor_scalar(half, src, eps, -0.5, ALU.add, ALU.mult))
                ch.link(v.tensor_scalar(y.bitcast(I32), sq.bitcast(I32), -0.5, float(0x5F3759DF), ALU.mult, ALU.add))
                ch.step(v.tensor_tensor(sq, y, y, ALU.mult))
                ch.link(v.tensor_scalar(big, y, 1.5, None, ALU.mult))
                ch.link(v.tensor_tensor(sq, sq, half, ALU.mult))
                ch.link(v.scalar_tensor_tensor(sq, sq, 5.0 / 3.0, sq, ALU.add, ALU.mult))
                ch.link(v.scalar_tensor_tensor(y, sq, 1.25, big, ALU.add, ALU.mult))
                ch.link(v.tensor_tensor(sq, y, y, ALU.mult))
                ch.link(v.tensor_tensor(sq, sq, half, ALU.mult))
                ch.link(v.scalar_tensor_tensor(y, sq, 1.5, y, ALU.add, ALU.mult))

            def scales(t0, t1):
                ch.wait()
                for i in range(t0, t1):
                    ch.step(v.bn_aggr(mv[:, i, :], stats[:, i, :]))
                ch.wait()
                inv_sqrt(rstd, mv[:, t0:t1, 1], LN_EPS, t0, t1)
                v.scalar_tensor_tensor(shift[:, t0:t1], mv[:, t0:t1, 0], -1.0, rstd[:, t0:t1], ALU.mult, ALU.mult)\
                 .then_inc(S("scaled"), 1)

            def add_normed(stage, src, last=False):
                for i in range(NT):
                    dve.wait_ge(S("normed"), NORMED[stage] + i + 1)
                    ins = v.tensor_tensor(xres[:, i, :], xres[:, i, :], src[:, i, :], ALU.add)
                    if last:
                        ins.then_inc(S("final"), 1)
                        continue
                    ch.step(ins)
                    if i >= 1:
                        ch.wait(back=1 if i == 1 else 2)
                        ch.step(v.bn_stats(stats[:, i - 1, :], xres[:, i - 1, :]))
                if not last:
                    ch.wait(back=1)
                    ch.step(v.bn_stats(stats[:, NT - 1, :], xres[:, NT - 1, :]))
                    scales(0, NT)

            def norm_second_half():
                for i in range(TPC, NT):
                    v.tensor_scalar(xn[:, i, 0:D], xres[:, i, :], mv[:, i, 0:1], rstd[:, i:i + 1],
                                    ALU.subtract, ALU.mult).then_inc(S("normed_dve"), 1)

            def xT_copy(tag):
                for k in range(KD):
                    dve.wait_ge(S("turned"), NC * turned(tag) + KD + k + 1)
                    v.tensor_copy(xT[:, k, CH:T], ps[:, KD + k, :]).then_inc(S("xT_dve"), 1)

            halves = (list(range(0, TPC)), list(range(TPC, NT)))
            for L in range(2):
                for n in range(NC if L == 0 else 0):
                    dve.wait_ge(S(f"x_in{n}"), 16)
                    for i in halves[n]:
                        ch.step(v.bn_stats(stats[:, i, :], xres[:, i, :]))
                    scales(TPC * n, TPC * (n + 1))
                if L == 1:
                    norm_second_half()
                xT_copy(f"a{L}")
                for m in range(KD):
                    for j in range(2 if L == 1 else 0):
                        n = 2 * m + j
                        q = qkf[:, j, m, :]
                        dve.wait_ge(S(f"qk_sb{L}"), (n + 1) * NC)
                        if n == 0:
                            dve.wait_ge(S("rope"), 32)
                        swap = [x ^ HM for x in range(32)]
                        ch.link(v.stream_shuffle(swapped[:, j, :], q, swap))
                        ch.link(v.tensor_tensor(swapped[:, j, :], swapped[:, j, :], sin_t[:, :], ALU.mult))
                        dve.wait_ge(S("by_cos"), n + 1)
                        v.tensor_tensor(q, by_cos[:, j, :], swapped[:, j, :], ALU.add).then_inc(S("roped"), 1)
                    for part in (1, 2):
                        for j in range(2):
                            if (m, j) in DVE_PARTS:
                                take_part(dve, L, m, j, part)

                for x in UNITS:
                    n = UNIT_NO[x]
                    if x[0] == "rows":
                        continue
                    dve.wait_ge(S(f"unit{L}"), n + 1)
                    if x[0] == "max":
                        _, g, u = x
                        part, i, h0, nh, _, w = MAX_UNITS[u]
                        v.tensor_reduce(mx[:, part, i, h0:h0 + nh],
                                        ps[:, n % RB, 0:nh * w].rearrange("p (h w) -> p h w", h=nh), AX.X, ALU.max)\
                         .then_inc(S(f"unit_out{L}"), 1)
                        if u + 1 in CHUNK_UNITS:
                            c = CHUNK_UNITS.index(u + 1)
                            its = slice(TPC * c, TPC * (c + 1))
                            dve.wait_ge(S(f"unit_out{L}"), EMPTIED[n])
                            if c == 1:
                                ch.link(v.tensor_tensor(mx[:, 1, its, :], mx[:, 1, its, :], mx[:, 0, its, :], ALU.max))
                            ch.link(v.tensor_scalar(nb[:, its, 0, :], mx[:, 1, its, :], -1.0, None, ALU.mult))
                            v.scalar_tensor_tensor(nb[:, its, 1, :], mx[:, 1, its, :], -1.0, nb[:, its, 0, :],
                                                   ALU.mult, ALU.subtract).then_inc(S(f"neg_max{L}"), 1)
                    else:
                        g, c = divmod(x[1], NC)
                        t = ps[:, n % RB, :].rearrange("p (i h d) -> p i h d", i=TPC, h=HG)
                        ch.link(v.reciprocal(rden[:, c, :, :], t[:, :, :, DH]))
                        v.tensor_tensor(
                            y[:, TPC * c:TPC * (c + 1), HG * DH * g:HG * DH * (g + 1)].rearrange(
                                "p i (h d) -> p i h d", h=HG),
                            t[:, :, :, 0:DH],
                            rden[:, c, :, :].rearrange("p i (h o) -> p i h o", o=1).broadcast_to([P, TPC, HG, DH]),
                            ALU.mult).then_inc(S(f"unit_out{L}"), 1)

                xT_copy(f"y{L}")
                for i in range(NT):
                    dve.wait_ge(S(f"attn_proj{L}"), i // 2 * 2 + 2)
                    ch.step(v.bn_stats(stats[:, i, :], ps[:, 4 + i // 2, i % 2 * D:(i % 2 + 1) * D]))
                scales(0, NT)
                add_normed(f"output{L}", hb)
                if L == 0:
                    norm_second_half()
                if L == 1:
                    dve.wait_ge(S("scaled"), SCALED["experts1"])
                    ch.link(v.tensor_tensor(msq[:, :], rstd[:, :], rstd[:, :], ALU.mult))
                    ch.link(v.tensor_tensor(msq[:, :], msq[:, :], mv[:, :, 1], ALU.mult))
                    inv_sqrt(msq, msq[:, :], RMS_EPS, 0, NT)
                    for i in range(NT):
                        dve.wait_ge(S("normed"), NORMED["experts1"] + i + 1)
                        v.scalar_tensor_tensor(xn[:, i, 0:D], hb[:, i, :], msq[:, i:i + 1], w_nm[:, :],
                                               ALU.mult, ALU.mult).then_inc(S("xn_f1"), 1)

                xT_copy(f"f{L}")
                if L == 0:
                    dve.wait_ge(S("bias_o"), 48)
                for n, tiles in enumerate(halves):
                    t0, t1 = tiles[0], tiles[-1] + 1
                    dve.wait_ge(S(f"logits_ps{L}"), n + 1)
                    lps = ps[:, 4 + n, 0:TPC * NR[L]].rearrange("p (t e) -> p t e", t=TPC)
                    if L == 0:
                        ch.link(v.tensor_tensor(
                            lg[:, t0:t1, 0:E], lps,
                            b_rt[:, :].rearrange("p (o e) -> p o e", o=1).broadcast_to([P, TPC, E]), ALU.add))
                    else:
                        ch.link(v.tensor_copy(lg[:, t0:t1, :], lps))
                    for i in tiles:
                        ch.step(v.max(top[:, i, :], lg[:, i, 0:E]))
                    ch.wait()
                    for i in tiles:
                        ch.step(v.max_index(tix[:, i, :], top[:, i, :], lg[:, i, 0:E]))
                    if n == NC - 1:
                        v.tensor_tensor(gate[:, :, :], top[:, :, 0:K], top[:, :, 0:1].broadcast_to([P, NT, K]),
                                        ALU.subtract).then_inc(S(f"less_top{L}"), 1)
                    ch.wait()
                    ch.link(v.tensor_copy(tixf[:, t0:t1, :], tix[:, t0:t1, 0:K]))
                    ch.link(v.tensor_tensor(
                        onehot[:, t0:t1],
                        iota_e[:, :].rearrange("p (a b e) -> p a b e", a=1, b=1).broadcast_to([P, TPC, K, E]),
                        tixf[:, t0:t1, :].rearrange("p t (k o) -> p t k o", o=1).broadcast_to([P, TPC, K, E]),
                        ALU.is_equal))
                    with nc.allow_low_precision(reason="zeros and ones"):
                        v.tensor_reduce(picked[:, t0:t1, :], onehot[:, t0:t1].rearrange("p t k e -> p t e k"), AX.X,
                                        ALU.add).then_inc(S(f"picked{L}"), 1)

                srest, erest = SHARED[L] - SFULL[L] * P, INTER[L] - P
                nsc = SFULL[L] + 1
                actv = acts[:, 0:nsc * T].rearrange("p (c t) -> p c t", c=nsc)

                def shared_mult(u):
                    n, j = divmod(u, nsc)
                    dve.wait_ge(S(f"s_silu{L}"), u + 1)
                    if j < SFULL[L]:
                        ins = v.tensor_tensor(actv[:, j, n * CH:(n + 1) * CH], ps[:, 2 * (u % 2) + 1, :],
                                              ssilu[:, u % 2, :], ALU.mult)
                    else:
                        up = slice(HALF, HALF + srest)
                        ins = v.tensor_tensor(actv[0:srest, j, n * CH:(n + 1) * CH], ps[up, 2 * (u % 2), :],
                                              ssilu[up, u % 2, :], ALU.mult)
                    ins.then_inc(S(f"s_act{L}"), 1)

                if L == 0:
                    dve.wait_ge(S("counts"), 1)
                    ch.link(v.tensor_copy(cnt[:, :], ps[0:E, 5, 0:1]))
                    ch.link(v.tensor_scalar(levels[:, :], lev[0:E, :], cnt[:, 0:1], None, ALU.is_lt))
                    ch.link(v.tensor_reduce(ntile[:, :], levels[:, :], AX.X, ALU.add))
                    v.tensor_scalar(upto_n[:, :], upto[:, :, :].rearrange("p a e -> p (a e)"), ntile[:, 0:1], None,
                                    ALU.mult).then_inc(S("upto_n"), 1)
                else:
                    v.tensor_tensor(gall[:, :, :], lg[:, :, 0:E], top[:, :, 0:1].broadcast_to([P, NT, E]),
                                    ALU.subtract).then_inc(S("less_top1"), 1)
                dve.wait_ge(S(f"gate_exp{L}"), 1 + L)
                ch.link(v.tensor_reduce(gsum[:, :], gate[:, :, :] if L == 0 else gall[:, :, :], AX.X, ALU.add))
                ch.link(v.reciprocal(gsum[:, :], gsum[:, :]))
                if L == 0:
                    ch.link(v.tensor_scalar(gsum[:, :], gsum[:, :], 1.8, None, ALU.mult))
                ch.link(v.tensor_tensor(xn[:, :, GATES_AT:TOKEN_AT], gate[:, :, :],
                                        gsum[:, :].rearrange("p (t o) -> p t o", o=1).broadcast_to([P, NT, K]), ALU.mult))
                if L == 1:
                    dve.wait_ge(S("sgate"), 1)
                    ch.link(v.tensor_scalar(sgate[:, :], sgate[:, :], 1.0, 0.5, ALU.add, ALU.mult))
                    shared_mult(0)
                    shared_mult(1)

                dve.wait_ge(S(f"ranks{L}"), 1)
                rank = ps[:, 4, 0:NT * E].rearrange("p (t e) -> p t e", t=NT)
                if L == 0:
                    dve.wait_ge(S("begins"), 1)
                    ch.link(v.tensor_scalar(tbeg[:, :], ps[:, 5, E:2 * E], float(P), None, ALU.mult))
                    ch.step(v.tensor_copy(tend[:, :], ps[0:1, 5, 2 * E:3 * E]))
                    ins = v.tensor_tensor(dest[:, :, :], rank,
                                          tbeg[:, :].rearrange("p (o e) -> p o e", o=1).broadcast_to([P, NT, E]), ALU.add)
                    ch.wait()
                else:
                    ch.step(v.tensor_scalar(dest[:, :, :], rank, CAP - 0.5, SKIP, ALU.is_gt, ALU.mult))
                    ch.link(v.tensor_scalar(tbeg[:, :], iota_e[:, :], float(CAP), None, ALU.mult))
                    ch.link(v.tensor_tensor(dest[:, :, :], dest[:, :, :], rank, ALU.add))
                    ins = v.tensor_tensor(dest[:, :, :], dest[:, :, :],
                                          tbeg[:, :].rearrange("p (o e) -> p o e", o=1).broadcast_to([P, NT, E]), ALU.add)
                ins.then_inc(S(f"dest_done{L}"), 1)
                dve.wait_ge(S(f"dest_done{L}"), 1)
                for t0, t1 in SLOT_TILES:
                    n = t1 - t0
                    ch.link(v.tensor_tensor(prod[:, t0:t1], onehot[:, t0:t1],
                                            dest[:, t0:t1, :].rearrange("p t (o e) -> p t o e", o=1)
                                            .broadcast_to([P, n, K, E]), ALU.mult))
                    ch.link(v.tensor_reduce(slot[:, t0:t1, :], prod[:, t0:t1], AX.X, ALU.add))
                    v.tensor_copy(slot_i[:, t0 * K:t1 * K], slot[:, t0:t1, :].rearrange("p t k -> p (t k)"))\
                     .then_inc(S(f"slot_no{L}"), 1)
                    v.tensor_copy(xn[:, t0:t1, SLOTS_AT:GATES_AT], slot[:, t0:t1, :]).then_inc(S(f"slot_no{L}"), 1)
                ch.step(v.tensor_copy(own[:, :], own_first[:, :]))
                if L == 0:
                    m3 = tmap.rearrange("p (i e) -> p i e", i=TILES[0])
                    ch.link(v.tensor_tensor(
                        m3, iota_t[:, :].rearrange("p (i o) -> p i o", o=1).broadcast_to([1, TILES[0], E]),
                        tend[:, :].rearrange("p (o e) -> p o e", o=1).broadcast_to([1, TILES[0], E]), ALU.is_ge))
                    ch.link(v.tensor_reduce(texp, m3, AX.X, ALU.add))
                    v.tensor_scalar(texp_i[:, :], texp, float(E - 1), None, ALU.min).then_inc(S("tile_expert"), 1)

                for u in range(2 if L == 1 else 0, nsc * NC):
                    shared_mult(u)
                if L == 1:
                    for i in range(NT):
                        dve.wait_ge(S("sh_down1"), i + 1)
                        v.scalar_tensor_tensor(shout[:, i, :], ps[:, 6 + i % 2, 0:D], sgate[:, i:i + 1], hb[:, i, :],
                                               ALU.mult, ALU.add).then_inc(S("sh_sb1"), 1)

                def e_pick(blk, r, first):
                    i = blk * RING + r
                    dve.wait_ge(S(f"rows_{r}"), 16 * (R0[L] + blk + 1))
                    if not (first and L == 0):
                        dve.wait_ge(S(f"added_{r % 2}"), 16 * (E0[L] // 2 + 2 * blk + r // 2 - 1))
                        dve.wait_ge(S("e_seen"), E0[L] + i - RING + 1)
                    v.scalar_tensor_tensor(mine[:, r, :], rows[:, r, SLOTS_AT:GATES_AT], own[:, r:r + 1],
                                           rows[:, r, GATES_AT:TOKEN_AT], ALU.is_equal, ALU.mult).then_inc(S("e_pick"), 1)
                    v.tensor_copy(token[:, r:r + 1], rows[:, r, TOKEN_AT:W].bitcast(I32)).then_inc(S("e_pick"), 1)

                def e_gate(blk, r):
                    i = blk * RING + r
                    dve.wait_ge(S("e_pick"), 2 * (E0[L] + i) + 2)
                    v.tensor_reduce(egate[:, r:r + 1], mine[:, r, :], AX.X, ALU.add).then_inc(S("e_gate"), 1)

                def e_mult(blk, r, first):
                    i = blk * RING + r
                    dve.wait_ge(S("e_silu"), 2 * (E0[L] + i) + 2)
                    if not (first and r < 2):
                        dve.wait_ge(S("e_down"), E0[L] + i - 1)
                    v.tensor_tensor(eact[:, r % 2, 0:P], ps[:, 2 + r % 2, P:2 * P], esilu[:, r % 2, 0:P], ALU.mult)\
                     .then_inc(S("e_act"), 1)
                    up = slice(HALF, HALF + erest)
                    v.tensor_tensor(eact[0:erest, r % 2, P:2 * P], ps[up, 2 + r % 2, 2 * P:3 * P],
                                    esilu[up, r % 2, P:2 * P], ALU.mult).then_inc(S("e_act"), 1)

                def e_out(blk, r, first):
                    i = blk * RING + r
                    dve.wait_ge(S("e_down"), E0[L] + i + 1)
                    dve.wait_ge(S("e_gate"), E0[L] + i + 1)
                    if not (first and r < 2 and L == 0):
                        dve.wait_ge(S(f"added_{r % 2}"), 16 * (E0[L] // 2 + 2 * blk + r // 2))
                    v.tensor_scalar(erows[:, r % 2, :], ps[:, 4 + r % 2, 0:D], egate[:, r:r + 1], None, ALU.mult)\
                     .then_inc(S("e_sb"), 1)

                def e_block(blk, first, last):
                    for r in range(RING):
                        e_pick(blk, r, first)
                        e_mult(blk, r, first)
                        e_gate(blk, r)
                        if not (first and r == 0):
                            e_out(blk + (-1 if r == 0 else 0), (r - 1) % RING, first)
                    if not last:
                        v.tensor_scalar(own[:, :], own[:, :], float(RING * P), None, ALU.add).then_inc(S("own"), 1)
                        dve.wait_ge(S("own"), L * (TILES[0] // RING - 1) + blk + 1)

                last = TILES[L] // RING - 1
                e_block(0, True, False)
                with dve.Fori(1, last) as blk:
                    e_block(blk, False, False)
                e_block(last, False, True)
                e_out(last, RING - 1, False)

                for n, tiles in enumerate(halves):
                    dve.wait_ge(S(f"sums_in{L}_{n}"), 32)
                    t0, t1 = tiles[0], tiles[-1] + 1
                    v.tensor_tensor(shout[:, t0:t1, :], shout[:, t0:t1, :], sum_odd[:, t0:t1, :], ALU.add)\
                     .then_inc(S(f"summed{L}"), 1)
                    dve.wait_ge(S(f"summed{L}"), n + 1)
                    for i in tiles:
                        ch.step(v.bn_stats(stats[:, i, :], shout[:, i, :]))
                scales(0, NT)
                add_normed(f"sum{L}", shout, last=(L == 1))


def kernel(**inputs):
    import concourse.bacc as bacc
    from concourse.bass_utils import run_bass_kernel_spmd

    g = {k: np.asarray(v) for k, v in inputs.items()}
    d = {}
    d["x"] = g["L0_attn_x"].reshape(T, D)

    def by_half(w):
        s = w.shape[:-1]
        return np.swapaxes(w.reshape(s + (KD, HM, DH)), -1, -2).reshape(s + (D,))

    d["qkv0"] = np.stack([f(g[f"L0_attn_{n}"].transpose(1, 0, 2).reshape(D, D))
                          for n, f in (("Wq", by_half), ("Wk", by_half), ("Wv", np.asarray))])
    d["qkv1"] = np.stack([f(g[f"L1_attn_{n}"].T) for n, f in (("wq", by_half), ("wk", by_half), ("wv", np.asarray))])
    d["wo0"] = g["L0_attn_Wo"]
    d["wo1"] = g["L1_attn_wo"].T
    d["bqk"] = np.stack([by_half(g[f"L0_attn_{n}"].reshape(D)).reshape(KD, P) for n in ("bq", "bk")]).transpose(2, 0, 1)
    d["bv"] = g["L0_attn_bv"].reshape(D)
    d["bo"] = g["L0_attn_bo"]
    d["router_b"] = g["L0_ffn_router_b"]
    d["w_norm"] = g["L1_ffn_w_norm"]
    d["router0"] = g["L0_ffn_router_w"].T
    d["router1"] = np.concatenate([g["L1_ffn_w_router"], g["L1_ffn_w_shared_gate"]], axis=1)

    def up(gate, upw):
        n = gate.shape[-1] // P * P
        fill = [(0, 0)] * (gate.ndim - 1) + [(0, HALF - (gate.shape[-1] - n))]
        both = np.concatenate([gate[..., :n], upw[..., :n], np.pad(gate[..., n:], fill), np.pad(upw[..., n:], fill)],
                              axis=-1)
        return np.swapaxes(both.reshape(both.shape[:-2] + (KD, P, both.shape[-1])), -3, -2)

    def expert(gate, upw, down):
        return np.concatenate([up(gate, upw).reshape(E, P, -1), down[:, :P]], axis=-1)

    down0 = g["L0_ffn_down_w"].transpose(0, 2, 1)
    d["ex0"] = expert(g["L0_ffn_gate_w"].transpose(0, 2, 1), g["L0_ffn_up_w"].transpose(0, 2, 1), down0)
    d["ex1"] = expert(g["L1_ffn_w_gate"], g["L1_ffn_w_up"], g["L1_ffn_w_down"])
    d["dn0"] = down0[:, P:]
    d["dn1"] = g["L1_ffn_w_down"][:, P:]
    d["sgu0"] = up(g["L0_ffn_shared_gate_w"].T, g["L0_ffn_shared_up_w"].T)
    d["sgu1"] = up(g["L1_ffn_sw_gate"], g["L1_ffn_sw_up"])
    d["sdn0"] = g["L0_ffn_shared_down_w"].T
    d["sdn1"] = g["L1_ffn_sw_down"]
    pos = np.arange(T, dtype=np.float32)[:, None]
    inv = (np.float32(10000.0) ** (-(np.arange(0, DH, 2, dtype=np.float32) / np.float32(DH)))).astype(np.float32)
    ang = np.repeat(pos * inv, 2, axis=1)
    sign = np.where(np.arange(DH) % 2 == 0, -1.0, 1.0).astype(np.float32)
    d["cos"] = np.repeat(np.cos(ang).T, HM, axis=0).astype(np.float32)
    d["sin"] = np.repeat((np.sin(ang) * sign).T, HM, axis=0).astype(np.float32)

    nc = bacc.Bacc("TRN2", target_bir_lowering=False, num_devices=1)
    arrays, args = {}, {}
    for name, x in d.items():
        x = np.ascontiguousarray(x)
        arrays[f"in_{name}"] = x
        args[name] = nc.dram_tensor(f"in_{name}", x.shape, mybir.dt.from_np(x.dtype), kind="ExternalInput").ap()
    out = nc.dram_tensor("out_x", (T, D), F32, kind="ExternalOutput").ap()
    build(nc, args, out)
    r = run_bass_kernel_spmd(nc, [arrays], core_ids=[0])
    return r.results[0]["out_x"].reshape(1, T, D)
```
